# Optimizing a Trainium2 kernel written in Bass

```python
import numpy as np
import jax
import jax.numpy as jnp

def _softmax(x, axis=-1):
    return jax.nn.softmax(x, axis=axis)

def _gelu(x):
    return jax.nn.gelu(x, approximate=True)

def _silu(x):
    return jax.nn.silu(x)

def _sigmoid(x):
    return jax.nn.sigmoid(x)

def _layernorm(x, axis=-1, eps=1e-05):
    m = jnp.mean(x, axis=axis, keepdims=True)
    v = jnp.var(x, axis=axis, keepdims=True)
    return (x - m) / jnp.sqrt(v + eps)

def _scatter_add(tgt, idx, src, axis=0):
    return tgt.at[idx].add(src)

def _segment_sum(src, seg, n):
    return jax.ops.segment_sum(src, seg, n)
kernel_name = 'mk_xattn_seq_d2_seqx_r2_c85a3e'

def setup_inputs(seed: int=0):
    np.random.seed(seed)
    _w = jnp.asarray

    def _rec_inputs():
        import jax
        import jax.numpy as jnp
        _rk = jax.random.key(seed)
        x = -0.0002928 + 1 * jax.random.normal(jax.random.fold_in(_rk, 1), (4, 2048, 512), jnp.float32)
        _lenS = 2048 - jax.random.randint(jax.random.fold_in(_rk, 7), (4,), 0, max(1, 2048 // 4) + 1, jnp.int32)
        _lenS2 = 154 - jax.random.randint(jax.random.fold_in(_rk, 8), (4,), 0, max(1, 154 // 4) + 1, jnp.int32)
        _ctx_1024P = jax.random.normal(jax.random.fold_in(_rk, 11), (4, 16, 512), jnp.float32)
        _ctx_1024c = jax.random.dirichlet(jax.random.fold_in(_rk, 511), 0.3 * jnp.ones((16,), jnp.float32), (4, 154))
        _ctx_1024t = jnp.einsum('bsk,bkd->bsd', _ctx_1024c, _ctx_1024P)
        _ctx_1024t = _ctx_1024t * jax.lax.rsqrt(jnp.mean(jnp.square(_ctx_1024t)) + 1e-12) * 0.953939
        ctx_1024 = -1.39393e-06 + 0.999914 * (_ctx_1024t + 0.3 * jax.random.normal(jax.random.fold_in(_rk, 611), (4, 154, 512), jnp.float32))
        _validS = jnp.arange(2048)[None, :] < _lenS[:, None]
        _validS2 = jnp.arange(154)[None, :] < _lenS2[:, None]
        _causal = jnp.tril(jnp.ones((2048, 2048), dtype=bool))
        mask_BxS2_bf1 = jnp.ones((4, 154), dtype=bool)
        return (x, ctx_1024, mask_BxS2_bf1)
    x, ctx_1024, mask_BxS2_bf1 = _rec_inputs()

    def _L0_xattn_setup():
        import jax, jax.numpy as jnp
        import numpy as np
        EPS = 1e-06
        N_HEADS = 16

        def rmsnorm(x, g):
            return x * jax.lax.rsqrt(jnp.mean(x * x, axis=-1, keepdims=True) + EPS) * g
        key = jax.random.key(seed)
        ks = jax.random.split(key, 8)
        B, Tq, Tc, dq, dc, dm = (2, 1024, 1024, 512, 512, 512)
        query = jax.random.normal(ks[0], (B, Tq, dq), dtype=jnp.float32)
        context = jax.random.normal(ks[1], (B, Tc, dc), dtype=jnp.float32)
        context_mask = jnp.ones((B, Tc), dtype=bool)
        s = 0.02
        Wq = jax.random.normal(ks[2], (dq, dm), dtype=jnp.float32) * s
        Wk = jax.random.normal(ks[3], (dc, dm), dtype=jnp.float32) * s
        Wv = jax.random.normal(ks[4], (dc, dm), dtype=jnp.float32) * s
        Wo = jax.random.normal(ks[5], (dm, dq), dtype=jnp.float32) * s
        g_q = jnp.ones((dq,), dtype=jnp.float32)
        g_c = jnp.ones((dc,), dtype=jnp.float32)
        g_out = jnp.ones((dq,), dtype=jnp.float32)
        return dict(query=query, context=context, context_mask=context_mask, Wq=Wq, Wk=Wk, Wv=Wv, Wo=Wo, g_q=g_q, g_c=g_c, g_out=g_out)
    _L0_xattn_all = _L0_xattn_setup()
    _L0_xattn_in = {k: v for k, v in _L0_xattn_all.items() if k in ('Wq', 'Wk', 'Wv', 'Wo', 'g_q', 'g_c', 'g_out')}
    del _L0_xattn_all

    def _L1_xattn_setup():
        import jax, jax.numpy as jnp
        import numpy as np
        B, L, D = (32, 256, 512)
        H, DK, DV = (8, 16, 16)

        def _xavier(key, shape):
            fan_in, fan_out = (shape[0], shape[1])
            std = (2.0 / (fan_in + fan_out)) ** 0.5
            return std * jax.random.normal(key, shape, dtype=jnp.float32)
        key = jax.random.key(seed)
        ks = jax.random.split(key, 11)
        return {'Q': jax.random.normal(ks[0], (B, L, D), jnp.float32), 'K': jax.random.normal(ks[1], (B, L, D), jnp.float32), 'V': jax.random.normal(ks[2], (B, L, D), jnp.float32), 'W_q': _xavier(ks[3], (D, H * DK)), 'W_k': _xavier(ks[4], (D, H * DK)), 'W_v': _xavier(ks[5], (D, H * DV)), 'W_o': _xavier(ks[6], (H * DV, D)), 'w1': _xavier(ks[7], (D, D)), 'b1': jnp.zeros((D,), jnp.float32), 'w2': _xavier(ks[8], (D, D)), 'b2': jnp.zeros((D,), jnp.float32)}
    _L1_xattn_all = _L1_xattn_setup()
    _L1_xattn_in = {k: v for k, v in _L1_xattn_all.items() if k in ('W_q', 'W_k', 'W_v', 'W_o', 'w1', 'b1', 'w2', 'b2')}
    del _L1_xattn_all
    return {'x': x, 'ctx_1024': ctx_1024, 'mask_BxS2_bf1': mask_BxS2_bf1, 'L0_xattn_Wq': _L0_xattn_in['Wq'], 'L0_xattn_Wk': _L0_xattn_in['Wk'], 'L0_xattn_Wv': _L0_xattn_in['Wv'], 'L0_xattn_Wo': _L0_xattn_in['Wo'], 'L0_xattn_g_q': _L0_xattn_in['g_q'], 'L0_xattn_g_c': _L0_xattn_in['g_c'], 'L0_xattn_g_out': _L0_xattn_in['g_out'], 'L1_xattn_W_q': _L1_xattn_in['W_q'], 'L1_xattn_W_k': _L1_xattn_in['W_k'], 'L1_xattn_W_v': _L1_xattn_in['W_v'], 'L1_xattn_W_o': _L1_xattn_in['W_o'], 'L1_xattn_w1': _L1_xattn_in['w1'], 'L1_xattn_b1': _L1_xattn_in['b1'], 'L1_xattn_w2': _L1_xattn_in['w2'], 'L1_xattn_b2': _L1_xattn_in['b2']}

def reference(x, ctx_1024, mask_BxS2_bf1, L0_xattn_Wq, L0_xattn_Wk, L0_xattn_Wv, L0_xattn_Wo, L0_xattn_g_q, L0_xattn_g_c, L0_xattn_g_out, L1_xattn_W_q, L1_xattn_W_k, L1_xattn_W_v, L1_xattn_W_o, L1_xattn_w1, L1_xattn_b1, L1_xattn_w2, L1_xattn_b2):
    import jax
    import jax.numpy as jnp

    def _L0_xattn_ref(query, context, context_mask, Wq, Wk, Wv, Wo, g_q, g_c, g_out):
        import jax, jax.numpy as jnp
        import numpy as np
        EPS = 1e-06
        N_HEADS = 16

        def rmsnorm(x, g):
            return x * jax.lax.rsqrt(jnp.mean(x * x, axis=-1, keepdims=True) + EPS) * g
        B, Tq, _ = query.shape
        Tc = context.shape[1]
        H = N_HEADS
        dm = Wq.shape[1]
        hd = dm // H
        scale = hd ** (-0.5)
        q_norm = rmsnorm(query, g_q)
        c_norm = rmsnorm(context, g_c)
        Q = (q_norm @ Wq).reshape(B, Tq, H, hd).transpose(0, 2, 1, 3)
        K = (c_norm @ Wk).reshape(B, Tc, H, hd).transpose(0, 2, 1, 3)
        V = (c_norm @ Wv).reshape(B, Tc, H, hd).transpose(0, 2, 1, 3)
        scores = jnp.einsum('bhqd,bhkd->bhqk', Q, K) * scale
        scores = jnp.where(context_mask[:, None, None, :], scores, -jnp.inf)
        attn = jax.nn.softmax(scores, axis=-1)
        attn = jnp.nan_to_num(attn, nan=0.0)
        out = jnp.einsum('bhqk,bhkd->bhqd', attn, V)
        out = out.transpose(0, 2, 1, 3).reshape(B, Tq, dm)
        out = out @ Wo
        return rmsnorm(query + out, g_out)

    def _L1_xattn_ref(Q, K, V, W_q, W_k, W_v, W_o, w1, b1, w2, b2):
        import jax, jax.numpy as jnp
        import numpy as np
        B, L, D = (32, 256, 512)
        H, DK, DV = (8, 16, 16)

        def _xavier(key, shape):
            fan_in, fan_out = (shape[0], shape[1])
            std = (2.0 / (fan_in + fan_out)) ** 0.5
            return std * jax.random.normal(key, shape, dtype=jnp.float32)
        b, lq, _ = Q.shape
        lk = K.shape[1]
        Qh = (Q @ W_q).reshape(b, lq, H, DK)
        Kh = (K @ W_k).reshape(b, lk, H, DK)
        Vh = (V @ W_v).reshape(b, lk, H, DV)
        scale = 1.0 / jnp.sqrt(jnp.float32(DK))
        scores = jnp.einsum('bqhd,bkhd->bhqk', Qh, Kh) * scale
        attn = jax.nn.softmax(scores, axis=-1)
        ctx = jnp.einsum('bhqk,bkhd->bqhd', attn, Vh).reshape(b, lq, H * DV)
        attn_out = ctx @ W_o
        X = Q + attn_out
        h = jax.nn.relu(X @ w1.T + b1)
        ffn_out = h @ w2.T + b2
        return ffn_out + X
    x = _L0_xattn_ref(x, ctx_1024, mask_BxS2_bf1, L0_xattn_Wq, L0_xattn_Wk, L0_xattn_Wv, L0_xattn_Wo, L0_xattn_g_q, L0_xattn_g_c, L0_xattn_g_out)
    x = _L1_xattn_ref(x, ctx_1024, ctx_1024, L1_xattn_W_q, L1_xattn_W_k, L1_xattn_W_v, L1_xattn_W_o, L1_xattn_w1, L1_xattn_b1, L1_xattn_w2, L1_xattn_b2)
    return x

_drawn_inputs = setup_inputs


def setup_inputs(seed=0):
    import zlib

    import numpy as np

    out = dict(_drawn_inputs(seed))
    spreads = {'L0_xattn_g_q': (1.0, 0.6),
     'L0_xattn_g_c': (1.0, 0.6),
     'L0_xattn_g_out': (1.0, 0.2),
     'L1_xattn_b1': (0.0, 0.1),
     'L1_xattn_b2': (0.0, 0.1)}
    factors = {'L0_xattn_Wq': 7.093, 'L0_xattn_Wk': 7.141}
    for name, (base, spread) in spreads.items():
        noise = np.random.default_rng([zlib.crc32(name.encode()), seed]).standard_normal(out[name].shape)
        drawn = base * np.exp(spread * noise) if base else spread * noise
        out[name] = jnp.asarray(drawn.astype(out[name].dtype))
    for name, factor in factors.items():
        out[name] = (out[name] * factor).astype(out[name].dtype)
    return out
```

```python
from contextlib import ExitStack

import concourse.bass as bass
from concourse import mybir

F32 = mybir.dt.float32
F16 = mybir.dt.float16
U8 = mybir.dt.uint8
ALU = mybir.AluOpType
ACT = mybir.ActivationFunctionType
AX = mybir.AxisListType

P = 128
D = 512
C = D // P
B, S, SK = 4, 2048, 154
KM = 128
KR = SK - KM
KP = 32
KA = KM + KP
T = 512
SUB = T // P
NT = B * S // T
TPB = S // T
H0, D0 = 16, 32
H1, D1 = 8, 16
G0 = H0 // 4
G1 = H1 // 4
EPS = 1e-6
WS = 64.0
UNIT = 2 * SK

K0_ST, K0_BLK, K0_V, K0_VR, K0_E, K0_ER = H0 * KA, G0 * 4 * SK, 2 * D, 2 * G0 * P, 2 * 4 * 32, 2 * 32
IMG0 = K0_ST + K0_BLK + K0_V + K0_VR + K0_E + K0_ER
K1_ST, K1_BLK, K1_V, K1_VR = H1 * KA, H1 * SK, 2 * H1 * 32, 2 * G1 * P
IMG1 = K1_ST + K1_BLK + K1_V + K1_VR


class Steps:

    def __init__(self, names):
        self.names = names.split() if isinstance(names, str) else list(names)
        assert len(set(self.names)) == len(self.names)
        self.at = {n: i + 1 for i, n in enumerate(self.names)}

    def upto(self, turn, name):
        return turn * len(self.names) + self.at[name]


def nums(fmt, n):
    return [fmt.format(i) for i in range(n)]


def order_sc0():
    return [("s", 0), ("s", 1), ("v", 0), ("s", 2), ("v", 1), ("s", 3), ("v", 2), ("v", 3)]


PRE_ACT = Steps("sq sqr")
PRE_POOL = Steps("r")
PRE_PE = Steps("ta0 tb0 k0 k1 k2 k3 v0 vr0 ta1 tb1 kk v1 vr1")
PRE_DVE = Steps("masks ms sc0 cn0 ct0 sum0 mean0 ck0 cks0 k0_0 k0_1 k0_2 k0_3 kst0 v0 vr0 "
                "ct1 sum1 mean1 ck1 cks1 kk km kst1 v1 vr1")

PE_A = Steps(nums("xt{}", SUB) + nums("q{}", G0) + nums("m{}", 32) + ["mt"]
             + [n for k, g in order_sc0() for n in (nums(f"s{g}" + "{}", 4) + [f"r{g}"] if k == "s" else [f"v{g}"])]
             + ["dt"] + nums("rb{}", G0) + nums("y{}", SUB) + nums("x2t{}", SUB))
ACT_A = Steps(nums("sq{}", SUB) + nums("xh{}", SUB) + nums("qh{}", G0) + ["negm"]
              + [n for g in range(G0) for n in nums(f"e{g}" + "{}", 4) + [f"er{g}"]]
              + ["dsb"] + nums("oh{}", G0) + nums("sqy{}", SUB)
              + [n for s in range(SUB) for n in (f"xf{s}", f"x2h{s}")])
DVE_A = Steps(["ms"] + nums("xn{}", SUB) + nums("xl{}", SUB) + nums("ql{}", G0) + nums("mx{}", 32) + nums("o{}", G0)
              + ["dm", "dd", "dg", "rc"] + [n for m in range(G0) for n in (f"on{m}", f"ol{m}")]
              + nums("y{}", SUB) + ["msy"] + nums("x2_{}", SUB) + nums("x2l{}", SUB))
POOL_A = Steps(["r"] + nums("rr{}", G0) + ["ry"])
PE_B = Steps(["q"] + nums("m{}", 16) + ["mt"]
             + [n for g in range(G1) for n in nums(f"s{g}" + "{}", 4) + [f"r{g}", f"v{g}"]]
             + ["od0", "od1", "ot"] + nums("xo{}", C) + nums("h{}", C) + nums("f{}", C) + nums("t{}", SUB))
ACT_B = Steps(["qh", "negm"] + [n for g in range(G1) for n in nums(f"e{g}" + "{}", 4) + [f"er{g}", f"od{g}"]]
              + ["oh"] + nums("xh{}", C) + nums("h{}", C) + nums("t{}", SUB))
DVE_B = Steps(["ql"] + nums("mx{}", 16) + ["rc0", "on0", "rc1", "on1", "ol"]
              + ["xo0", "xo1", "xl0", "xo2", "xl1", "xo3", "xl2", "xl3"]
              + [n for f in range(C) for n in (f"hh{f}", f"hl{f}")] + nums("f{}", C))
POOL_B = Steps(nums("xb{}", C))

RING_A = nums("xt{}", SUB) + nums("q{}", G0) + nums("m{}", 32) + ["mt"] \
    + [n for k, g in order_sc0() if k == "s" for n in nums(f"s{g}" + "{}", 4) + [f"r{g}"]] \
    + ["dt"] + nums("rb{}", G0) + nums("y{}", SUB) + nums("x2t{}", SUB)
READER_A = {**{f"xt{s}": ("dve", f"xl{s}") for s in range(SUB)}, **{f"q{m}": ("dve", f"ql{m}") for m in range(G0)},
            **{f"m{n}": ("dve", f"mx{n}") for n in range(32)}, "mt": ("act", "negm"),
            **{f"s{g}{j}": ("act", f"e{g}{j}") for g in range(G0) for j in range(4)},
            **{f"r{g}": ("act", f"er{g}") for g in range(G0)}, "dt": ("dve", "dd"),
            **{f"rb{m}": ("dve", f"on{m}") for m in range(G0)}, **{f"y{s}": ("dve", f"y{s}") for s in range(SUB)},
            **{f"x2t{s}": ("dve", f"x2l{s}") for s in range(SUB)}}
RING_B = ["q"] + nums("m{}", 16) + ["mt"] + [n for g in range(G1) for n in nums(f"s{g}" + "{}", 4) + [f"r{g}"]] \
    + ["od0", "od1", "ot"] + nums("xo{}", C) + nums("h{}", C) + nums("f{}", C) + nums("t{}", SUB)
READER_B = {"q": ("dve", "ql"), **{f"m{n}": ("dve", f"mx{n}") for n in range(16)}, "mt": ("act", "negm"),
            **{f"s{g}{j}": ("act", f"e{g}{j}") for g in range(G1) for j in range(4)},
            **{f"r{g}": ("act", f"er{g}") for g in range(G1)}, "od0": ("dve", "on0"), "od1": ("dve", "on1"),
            "ot": ("dve", "ol"), **{f"xo{m}": ("dve", f"xo{m}") for m in range(C)},
            **{f"h{f}": ("act", f"h{f}") for f in range(C)}, **{f"f{m}": ("dve", f"f{m}") for m in range(C)},
            **{f"t{s}": ("act", f"t{s}") for s in range(SUB)}}
NB_A, NB_B = 3, 2
QS0 = D0 ** -0.5 / WS
QS1 = D1 ** -0.5 / WS


def bank_before(ring, nbanks, unit):
    i = ring.index(unit)
    same = [j for j in range(len(ring)) if j % nbanks == i % nbanks]
    k = same.index(i)
    return (ring[same[k - 1]], 0) if k else (ring[same[-1]], 1)


def bank_a(unit):
    return RING_A.index(unit) % NB_A


def bank_b(unit):
    return RING_B.index(unit) % NB_B


def static_first(t):
    return isinstance(t, int) and t == 0


def batch_of(t):
    return t // TPB


def build(nc, x, ctxt, mask, mask_col, wq, wk, wv, wo, gq, gc, gout, wq1, wk1, wv1, wo1, w1t, b1, w2t, b2, out):
    stack = ExitStack()
    with stack:
        def sb(name, shape, dt=F32):
            return stack.enter_context(nc.sbuf_tensor(name, shape, dt))

        def sem(name):
            return stack.enter_context(nc.semaphore(name))

        WQ, WO, W1, W2 = (sb(n, [P, 2, C, D], F16) for n in ("WQ", "WO", "W1", "W2"))
        WQ1 = sb("WQ1", [P, 2, C, P], F16)
        WO1 = sb("WO1", [P, 2, 1, D], F16)
        ident = sb("ident", [P, P])
        gout_b = sb("gout_b", [P, D])
        gq_c, gc_c, b1_c, b2_c = (sb(n, [P, C]) for n in ("gq_c", "gc_c", "b1_c", "b2_c"))
        one = sb("one", [P, 1])
        mhalf = sb("mhalf", [P, SUB])
        img0 = sb("img0", [P, IMG0], F16)
        img1 = sb("img1", [P, IMG1], F16)
        o = 0
        Kst = img0[:, o:o + K0_ST].rearrange("p (h k) -> p h k", h=H0); o += K0_ST
        Kblk = img0[:, o:o + K0_BLK].rearrange("p (m k) -> p m k", m=G0); o += K0_BLK
        V0 = img0[:, o:o + K0_V].bitcast(F32); o += K0_V
        V0r = img0[:, o:o + K0_VR].bitcast(F32).rearrange("p (m k) -> p m k", m=G0); o += K0_VR
        E0 = img0[:, o:o + K0_E].bitcast(F32); o += K0_E
        E0r = img0[:, o:o + K0_ER].bitcast(F32)
        o = 0
        K1st = img1[:, o:o + K1_ST].rearrange("p (h k) -> p h k", h=H1); o += K1_ST
        K1blk = img1[:, o:o + K1_BLK]; o += K1_BLK
        V1 = img1[:, o:o + K1_V].bitcast(F32).rearrange("p (h k) -> p h k", h=H1); o += K1_V
        V1r = img1[:, o:o + K1_VR].bitcast(F32).rearrange("p (g k) -> p g k", g=G1)
        xin = sb("xin", [P, SUB, D])
        xn = sb("xn", [P, 2, D])
        ybuf = sb("ybuf", [P, SUB, D])
        AT = sb("AT", [P, 2, C, T], F16)
        Qs = sb("Qs", [P, 2, G0, T], F16)
        Qst = sb("Qst", [P, H0, T], F16)
        Pr = sb("Pr", [P, 10, T])
        Ou = sb("Ou", [P, G0, T])
        Dsb = sb("Dsb", [P, T])
        mx = sb("mx", [P, SUB, H0])
        negm = sb("negm", [H0, T], F16)
        dq = sb("dq", [P, SUB, H0])
        rq = sb("rq", [P, SUB, H0])
        junk = sb("junk", [P, D], F16)
        ss, r1, ssy, ry = (sb(n, [P, SUB]) for n in ("ss", "r1", "ssy", "ry"))
        ms, msy = sb("ms", [P, SUB]), sb("msy", [P, SUB])
        XT = sb("XT", [P, C, T])
        XS = sb("XS", [P, 2, C, T], F16)
        Q1s = sb("Q1s", [P, 2, T], F16)
        Q1st = sb("Q1st", [P, 4, T], F16)
        P1 = sb("P1", [P, 5, T])
        OD = sb("OD", [P, G1, T])
        rq1 = sb("rq1", [P, G1, SUB, 4])
        On1 = sb("On1", [P, SUB, P])
        O1s = sb("O1s", [P, 2, T], F16)
        mx1 = sb("mx1", [P, SUB, H1])
        negm1 = sb("negm1", [H1, T], F16)
        Ht = sb("Ht", [P, 2, T])
        HS = sb("HS", [P, 2, C, T], F16)
        outb = sb("outb", [P, 2, D])
        mrow_u8 = sb("mrow_u8", [P, SK], U8)
        mcol_u8, mrem_u8 = sb("mcol_u8", [P, 1], U8), sb("mrem_u8", [P, 1], U8)
        mcol, mrem = sb("mcol", [P, 1]), sb("mrem", [P, 1])
        quad, par, sel, valid = sb("quad", [P, 4]), sb("par", [P, 2]), sb("sel", [P, H1]), sb("valid", [P, 1])
        junk2 = sb("junk2", [P, D], F16)
        cntv, cntm, cntr = sb("cntv", [P, 1]), sb("cntm", [P, 1]), sb("cntr", [P, 1])
        ssc, msc, rsc = sb("ssc", [P, 2]), sb("msc", [P, 2]), sb("rsc", [P, 2])
        scl = sb("scl", [P, 2])
        csum, cnt, mean = sb("csum", [P, C]), sb("cnt", [P, 1]), sb("mean", [P, C])
        stage = [xin, ybuf]
        stage_small = Ou
        WKV = Qst[:, :, :].rearrange("p (w q c) n -> p w q c n", w=2, q=2)
        WKV1 = Q1st[:, :, :].rearrange("p (w q) (c n) -> p w q c n", w=2, c=C)
        crow = Pr
        cn = XT
        cT = OD[:, :, :].rearrange("p a b -> p (a b)")[:, 0:C * KA].rearrange("p (c k) -> p c k", c=C)
        ck32 = Ht[:, :, :].rearrange("p a b -> p (a b)")[:, 0:C * KA].rearrange("p (c k) -> p c k", c=C)
        inv = [outb[:, 0, 0:KA], outb[:, 1, 0:KA]]
        ATf = AT[:, :, :, :].rearrange("p a c t -> p (a c t)")
        cks = ATf[:, 0:2 * C * KA].rearrange("p (a c k) -> p a c k", a=2, c=C)
        cvs = ATf[:, 2 * C * KA:4 * C * KA].rearrange("p (a c k) -> p a c k", a=2, c=C)
        KTs = Qs[:, :, :, 0:KA]
        psum = [stack.enter_context(nc.psum_tensor(f"bank{i}", [P, T], F32)) for i in range(8)]
        ring_a, bank_o, bank_d, ring_b, bank_o1 = psum[0:3], psum[3], psum[4], psum[5:7], psum[7]
        image0 = nc.dram_tensor("image0", [B * P, IMG0 // 2], F32, kind="Internal").ap()
        image1 = nc.dram_tensor("image1", [B * P, IMG1 // 2], F32, kind="Internal").ap()

        const_ready, weights_in, vec_in = sem("const_ready"), sem("weights_in"), sem("vec_in")
        stage_in = [sem("stage_in0"), sem("stage_in1")]
        weight_hi, weight_split, weight_g = sem("weight_hi"), sem("weight_split"), sem("weight_g")
        pre_zero = sem("pre_zero")
        pre_act, pre_pool, pre_pe, pre_dve = (sem(n) for n in ("pre_act", "pre_pool", "pre_pe", "pre_dve"))
        ctx_in, image_out = sem("ctx_in"), sem("image_out")
        pre_tmp, pre_tmp2, pre_kt = sem("pre_tmp"), sem("pre_tmp2"), sem("pre_kt")
        N_ZERO = 9 + 6 + 1 + 4 * G1 + 2
        pe_a, act_a, dve_a, pool_a = (sem(n) for n in ("pe_a", "act_a", "dve_a", "pool_a"))
        pe_b, act_b, dve_b, pool_b = (sem(n) for n in ("pe_b", "act_b", "dve_b", "pool_b"))
        x_in, kv0_in, kv1_in = sem("x_in"), sem("kv0_in"), sem("kv1_in")
        stack0_in, stack1_in, max0_in, max1_in = (sem(n) for n in ("stack0_in", "stack1_in", "max0_in", "max1_in"))
        out_done = [sem("out_done0"), sem("out_done1")]
        N_STACK = 12 * 16

        block = stack.enter_context(nc.Block())

        BIG = [(wk, gc_c, lambda q, c: WKV[:, 0, q, c, :]), (wv, gc_c, lambda q, c: WKV[:, 1, q, c, :]),
               (wq, gq_c, lambda q, c: WQ[:, q, c, :]), (wo, None, lambda q, c: WO[:, q, c, :]),
               (w1t, None, lambda q, c: W1[:, q, c, :]), (w2t, None, lambda q, c: W2[:, q, c, :])]
        SMALL = [(wk1, lambda q: WKV1[:, 0, q, :, :].rearrange("p c n -> p (c n)")),
                 (wv1, lambda q: WKV1[:, 1, q, :, :].rearrange("p c n -> p (c n)")),
                 (wq1, lambda q: WQ1[:, q, :, :].rearrange("p c n -> p (c n)")),
                 (wo1, lambda q: WO1[:, q, 0, :])]

        def started(e):
            e.wait_ge(image_out, 32 * B)
            e.wait_ge(weight_split, 4 * len(BIG) + len(SMALL))

        @block.sync
        def _(sp):
            for v, dst in ((gq, gq_c), (gc, gc_c), (b1, b1_c), (b2, b2_c)):
                sp.dma_start(dst[:, :], v).then_inc(vec_in, 16)
            sp.dma_start(gout_b[:, :], gout.rearrange("(a n) -> a n", a=1).to_broadcast([P, D])).then_inc(vec_in, 16)
            for i, (w, _) in enumerate(SMALL):
                src = w.rearrange("(c p) n -> p c n", p=P)
                dst = stage_small[:, i, :].rearrange("p (c n) -> p c n", c=src.shape[1])
                sp.dma_start(dst, src).then_inc(weights_in, 16)
            for i, (w, _, _) in enumerate(BIG):
                if i >= 2:
                    sp.wait_ge(weight_split, 4 * (i - 1) + len(SMALL))
                    sp.wait_ge(stage_in[i % 2], 16 * (i // 2))
                sp.dma_start(stage[i % 2][:, :, :], w.rearrange("(c p) n -> p c n", p=P)).then_inc(stage_in[i % 2], 16)
            sp.wait_ge(pre_zero, N_ZERO)

            def load_context(b):
                sp.dma_start(crow[:, 0, :], ctxt[bass.ds(b * SK, KM), :]).then_inc(ctx_in, 16)
                sp.dma_start(crow[0:KR, 1, :], ctxt[bass.ds(b * SK + KM, KR), :]).then_inc(ctx_in, 16)
                sp.dma_start(mrow_u8[:, :], mask[bass.ds(b, 1), :].to_broadcast([P, SK])).then_inc(ctx_in, 16)
                sp.dma_start(mcol_u8[:, :], mask_col[bass.ds(b * SK, KM), :]).then_inc(ctx_in, 16)
                for j in range(4):
                    sp.dma_start(mrem_u8[32 * j:32 * j + KR, :],
                                 mask_col[bass.ds(b * SK + KM, KR), :]).then_inc(ctx_in, 16)

            def store_images(b):
                sp.wait_ge(pre_dve, PRE_DVE.upto(b, "vr0"))
                sp.dma_start(image0[bass.ds(b * P, P), :], img0[:, :].bitcast(F32)).then_inc(image_out, 16)
                sp.wait_ge(pre_dve, PRE_DVE.upto(b, "vr1"))
                sp.dma_start(image1[bass.ds(b * P, P), :], img1[:, :].bitcast(F32)).then_inc(image_out, 16)

            load_context(0)
            with sp.Fori(0, B - 1) as b:
                store_images(b)
                sp.wait_ge(image_out, 32 * b + 32)
                load_context(b + 1)
            store_images(B - 1)
            started(sp)

            def step(a, b_, x_next):
                if b_ is not None:
                    if not static_first(b_):
                        sp.wait_ge(pe_b, PE_B.upto(b_ - 1, "v1"))
                    sp.dma_start(img1[:, :].bitcast(F32), image1[bass.ds(batch_of(b_) * P, P), :]).then_inc(kv1_in, 16)
                if a is not None:
                    if not static_first(a):
                        sp.wait_ge(pe_a, PE_A.upto(a - 1, "v3"))
                    sp.dma_start(img0[:, :].bitcast(F32), image0[bass.ds(batch_of(a) * P, P), :]).then_inc(kv0_in, 16)
                if b_ is not None:
                    if not static_first(b_):
                        sp.wait_ge(pe_b, PE_B.upto(b_ - 1, "r1"))
                    sp.wait_ge(dve_b, DVE_B.upto(b_, "ql"))
                    sp.wait_ge(act_b, ACT_B.upto(b_, "qh"))
                    for piece, part in enumerate((0, 0, 1)):
                        for j in range(4):
                            sp.dma_start(Q1st[32 * piece:32 * piece + 32, j, :],
                                         Q1s[32 * j:32 * j + 32, part, :]).then_inc(stack1_in, 16)
                if a is not None:
                    if not static_first(a):
                        sp.wait_ge(pe_a, PE_A.upto(a - 1, "r3"))
                    sp.wait_ge(act_a, ACT_A.upto(a, "qh3"))
                    sp.wait_ge(dve_a, DVE_A.upto(a, "ql3"))
                    for piece, part in enumerate((0, 0, 1)):
                        for j in range(4):
                            sp.dma_start(Qst[32 * piece:32 * piece + 32, j::4, :],
                                         Qs[32 * j:32 * j + 32, part, :, :]).then_inc(stack0_in, 16)
                if b_ is not None:
                    sp.wait_ge(act_b, ACT_B.upto(b_, "negm"))
                    sp.dma_start(Q1st[96:98, :, :], negm1[:, :]).then_inc(max1_in, 16)
                if a is not None:
                    sp.wait_ge(act_a, ACT_A.upto(a, "negm"))
                    sp.dma_start(Qst[96:97, :, :], negm[:, :]).then_inc(max0_in, 16)
                if b_ is not None:
                    for s in range(SUB):
                        sp.wait_ge(act_b, ACT_B.upto(b_, f"t{s}"))
                        sp.dma_start(out[bass.ds(b_ * T + s * P, P), :], outb[:, s % 2, :]).then_inc(out_done[s % 2], 16)
                if x_next is not None:
                    sp.wait_ge(dve_a, DVE_A.upto(a, "y3"))
                    load_x(x_next)

            def load_x(t):
                sp.dma_start(xin[:, :, :], x[bass.ds(t * T, T), :].rearrange("(s p) d -> p s d", p=P)).then_inc(x_in, 16)

            load_x(0)
            step(0, None, 1)
            step(1, 0, 2)
            with sp.Fori(1, NT - 2) as i:
                step(i + 1, i, i + 2)
            step(NT - 1, NT - 2, None)
            step(None, NT - 1, None)
            for k in range(2):
                sp.wait_ge(out_done[k], 2 * 16 * NT)

        @block.gpsimd
        def _(pool):
            pool.memset(ident[:, :], 0.0).then_inc(const_ready, 1)
            pool.memset(quad[:, :], 0.0).then_inc(const_ready, 1)
            pool.memset(par[:, :], 0.0).then_inc(const_ready, 1)
            pool.memset(sel[:, :], 0.0).then_inc(const_ready, 1)
            pool.memset(mhalf[:, :], -0.5).then_inc(const_ready, 1)
            pool.memset(one[:, :], 1.0).then_inc(const_ready, 1)
            pool.memset(K1st, 0.0).then_inc(const_ready, 1)
            pool.wait_ge(const_ready, 7)
            pool.affine_select(out=ident[:, :], in_=ident[:, :], compare_op=ALU.not_equal, fill=1.0, base=0,
                               pattern=[[-1, P]], channel_multiplier=1).then_inc(const_ready, 1)
            pool.affine_select(out=sel[:, :], in_=sel[:, :], compare_op=ALU.is_gt, fill=1.0, base=0,
                               pattern=[[D1, H1]], channel_multiplier=-1).then_inc(const_ready, 1)
            pool.affine_select(out=quad[:, :], in_=quad[:, :], compare_op=ALU.is_gt, fill=1.0, base=0,
                               pattern=[[32, 4]], channel_multiplier=-1).then_inc(const_ready, 1)
            pool.wait_ge(const_ready, 10)
            pool.affine_select(out=sel[:, :], in_=sel[:, :], compare_op=ALU.is_gt, fill=0.0, base=D1,
                               pattern=[[D1, H1]], channel_multiplier=-1).then_inc(const_ready, 1)
            pool.affine_select(out=quad[:, :], in_=quad[:, :], compare_op=ALU.is_gt, fill=0.0, base=32,
                               pattern=[[32, 4]], channel_multiplier=-1).then_inc(const_ready, 1)
            pool.wait_ge(const_ready, 12)
            with pool.Fori(0, B) as b:
                pool.wait_ge(pre_dve, PRE_DVE.upto(b, "ms"))
                pool.tensor_tensor(rsc[:, :], msc[:, :], mhalf[:, 0:2], ALU.pow).then_inc(pre_pool, 1)
            started(pool)

            def norm_x(a):
                pool.wait_ge(dve_a, DVE_A.upto(a, "ms"))
                pool.tensor_tensor(r1[:, :], ms[:, :], mhalf[:, :], ALU.pow).then_inc(pool_a, 1)

            def spread(a, m):
                if m == 0:
                    pool.wait_ge(dve_a, DVE_A.upto(a, "rc"))
                if m >= 2:
                    pool.wait_ge(pe_a, PE_A.upto(a, f"rb{m - 2}"))
                pool.tensor_tensor(xn[:, m % 2, :].rearrange("p (s j r) -> p s j r", s=SUB, j=4),
                                   rq[:, :, 4 * m:4 * m + 4].unsqueeze(3).to_broadcast([P, SUB, 4, D0]),
                                   one[:, :].unsqueeze(2).unsqueeze(3).to_broadcast([P, SUB, 4, D0]),
                                   ALU.mult).then_inc(pool_a, 1)

            def norm_y(a):
                pool.wait_ge(dve_a, DVE_A.upto(a, "msy"))
                pool.tensor_tensor(ry[:, :], msy[:, :], mhalf[:, :], ALU.pow).then_inc(pool_a, 1)

            def add_b2(b_, m):
                pool.wait_ge(dve_b, DVE_B.upto(b_, f"xl{m}"))
                pool.tensor_tensor(XT[:, m, :], XT[:, m, :], b2_c[:, m:m + 1].to_broadcast([P, T]), ALU.add).then_inc(pool_b, 1)

            def step(a, b_):
                if a is not None:
                    norm_x(a)
                if b_ is not None:
                    for m in range(C):
                        add_b2(b_, m)
                if a is not None:
                    for m in range(G0):
                        spread(a, m)
                    norm_y(a)

            step(0, None)
            step(1, 0)
            with pool.Fori(1, NT - 1) as i:
                step(i + 1, i)
            step(None, NT - 1)

        @block.scalar
        def _(act):
            act.wait_ge(weights_in, 16 * len(SMALL))
            for i, (_, dst) in enumerate(SMALL):
                act.activation(dst(0), stage_small[:, i, :], ACT.Copy, scale=WS).then_inc(weight_hi, 1)
            act.wait_ge(vec_in, 16 * 5)
            for i, (_, g, dst) in enumerate(BIG):
                if g is None:
                    act.wait_ge(stage_in[i % 2], 16 * (i // 2 + 1))
                else:
                    act.wait_ge(weight_g, 4 * (i + 1))
                for c in range(C):
                    act.activation(dst(0, c), stage[i % 2][:, c, :], ACT.Copy, scale=WS).then_inc(weight_hi, 1)
            act.wait_ge(pre_zero, N_ZERO)
            with act.Fori(0, B) as b:
                act.wait_ge(ctx_in, 128 * b + 128)
                act.activation(junk[:, :], crow[:, 0, :], ACT.Square, accum_out=ssc[:, 0:1]).then_inc(pre_act, 1)
                act.activation(junk2[0:KP, :], crow[0:KP, 1, :], ACT.Square, accum_out=ssc[0:KP, 1:2]).then_inc(pre_act, 1)
            started(act)

            def norm_x(a):
                act.wait_ge(x_in, 16 * a + 16)
                for s in range(SUB):
                    if s >= 2:
                        act.wait_ge(act_a, ACT_A.upto(a, f"sq{s - 2}"))
                    act.activation(junk[:, :] if s % 2 else junk2[:, :], xin[:, s, :], ACT.Square,
                                   accum_out=ss[:, s:s + 1]).then_inc(act_a, 1)

            def x_hi(a, s):
                act.wait_ge(pe_a, PE_A.upto(a, f"xt{s}"))
                act.activation(AT[:, 0, :, s * P:(s + 1) * P], ring_a[bank_a(f"xt{s}")][:, :].rearrange(
                    "p (c q) -> p c q", c=C), ACT.Copy).then_inc(act_a, 1)

            def q_hi(a, m):
                act.wait_ge(pe_a, PE_A.upto(a, f"q{m}"))
                if m == 0 and not static_first(a):
                    act.wait_ge(stack0_in, N_STACK * a)
                act.activation(Qs[:, 0, m, :], ring_a[bank_a(f"q{m}")][:, :], ACT.Copy,
                               scale=QS0).then_inc(act_a, 1)

            def neg_max(a):
                act.wait_ge(pe_a, PE_A.upto(a, "mt"))
                if not static_first(a):
                    act.wait_ge(max0_in, 16 * a)
                act.activation(negm[:, :], ring_a[bank_a("mt")][0:H0, :], ACT.Copy, scale=-1.0).then_inc(act_a, 1)

            def exps(a, g):
                for j in range(5):
                    unit = f"s{g}{j}" if j < 4 else f"r{g}"
                    act.wait_ge(pe_a, PE_A.upto(a, unit))
                    act.activation(Pr[:, 5 * (g % 2) + j, :], ring_a[bank_a(unit)][:, :], ACT.Exp).then_inc(act_a, 1)

            def den(a):
                act.wait_ge(pe_a, PE_A.upto(a, "v3"))
                act.activation(Dsb[:, :], bank_d[:, :], ACT.Copy).then_inc(act_a, 1)

            def o_hi(a, m):
                act.wait_ge(dve_a, DVE_A.upto(a, f"on{m}"))
                act.activation(AT[:, 0, m, :], Ou[:, m, :], ACT.Copy).then_inc(act_a, 1)

            def y_sq(a, s):
                act.wait_ge(dve_a, DVE_A.upto(a, f"y{s}"))
                if s >= 2:
                    act.wait_ge(act_a, ACT_A.upto(a, f"sqy{s - 2}"))
                act.activation(junk[:, :] if s % 2 else junk2[:, :], ybuf[:, s, :], ACT.Square,
                               accum_out=ssy[:, s:s + 1]).then_inc(act_a, 1)

            def x2_evac(a, s):
                act.wait_ge(pe_a, PE_A.upto(a, f"x2t{s}"))
                src = ring_a[bank_a(f"x2t{s}")][:, :].rearrange("p (c q) -> p c q", c=C)
                act.activation(XT[:, :, s * P:(s + 1) * P], src, ACT.Copy).then_inc(act_a, 1)
                act.activation(XS[:, 0, :, s * P:(s + 1) * P], src, ACT.Copy).then_inc(act_a, 1)

            def q1_hi(b_):
                act.wait_ge(pe_b, PE_B.upto(b_, "q"))
                if not static_first(b_):
                    act.wait_ge(stack1_in, N_STACK * b_)
                act.activation(Q1s[:, 0, :], ring_b[bank_b("q")][:, :], ACT.Copy, scale=QS1).then_inc(act_b, 1)

            def neg_max1(b_):
                act.wait_ge(pe_b, PE_B.upto(b_, "mt"))
                if not static_first(b_):
                    act.wait_ge(max1_in, 16 * b_)
                act.activation(negm1[:, :], ring_b[bank_b("mt")][0:H1, :], ACT.Copy, scale=-1.0).then_inc(act_b, 1)

            def exps1(b_, g):
                for j in range(5):
                    unit = f"s{g}{j}" if j < 4 else f"r{g}"
                    act.wait_ge(pe_b, PE_B.upto(b_, unit))
                    act.activation(P1[:, j, :], ring_b[bank_b(unit)][:, :], ACT.Exp).then_inc(act_b, 1)

            def od(b_, g):
                act.wait_ge(pe_b, PE_B.upto(b_, f"v{g}"))
                act.activation(OD[:, g, :], bank_o1[:, :], ACT.Copy).then_inc(act_b, 1)

            def o1_hi(b_):
                act.wait_ge(pe_b, PE_B.upto(b_, "ot"))
                act.activation(O1s[:, 0, :], ring_b[bank_b("ot")][:, :], ACT.Copy).then_inc(act_b, 1)

            def x_split(b_, m):
                act.wait_ge(dve_b, DVE_B.upto(b_, f"xo{m}"))
                act.activation(XS[:, 0, m, :], XT[:, m, :], ACT.Copy).then_inc(act_b, 1)

            def hidden(b_, f):
                act.wait_ge(pe_b, PE_B.upto(b_, f"h{f}"))
                if f >= 2:
                    act.wait_ge(dve_b, DVE_B.upto(b_, f"hl{f - 2}"))
                act.activation(Ht[:, f % 2, :], ring_b[bank_b(f"h{f}")][:, :], ACT.Relu, bias=b1_c[:, f:f + 1],
                               scale=1.0 / WS).then_inc(act_b, 1)

            def out_copy(b_, s):
                act.wait_ge(pe_b, PE_B.upto(b_, f"t{s}"))
                if s >= 2 or not static_first(b_):
                    act.wait_ge(out_done[s % 2], 16 * (2 * b_ + s // 2))
                act.activation(outb[:, s % 2, :], ring_b[bank_b(f"t{s}")][:, :], ACT.Copy).then_inc(act_b, 1)

            def step(a, b_):
                A, Bq = a is not None, b_ is not None
                if A: norm_x(a)
                if Bq: q1_hi(b_)
                if A:
                    for s in range(SUB):
                        x_hi(a, s)
                    for m in range(G0):
                        q_hi(a, m)
                if Bq:
                    neg_max1(b_)
                    exps1(b_, 0)
                    od(b_, 0)
                    exps1(b_, 1)
                    od(b_, 1)
                    o1_hi(b_)
                    for m in range(C):
                        x_split(b_, m)
                    hidden(b_, 0)
                    hidden(b_, 1)
                if A: neg_max(a)
                if Bq:
                    hidden(b_, 2)
                    hidden(b_, 3)
                if A:
                    for g in range(G0):
                        exps(a, g)
                    den(a)
                    for m in range(G0):
                        o_hi(a, m)
                if Bq:
                    for s in range(SUB):
                        out_copy(b_, s)
                if A:
                    for s in range(SUB):
                        y_sq(a, s)
                    for s in range(SUB):
                        x2_evac(a, s)

            step(0, None)
            step(1, 0)
            with act.Fori(1, NT - 1) as i:
                step(i + 1, i)
            step(None, NT - 1)

        @block.vector
        def _(dve):
            zeroed = [(img0[:, :].bitcast(F32), 0.0), (img1[:, K1_ST:].bitcast(F32), 0.0), (crow[:, 1, :], 0.0),
                      (cn[:, 1, :], 0.0), (mrem_u8[:, :], 0), (inv[0], 1.0), (inv[1], 0.0), (ssc[:, :], 1.0),
                      (valid[:, :], 0.0)]
            for ap, v in zeroed:
                dve.memset(ap, v).then_inc(pre_zero, 1)
            dve.wait_ge(pre_zero, len(zeroed))
            later = [(Kst[96:97, :, :], 1.0), (inv[1][:, SK:KA], 1.0)] \
                + [(valid[32 * j:32 * j + KR, :], 1.0) for j in range(4)]
            for ap, v in later:
                dve.memset(ap, v).then_inc(pre_zero, 1)
            dve.wait_ge(pre_zero, len(zeroed) + len(later))
            dve.memset(V1[:, :, D1:2 * D1], 1.0).then_inc(pre_zero, 1)
            for g in range(G1):
                for j in range(4):
                    dve.tensor_copy(V1r[32 * j:32 * j + 32, g, 32 * j + D1:32 * j + 2 * D1],
                                    valid[32 * j:32 * j + 32, :].to_broadcast([32, D1])).then_inc(pre_zero, 1)
            dve.wait_ge(const_ready, 12)
            dve.tensor_copy(K1st[96:98, :, :].rearrange("p (j a) k -> p j a k", a=2),
                            ident[96:98, 96:98].unsqueeze(1).unsqueeze(3).to_broadcast([2, 4, 2, KA])).then_inc(pre_zero, 1)
            dve.tensor_reduce(par[:, :], sel[:, :].rearrange("p (j a) -> p a j", a=2), AX.X, ALU.add).then_inc(pre_zero, 1)

            for i, (_, dst) in enumerate(SMALL):
                dve.wait_ge(weight_hi, i + 1)
                dve.scalar_tensor_tensor(dst(1), stage_small[:, i, :], WS, dst(0), ALU.mult, ALU.subtract).then_inc(weight_split, 1)
            dve.wait_ge(vec_in, 16 * 5)
            done_g = 0
            for i, (_, g, dst) in enumerate(BIG):
                if g is not None:
                    dve.wait_ge(stage_in[i % 2], 16 * (i // 2 + 1))
                    for c in range(C):
                        dve.tensor_scalar(stage[i % 2][:, c, :], stage[i % 2][:, c, :], g[:, c:c + 1], None,
                                          ALU.mult).then_inc(weight_g, 1)
                for c in range(C):
                    dve.wait_ge(weight_hi, len(SMALL) + 4 * i + c + 1)
                    dve.scalar_tensor_tensor(dst(1, c), stage[i % 2][:, c, :], WS, dst(0, c), ALU.mult,
                                             ALU.subtract).then_inc(weight_split, 1)

            with dve.Fori(0, B) as b:
                def done(name):
                    dve.wait_ge(pre_dve, PRE_DVE.upto(b, name))

                dve.wait_ge(ctx_in, 128 * b + 128)
                dve.tensor_copy(mcol[:, :], mcol_u8[:, :])
                dve.tensor_copy(mrem[:, :], mrem_u8[:, :])
                dve.tensor_scalar(inv[0][:, 0:SK], mrow_u8[:, :], -1.0, 1.0, ALU.mult, ALU.add).then_inc(pre_dve, 1)
                dve.wait_ge(pre_act, PRE_ACT.upto(b, "sqr"))
                dve.tensor_scalar(msc[:, :], ssc[:, :], 1.0 / D, EPS, ALU.mult, ALU.add).then_inc(pre_dve, 1)
                dve.wait_ge(pre_pool, PRE_POOL.upto(b, "r"))
                dve.tensor_tensor(scl[:, 0:1], rsc[:, 0:1], mcol[:, :], ALU.mult)
                dve.tensor_tensor(scl[:, 1:2], rsc[:, 1:2], mrem[:, :], ALU.mult).then_inc(pre_dve, 1)
                done("sc0")
                dve.tensor_scalar(cn[:, 0, :], crow[:, 0, :], scl[:, 0:1], None, ALU.mult)
                dve.tensor_scalar(cn[0:KP, 1, :], crow[0:KP, 1, :], scl[0:KP, 1:2], None, ALU.mult).then_inc(pre_dve, 1)
                for layer in range(2):
                    L = str(layer)
                    dve.wait_ge(pre_pe, PRE_PE.upto(b, "tb" + L))
                    dve.tensor_copy(cT[:, :, 0:KM], psum[0][:, :].rearrange("p (c k) -> p c k", c=C))
                    dve.tensor_copy(cT[:, :, KM:KA], psum[1][:, 0:C * KP].rearrange("p (c k) -> p c k", c=C)).then_inc(pre_dve, 1)
                    done("ct" + L)
                    dve.tensor_reduce(csum[:, :], cT, AX.X, ALU.add)
                    dve.tensor_reduce(cnt[:, :], inv[layer][:, 0:SK], AX.X, ALU.add).then_inc(pre_dve, 1)
                    done("sum" + L)
                    dve.tensor_scalar(cntv[:, :], cnt[:, :], -1.0, float(SK), ALU.mult, ALU.add).then_inc(pre_tmp, 1)
                    dve.wait_ge(pre_tmp, 6 * b + 3 * layer + 1)
                    dve.tensor_scalar(cntm[:, :], cntv[:, :], 1.0, None, ALU.max).then_inc(pre_tmp, 1)
                    dve.wait_ge(pre_tmp, 6 * b + 3 * layer + 2)
                    dve.reciprocal(cntr[:, :], cntm[:, :]).then_inc(pre_tmp, 1)
                    dve.wait_ge(pre_tmp, 6 * b + 3 * layer + 3)
                    dve.tensor_scalar(mean[:, :], csum[:, :], cntr[:, :], None, ALU.mult).then_inc(pre_dve, 1)
                    done("mean" + L)
                    for c in range(C):
                        ins = dve.scalar_tensor_tensor(ck32[:, c, :], inv[layer], mean[:, c:c + 1], cT[:, c, :],
                                                       ALU.mult, ALU.add)
                    dve.tensor_copy(cvs[:, 0, :, :], cT).then_inc(pre_dve, 1)
                    done("ck" + L)
                    dve.tensor_copy(cks[:, 0, :, :], ck32)
                    dve.tensor_tensor(cvs[:, 1, :, :], cT, cvs[:, 0, :, :], ALU.subtract).then_inc(pre_tmp2, 1)
                    dve.wait_ge(pre_tmp2, 2 * b + layer + 1)
                    dve.tensor_tensor(cks[:, 1, :, :], ck32, cks[:, 0, :, :], ALU.subtract).then_inc(pre_dve, 1)
                    if layer == 0:
                        for m in range(G0):
                            dve.wait_ge(pre_pe, PRE_PE.upto(b, f"k{m}"))
                            dve.tensor_scalar(KTs[:, 0, m, :], psum[2 + m][:, 0:KA], 1.0 / WS, None, ALU.mult).then_inc(pre_kt, 1)
                            dve.wait_ge(pre_kt, 5 * b + m + 1)
                            dve.scalar_tensor_tensor(KTs[:, 1, m, :], psum[2 + m][:, 0:KA], 1.0 / WS, KTs[:, 0, m, :],
                                                     ALU.mult, ALU.subtract).then_inc(pre_dve, 1)
                        done("k0_3")
                        for j in range(4):
                            for piece, part in enumerate((0, 1, 0)):
                                dve.tensor_copy(Kst[32 * piece:32 * piece + 32, j::4, :],
                                                KTs[32 * j:32 * j + 32, part, :, :])
                            ins = dve.tensor_copy(Kblk[32 * j:32 * j + 32, :, j * SK:(j + 1) * SK],
                                                  KTs[32 * j:32 * j + 32, 0, :, 0:SK])
                        ins.then_inc(pre_dve, 1)
                        dve.wait_ge(pre_pe, PRE_PE.upto(b, "v0"))
                        dve.tensor_copy(E0[:, 0:3 * 33 + 1:33], mcol[:, :].to_broadcast([P, 4]))
                        dve.tensor_scalar(E0r[:, 4:8], quad[:, :], mrem[:, :], None, ALU.mult)
                        dve.tensor_scalar(V0, psum[6][:, :], 1.0 / WS, None, ALU.mult).then_inc(pre_dve, 1)
                        dve.wait_ge(pre_pe, PRE_PE.upto(b, "vr0"))
                        for j in range(4):
                            q = slice(32 * j, 32 * j + 32)
                            ins = dve.tensor_scalar(V0r[q, :, 32 * j:32 * j + 32], psum[7][q, 0:G0 * D0].rearrange(
                                "p (m d) -> p m d", m=G0), 1.0 / WS, None, ALU.mult)
                        ins.then_inc(pre_dve, 1)
                    else:
                        dve.wait_ge(pre_pe, PRE_PE.upto(b, "kk"))
                        dve.tensor_scalar(KTs[:, 0, 0, :], psum[2][:, 0:KA], 1.0 / WS, None, ALU.mult).then_inc(pre_kt, 1)
                        dve.wait_ge(pre_kt, 5 * b + 5)
                        dve.scalar_tensor_tensor(KTs[:, 1, 0, :], psum[2][:, 0:KA], 1.0 / WS, KTs[:, 0, 0, :],
                                                 ALU.mult, ALU.subtract).then_inc(pre_dve, 1)
                        done("kk")
                        for a in range(2):
                            ins = dve.tensor_scalar(KTs[:, :, 1 + a, :], KTs[:, :, 0, :], par[:, a:a + 1], None, ALU.mult)
                        ins.then_inc(pre_dve, 1)
                        done("km")
                        for j in range(4):
                            for piece, part in enumerate((0, 1, 0)):
                                dve.tensor_copy(K1st[32 * piece:32 * piece + 32, 2 * j:2 * j + 2, :],
                                                KTs[32 * j:32 * j + 32, part, 1:3, :])
                        for h in range(H1):
                            ins = dve.tensor_scalar(K1blk[:, h * SK:(h + 1) * SK], KTs[:, 0, 0, 0:SK], sel[:, h:h + 1],
                                                    None, ALU.mult)
                        ins.then_inc(pre_dve, 1)
                        dve.wait_ge(pre_pe, PRE_PE.upto(b, "v1"))
                        dve.tensor_scalar(V1[:, :, 0:D1], psum[6][:, 0:H1 * D1].rearrange("p (h d) -> p h d", h=H1),
                                          1.0 / WS, None, ALU.mult).then_inc(pre_dve, 1)
                        dve.wait_ge(pre_pe, PRE_PE.upto(b, "vr1"))
                        for j in range(4):
                            q = slice(32 * j, 32 * j + 32)
                            ins = dve.tensor_scalar(V1r[q, :, 32 * j:32 * j + D1], psum[7][q, 0:G1 * D1].rearrange(
                                "p (g d) -> p g d", g=G1), 1.0 / WS, None, ALU.mult)
                        ins.then_inc(pre_dve, 1)
            started(dve)

            def norm_x(a, s):
                if s == 0:
                    dve.wait_ge(act_a, ACT_A.upto(a, "sq3"))
                    dve.tensor_scalar(ms[:, :], ss[:, :], 1.0 / D, EPS, ALU.mult, ALU.add).then_inc(dve_a, 1)
                    dve.wait_ge(pool_a, POOL_A.upto(a, "r"))
                if s >= 2:
                    dve.wait_ge(pe_a, PE_A.upto(a, f"xt{s - 2}"))
                dve.tensor_scalar(xn[:, s % 2, :], xin[:, s, :], r1[:, s:s + 1], None, ALU.mult).then_inc(dve_a, 1)

            def x_lo(a, s):
                dve.wait_ge(act_a, ACT_A.upto(a, f"xh{s}"))
                q = slice(s * P, (s + 1) * P)
                dve.tensor_tensor(AT[:, 1, :, q], ring_a[bank_a(f"xt{s}")][:, :].rearrange("p (c q) -> p c q", c=C),
                                  AT[:, 0, :, q], ALU.subtract).then_inc(dve_a, 1)

            def q_lo(a, m):
                dve.wait_ge(act_a, ACT_A.upto(a, f"qh{m}"))
                if m == 0 and not static_first(a):
                    dve.wait_ge(stack0_in, N_STACK * a)
                dve.scalar_tensor_tensor(Qs[:, 1, m, :], ring_a[bank_a(f"q{m}")][:, :], QS0, Qs[:, 0, m, :],
                                         ALU.mult, ALU.subtract).then_inc(dve_a, 1)

            def maxima(a, n):
                s, m, half = n // 8, n % 8 // 2, n % 2
                dve.wait_ge(pe_a, PE_A.upto(a, f"m{n}"))
                dve.tensor_reduce(mx[:, s, 4 * m + 2 * half:4 * m + 2 * half + 2],
                                  ring_a[bank_a(f"m{n}")][:, 0:UNIT].rearrange("p (h k) -> p h k", h=2),
                                  AX.X, ALU.max).then_inc(dve_a, 1)

            def o_evac(a, m):
                dve.wait_ge(pe_a, PE_A.upto(a, f"v{m}"))
                dve.tensor_copy(Ou[:, m, :], bank_o[:, :]).then_inc(dve_a, 1)

            def den(a):
                dve.wait_ge(pe_a, PE_A.upto(a, "dt"))
                src = ring_a[bank_a("dt")][:, :].rearrange("p (s r) -> p s r", s=SUB)
                main = src.rearrange("p s (j m) -> p s m j", j=4)[:, :, 0:4, :]
                rest = src.rearrange("p s (m j) -> p s m j", m=4)[:, :, :, 4:8]
                dst = dq[:, :, :].rearrange("p s (m j) -> p s m j", m=4)
                dve.tensor_copy(dst, main).then_inc(dve_a, 1)
                dve.wait_ge(dve_a, DVE_A.upto(a, "dm"))
                dve.tensor_tensor(rq[:, :, :].rearrange("p s (m j) -> p s m j", m=4), rest, dst, ALU.add).then_inc(dve_a, 1)
                dve.wait_ge(dve_a, DVE_A.upto(a, "dd"))
                dve.tensor_scalar(dq[:, :, :], rq[:, :, :], 1e-30, None, ALU.max).then_inc(dve_a, 1)
                dve.wait_ge(dve_a, DVE_A.upto(a, "dg"))
                dve.reciprocal(rq[:, :, :], dq[:, :, :]).then_inc(dve_a, 1)

            def o_norm(a, m):
                dve.wait_ge(pe_a, PE_A.upto(a, f"rb{m}"))
                if m == 0:
                    dve.wait_ge(dve_a, DVE_A.upto(a, "o3"))
                dve.tensor_tensor(Ou[:, m, :], ring_a[bank_a(f"rb{m}")][:, :], Ou[:, m, :], ALU.mult).then_inc(dve_a, 1)

            def o_lo(a, m):
                dve.wait_ge(act_a, ACT_A.upto(a, f"oh{m}"))
                dve.tensor_tensor(AT[:, 1, m, :], Ou[:, m, :], AT[:, 0, m, :], ALU.subtract).then_inc(dve_a, 1)

            def residual_y(a, s):
                dve.wait_ge(pe_a, PE_A.upto(a, f"y{s}"))
                dve.scalar_tensor_tensor(ybuf[:, s, :], ring_a[bank_a(f"y{s}")][:, :], 1.0 / WS, xin[:, s, :],
                                         ALU.mult, ALU.add).then_inc(dve_a, 1)

            def norm_y(a, s):
                if s == 0:
                    dve.wait_ge(act_a, ACT_A.upto(a, "sqy3"))
                    dve.tensor_scalar(msy[:, :], ssy[:, :], 1.0 / D, EPS, ALU.mult, ALU.add).then_inc(dve_a, 1)
                    dve.wait_ge(pool_a, POOL_A.upto(a, "ry"))
                dve.scalar_tensor_tensor(ybuf[:, s, :], ybuf[:, s, :], ry[:, s:s + 1], gout_b[:, :], ALU.mult,
                                         ALU.mult).then_inc(dve_a, 1)

            def x2_lo(a, s):
                dve.wait_ge(act_a, ACT_A.upto(a, f"x2h{s}"))
                q = slice(s * P, (s + 1) * P)
                dve.tensor_tensor(XS[:, 1, :, q], ring_a[bank_a(f"x2t{s}")][:, :].rearrange("p (c q) -> p c q", c=C),
                                  XS[:, 0, :, q], ALU.subtract).then_inc(dve_a, 1)

            def q1_lo(b_):
                dve.wait_ge(act_b, ACT_B.upto(b_, "qh"))
                if not static_first(b_):
                    dve.wait_ge(stack1_in, N_STACK * b_)
                dve.scalar_tensor_tensor(Q1s[:, 1, :], ring_b[bank_b("q")][:, :], QS1, Q1s[:, 0, :],
                                         ALU.mult, ALU.subtract).then_inc(dve_b, 1)

            def maxima1(b_, n):
                s, j = n // 4, n % 4
                dve.wait_ge(pe_b, PE_B.upto(b_, f"m{n}"))
                dve.tensor_reduce(mx1[:, s, j::4], ring_b[bank_b(f"m{n}")][:, 0:UNIT].rearrange("p (h k) -> p h k", h=2),
                                  AX.X, ALU.max).then_inc(dve_b, 1)

            def o1_norm(b_, g):
                src = ring_b[bank_b(f"od{g}")][:, :].rearrange("p (s j k) -> p s j k", s=SUB, j=4)
                dve.wait_ge(pe_b, PE_B.upto(b_, f"od{g}"))
                dve.reciprocal(rq1[:, g, :, :].unsqueeze(3), src[:, :, :, D1:D1 + 1]).then_inc(dve_b, 1)
                dve.wait_ge(dve_b, DVE_B.upto(b_, f"rc{g}"))
                dst = On1[:, :, 64 * g:64 * g + 64].rearrange("p s (j d) -> p s j d", j=4)
                dve.tensor_tensor(dst, src[:, :, :, 0:D1], rq1[:, g, :, :].unsqueeze(3).to_broadcast([P, SUB, 4, D1]),
                                  ALU.mult).then_inc(dve_b, 1)

            def o1_lo(b_):
                dve.wait_ge(act_b, ACT_B.upto(b_, "oh"))
                dve.tensor_tensor(O1s[:, 1, :], ring_b[bank_b("ot")][:, :], O1s[:, 0, :], ALU.subtract).then_inc(dve_b, 1)

            def residual_x(b_, m):
                dve.wait_ge(pe_b, PE_B.upto(b_, f"xo{m}"))
                dve.scalar_tensor_tensor(XT[:, m, :], ring_b[bank_b(f"xo{m}")][:, :], 1.0 / WS, XT[:, m, :],
                                         ALU.mult, ALU.add).then_inc(dve_b, 1)

            def x_split(b_, m):
                dve.wait_ge(act_b, ACT_B.upto(b_, f"xh{m}"))
                dve.tensor_tensor(XS[:, 1, m, :], XT[:, m, :], XS[:, 0, m, :], ALU.subtract).then_inc(dve_b, 1)

            def hidden(b_, f):
                dve.wait_ge(act_b, ACT_B.upto(b_, f"h{f}"))
                dve.tensor_copy(HS[:, 0, f, :], Ht[:, f % 2, :]).then_inc(dve_b, 1)
                dve.wait_ge(dve_b, DVE_B.upto(b_, f"hh{f}"))
                dve.tensor_tensor(HS[:, 1, f, :], Ht[:, f % 2, :], HS[:, 0, f, :], ALU.subtract).then_inc(dve_b, 1)

            def residual_out(b_, m):
                dve.wait_ge(pe_b, PE_B.upto(b_, f"f{m}"))
                dve.wait_ge(pool_b, POOL_B.upto(b_, f"xb{m}"))
                dve.scalar_tensor_tensor(XT[:, m, :], ring_b[bank_b(f"f{m}")][:, :], 1.0 / WS, XT[:, m, :],
                                         ALU.mult, ALU.add).then_inc(dve_b, 1)

            def step(a, b_):
                A, Bq = a is not None, b_ is not None
                if A:
                    for s in range(SUB):
                        norm_x(a, s)
                if Bq: q1_lo(b_)
                if A:
                    for s in range(SUB):
                        x_lo(a, s)
                for m in range(4):
                    if A: q_lo(a, m)
                    if Bq:
                        for n in range(4 * m, 4 * m + 4):
                            maxima1(b_, n)
                if A:
                    for n in range(24):
                        maxima(a, n)
                if Bq:
                    o1_norm(b_, 0)
                    o1_norm(b_, 1)
                    o1_lo(b_)
                    residual_x(b_, 0)
                    residual_x(b_, 1)
                    x_split(b_, 0)
                    residual_x(b_, 2)
                    x_split(b_, 1)
                    residual_x(b_, 3)
                    x_split(b_, 2)
                    x_split(b_, 3)
                if A:
                    for n in range(24, 32):
                        maxima(a, n)
                if Bq:
                    for f in range(C):
                        hidden(b_, f)
                if A:
                    for m in range(G0):
                        o_evac(a, m)
                    den(a)
                if Bq:
                    residual_out(b_, 0)
                    residual_out(b_, 1)
                if A:
                    o_norm(a, 0)
                    o_lo(a, 0)
                    o_norm(a, 1)
                    o_lo(a, 1)
                if Bq: residual_out(b_, 2)
                if A:
                    o_norm(a, 2)
                    o_lo(a, 2)
                    o_norm(a, 3)
                    o_lo(a, 3)
                if Bq: residual_out(b_, 3)
                if A:
                    for s in range(SUB):
                        residual_y(a, s)
                    for s in range(SUB):
                        norm_y(a, s)
                    for s in range(SUB):
                        x2_lo(a, s)

            step(0, None)
            step(1, 0)
            with dve.Fori(1, NT - 1) as i:
                step(i + 1, i)
            step(None, NT - 1)

        @block.tensor
        def _(pe):
            PASSES = ((0, 0), (1, 0), (0, 1))

            def split_matmul(dst, lhs, rhs, chunks):
                n, last = 0, len(PASSES) * chunks
                for c in range(chunks):
                    for p, q in PASSES:
                        n += 1
                        ins = pe.matmul(dst, lhs(p, c), rhs(q, c), start=n == 1, stop=n == last)
                return ins

            pe.wait_ge(const_ready, 8)
            pe.wait_ge(weight_split, 4 * 2 + len(SMALL))
            with pe.Fori(0, B) as b:
                for layer in range(2):
                    L = str(layer)
                    src = cn if layer == 0 else crow
                    if layer == 0:
                        pe.wait_ge(pre_dve, PRE_DVE.upto(b, "cn0"))
                    else:
                        pe.wait_ge(pre_dve, PRE_DVE.upto(b, "vr0"))
                    for c in range(C):
                        ins = pe.transpose(psum[0][:, c * P:(c + 1) * P], src[:, 0, c * P:(c + 1) * P], ident[:, :])
                    ins.then_inc(pre_pe, 1)
                    for c in range(C):
                        ins = pe.transpose(psum[1][:, c * KP:(c + 1) * KP], src[0:KP, 1, c * P:(c + 1) * P],
                                           ident[0:KP, 0:KP])
                    ins.then_inc(pre_pe, 1)
                    pe.wait_ge(pre_dve, PRE_DVE.upto(b, "cks" + L))
                    if layer == 0:
                        for m in range(G0):
                            split_matmul(psum[2 + m][:, 0:KA], lambda p, c: WKV[:, 0, p, c, m * P:(m + 1) * P],
                                         lambda q, c: cks[:, q, c, :], C).then_inc(pre_pe, 1)
                        split_matmul(psum[6][:, :], lambda p, c: cvs[:, p, c, 0:KM],
                                     lambda q, c: WKV[:, 1, q, c, :], C).then_inc(pre_pe, 1)
                        for j in range(4):
                            ins = split_matmul(
                                psum[7][32 * j:32 * j + 32, 0:G0 * D0], lambda p, c: cvs[:, p, c, KM:KA],
                                lambda q, c: WKV[:, 1, q, c, :].rearrange("p (m n) -> p m n", m=G0)[
                                    :, :, 32 * j:32 * j + 32], C)
                        ins.then_inc(pre_pe, 1)
                    else:
                        split_matmul(psum[2][:, 0:KA], lambda p, c: WKV1[:, 0, p, c, :],
                                     lambda q, c: cks[:, q, c, :], C).then_inc(pre_pe, 1)
                        split_matmul(psum[6][:, 0:P], lambda p, c: cvs[:, p, c, 0:KM],
                                     lambda q, c: WKV1[:, 1, q, c, :], C).then_inc(pre_pe, 1)
                        for j in range(4):
                            ins = split_matmul(
                                psum[7][32 * j:32 * j + 32, 0:G1 * D1], lambda p, c: cvs[:, p, c, KM:KA],
                                lambda q, c: WKV1[:, 1, q, c, :].rearrange("p (g n) -> p g n", g=G1)[
                                    :, :, D1 * j:D1 * j + D1], C)
                        ins.then_inc(pre_pe, 1)
            started(pe)

            def wait_bank(ring, nbanks, reader, sems, steps, t, unit):
                before, ago = bank_before(ring, nbanks, unit)
                if ago and static_first(t):
                    return
                engine, name = reader[before]
                pe.wait_ge(sems[engine], steps[engine].upto(t - ago, name))

            def free_a(a, unit):
                wait_bank(RING_A, NB_A, READER_A, {"act": act_a, "dve": dve_a}, {"act": ACT_A, "dve": DVE_A}, a, unit)
                return ring_a[bank_a(unit)]

            def free_b(b_, unit):
                wait_bank(RING_B, NB_B, READER_B, {"act": act_b, "dve": dve_b}, {"act": ACT_B, "dve": DVE_B}, b_, unit)
                return ring_b[bank_b(unit)]

            def x_transpose(a, s):
                bank = free_a(a, f"xt{s}")
                pe.wait_ge(dve_a, DVE_A.upto(a, f"xn{s}"))
                for c in range(C):
                    ins = pe.transpose(bank[:, c * P:(c + 1) * P], xn[:, s % 2, c * P:(c + 1) * P], ident[:, :])
                ins.then_inc(pe_a, 1)

            def query(a, m):
                bank = free_a(a, f"q{m}")
                if m == 0:
                    pe.wait_ge(dve_a, DVE_A.upto(a, "xl3"))
                split_matmul(bank[:, :], lambda p, c: WQ[:, p, c, m * P:(m + 1) * P],
                             lambda q, c: AT[:, q, c, :], C).then_inc(pe_a, 1)

            def max_unit(a, n):
                s, m, half = n // 8, n % 8 // 2, n % 2
                bank = free_a(a, f"m{n}")
                if n == 0:
                    pe.wait_ge(act_a, ACT_A.upto(a, "qh3"))
                    pe.wait_ge(kv0_in, 16 * a + 16)
                pe.matmul(bank[:, 0:UNIT], Qs[:, 0, m, s * P:(s + 1) * P], Kblk[:, m, half * UNIT:(half + 1) * UNIT],
                          start=True, stop=True).then_inc(pe_a, 1)

            def max_transpose(a):
                bank = free_a(a, "mt")
                pe.wait_ge(dve_a, DVE_A.upto(a, "mx31"))
                for s in range(SUB):
                    ins = pe.transpose(bank[0:H0, s * P:(s + 1) * P], mx[:, s, :], ident[:, :])
                ins.then_inc(pe_a, 1)

            def scores(a, g):
                if g == 0:
                    pe.wait_ge(stack0_in, N_STACK * (a + 1))
                    pe.wait_ge(max0_in, 16 * a + 16)
                for j in range(4):
                    bank = free_a(a, f"s{g}{j}")
                    pe.matmul(bank[:, :], Kst[0:97, 4 * g + j, 0:KM], Qst[0:97, 4 * g + j, :],
                              start=True, stop=True).then_inc(pe_a, 1)
                bank = free_a(a, f"r{g}")
                for j in range(4):
                    ins = pe.matmul(bank[32 * j:32 * j + 32, :], Kst[0:97, 4 * g + j, KM:KA], Qst[0:97, 4 * g + j, :],
                                    start=True, stop=True)
                ins.then_inc(pe_a, 1)

            def values(a, g):
                slot = 5 * (g % 2)
                if g:
                    pe.wait_ge(dve_a, DVE_A.upto(a, f"o{g - 1}"))
                elif not static_first(a):
                    pe.wait_ge(dve_a, DVE_A.upto(a - 1, "o3"))
                    pe.wait_ge(act_a, ACT_A.upto(a - 1, "dsb"))
                pe.wait_ge(act_a, ACT_A.upto(a, f"er{g}"))
                pe.matmul(bank_o[:, :], V0r[:, g, :], Pr[:, slot + 4, :], start=True, stop=False)
                for j in range(4):
                    h = 4 * g + j
                    pe.matmul(bank_o[32 * j:32 * j + 32, :], V0[:, h * D0:(h + 1) * D0], Pr[:, slot + j, :],
                              start=False, stop=True)
                for j in range(4):
                    pe.matmul(bank_d[32 * j:32 * j + 32, :], E0[:, 32 * g:32 * g + 32], Pr[:, slot + j, :],
                              start=g == 0, stop=False, skip_group_check=True)
                pe.matmul(bank_d[32 * g:32 * g + 32, :], E0r[:, :], Pr[:, slot + 4, :],
                          start=False, stop=g == G0 - 1, skip_group_check=True).then_inc(pe_a, 1)

            def den_transpose(a):
                bank = free_a(a, "dt")
                pe.wait_ge(act_a, ACT_A.upto(a, "dsb"))
                for s in range(SUB):
                    ins = pe.transpose(bank[:, s * P:(s + 1) * P], Dsb[:, s * P:(s + 1) * P], ident[:, :])
                ins.then_inc(pe_a, 1)

            def den_spread(a, m):
                bank = free_a(a, f"rb{m}")
                pe.wait_ge(pool_a, POOL_A.upto(a, f"rr{m}"))
                for s in range(SUB):
                    ins = pe.transpose(bank[:, s * P:(s + 1) * P], xn[:, m % 2, s * P:(s + 1) * P], ident[:, :])
                ins.then_inc(pe_a, 1)

            def project_out(a, s):
                bank = free_a(a, f"y{s}")
                if s == 0:
                    pe.wait_ge(dve_a, DVE_A.upto(a, "ol3"))
                split_matmul(bank[:, :], lambda p, c: AT[:, p, c, s * P:(s + 1) * P],
                             lambda q, c: WO[:, q, c, :], C).then_inc(pe_a, 1)

            def x2_transpose(a, s):
                bank = free_a(a, f"x2t{s}")
                pe.wait_ge(dve_a, DVE_A.upto(a, f"x2_{s}"))
                for c in range(C):
                    ins = pe.transpose(bank[:, c * P:(c + 1) * P], ybuf[:, s, c * P:(c + 1) * P], ident[:, :])
                ins.then_inc(pe_a, 1)

            def query1(b_):
                bank = free_b(b_, "q")
                pe.wait_ge(dve_a, DVE_A.upto(b_, "x2l3"))
                split_matmul(bank[:, :], lambda p, c: WQ1[:, p, c, :], lambda q, c: XS[:, q, c, :], C).then_inc(pe_b, 1)

            def max_unit1(b_, n):
                s, j = n // 4, n % 4
                bank = free_b(b_, f"m{n}")
                if n == 0:
                    pe.wait_ge(act_b, ACT_B.upto(b_, "qh"))
                    pe.wait_ge(kv1_in, 16 * b_ + 16)
                pe.matmul(bank[:, 0:UNIT], Q1s[:, 0, s * P:(s + 1) * P], K1blk[:, j * UNIT:(j + 1) * UNIT],
                          start=True, stop=True).then_inc(pe_b, 1)

            def max_transpose1(b_):
                bank = free_b(b_, "mt")
                pe.wait_ge(dve_b, DVE_B.upto(b_, "mx15"))
                for s in range(SUB):
                    ins = pe.transpose(bank[0:H1, s * P:(s + 1) * P], mx1[:, s, :], ident[:, :])
                ins.then_inc(pe_b, 1)

            def scores1(b_, g):
                if g == 0:
                    pe.wait_ge(stack1_in, N_STACK * (b_ + 1))
                    pe.wait_ge(max1_in, 16 * b_ + 16)
                for j in range(4):
                    h = 4 * g + j
                    bank = free_b(b_, f"s{g}{j}")
                    pe.matmul(bank[:, :], K1st[0:98, h, 0:KM], Q1st[0:98, h // 2, :], start=True,
                              stop=True).then_inc(pe_b, 1)
                bank = free_b(b_, f"r{g}")
                for j in range(4):
                    h = 4 * g + j
                    ins = pe.matmul(bank[32 * j:32 * j + 32, :], K1st[0:98, h, KM:KA], Q1st[0:98, h // 2, :],
                                    start=True, stop=True)
                ins.then_inc(pe_b, 1)

            def values1(b_, g):
                if g:
                    pe.wait_ge(act_b, ACT_B.upto(b_, "od0"))
                elif not static_first(b_):
                    pe.wait_ge(act_b, ACT_B.upto(b_ - 1, "od1"))
                pe.wait_ge(act_b, ACT_B.upto(b_, f"er{g}"))
                pe.matmul(bank_o1[:, :], V1r[:, g, :], P1[:, 4, :], start=True, stop=False)
                for j in range(4):
                    ins = pe.matmul(bank_o1[32 * j:32 * j + 32, :], V1[:, 4 * g + j, :], P1[:, j, :],
                                    start=False, stop=True)
                ins.then_inc(pe_b, 1)

            def o1_transpose(b_, g):
                bank = free_b(b_, f"od{g}")
                pe.wait_ge(act_b, ACT_B.upto(b_, f"od{g}"))
                for s in range(SUB):
                    ins = pe.transpose(bank[:, s * P:(s + 1) * P], OD[:, g, s * P:(s + 1) * P], ident[:, :])
                ins.then_inc(pe_b, 1)

            def o1_back(b_):
                bank = free_b(b_, "ot")
                pe.wait_ge(dve_b, DVE_B.upto(b_, "on1"))
                for s in range(SUB):
                    ins = pe.transpose(bank[:, s * P:(s + 1) * P], On1[:, s, :], ident[:, :])
                ins.then_inc(pe_b, 1)

            def project_out1(b_, m):
                bank = free_b(b_, f"xo{m}")
                if m == 0:
                    pe.wait_ge(dve_b, DVE_B.upto(b_, "ol"))
                split_matmul(bank[:, :], lambda p, c: WO1[:, p, c, m * P:(m + 1) * P],
                             lambda q, c: O1s[:, q, :], 1).then_inc(pe_b, 1)

            def hidden(b_, f):
                bank = free_b(b_, f"h{f}")
                if f == 0:
                    pe.wait_ge(dve_b, DVE_B.upto(b_, "xl3"))
                split_matmul(bank[:, :], lambda p, c: W1[:, p, c, f * P:(f + 1) * P],
                             lambda q, c: XS[:, q, c, :], C).then_inc(pe_b, 1)

            def ffn_out(b_, m):
                bank = free_b(b_, f"f{m}")
                if m == 0:
                    pe.wait_ge(dve_b, DVE_B.upto(b_, "hl3"))
                split_matmul(bank[:, :], lambda p, c: W2[:, p, c, m * P:(m + 1) * P],
                             lambda q, c: HS[:, q, c, :], C).then_inc(pe_b, 1)

            def out_transpose(b_, s):
                bank = free_b(b_, f"t{s}")
                if s == 0:
                    pe.wait_ge(dve_b, DVE_B.upto(b_, "f3"))
                for c in range(C):
                    ins = pe.transpose(bank[:, c * P:(c + 1) * P], XT[:, c, s * P:(s + 1) * P], ident[:, :])
                ins.then_inc(pe_b, 1)

            def step(a, b_):
                A, Bq = a is not None, b_ is not None

                def maxima(lo, hi):
                    if A:
                        for n in range(lo, hi):
                            max_unit(a, n)

                if Bq: query1(b_)
                if A:
                    for s in range(SUB):
                        x_transpose(a, s)
                for m in range(4):
                    if A: query(a, m)
                    if Bq:
                        for n in range(4 * m, 4 * m + 4):
                            max_unit1(b_, n)
                if Bq: max_transpose1(b_)
                maxima(0, 8)
                if Bq: scores1(b_, 0)
                maxima(8, 12)
                if Bq:
                    values1(b_, 0)
                    scores1(b_, 1)
                maxima(12, 16)
                if Bq: values1(b_, 1)
                maxima(16, 20)
                if Bq:
                    o1_transpose(b_, 0)
                    o1_transpose(b_, 1)
                maxima(20, 24)
                if Bq:
                    o1_back(b_)
                    for m in range(C):
                        project_out1(b_, m)
                maxima(24, 28)
                if Bq: hidden(b_, 0)
                maxima(28, 32)
                if Bq: hidden(b_, 1)
                if A: max_transpose(a)
                if Bq:
                    hidden(b_, 2)
                    hidden(b_, 3)
                if A:
                    for kind, g in order_sc0():
                        if kind == "s":
                            scores(a, g)
                        else:
                            values(a, g)
                    den_transpose(a)
                if Bq:
                    ffn_out(b_, 0)
                    ffn_out(b_, 1)
                if A:
                    den_spread(a, 0)
                    den_spread(a, 1)
                if Bq: ffn_out(b_, 2)
                if A:
                    den_spread(a, 2)
                    den_spread(a, 3)
                if Bq:
                    ffn_out(b_, 3)
                    for s in range(SUB):
                        out_transpose(b_, s)
                if A:
                    for s in range(SUB):
                        project_out(a, s)
                    for s in range(SUB):
                        x2_transpose(a, s)

            step(0, None)
            step(1, 0)
            with pe.Fori(1, NT - 1) as i:
                step(i + 1, i)
            step(None, NT - 1)


def kernel(x, ctx_1024, mask_BxS2_bf1, L0_xattn_Wq, L0_xattn_Wk, L0_xattn_Wv, L0_xattn_Wo, L0_xattn_g_q,
           L0_xattn_g_c, L0_xattn_g_out, L1_xattn_W_q, L1_xattn_W_k, L1_xattn_W_v, L1_xattn_W_o, L1_xattn_w1,
           L1_xattn_b1, L1_xattn_w2, L1_xattn_b2):
    import numpy as np
    import concourse.bacc as bacc
    from concourse.bass_utils import run_bass_kernel_spmd

    def by_chunk(v):
        return np.asarray(v).reshape(C, P).T

    nc = bacc.Bacc("TRN2", target_bir_lowering=False, num_devices=1)
    arrays = {
        "x": np.asarray(x).reshape(B * S, D), "ctxt": np.asarray(ctx_1024).reshape(B * SK, D),
        "mask": np.asarray(mask_BxS2_bf1).view(np.uint8), "mask_col": np.asarray(mask_BxS2_bf1).view(np.uint8).reshape(B * SK, 1),
        "wq": L0_xattn_Wq, "wk": L0_xattn_Wk, "wv": L0_xattn_Wv, "wo": L0_xattn_Wo,
        "gq": by_chunk(L0_xattn_g_q), "gc": by_chunk(L0_xattn_g_c), "gout": L0_xattn_g_out,
        "wq1": L1_xattn_W_q, "wk1": L1_xattn_W_k, "wv1": L1_xattn_W_v, "wo1": L1_xattn_W_o,
        "w1t": np.asarray(L1_xattn_w1).T, "b1": by_chunk(L1_xattn_b1), "w2t": np.asarray(L1_xattn_w2).T, "b2": by_chunk(L1_xattn_b2),
    }
    arrays = {n: np.ascontiguousarray(a) for n, a in arrays.items()}
    aps = {n: nc.dram_tensor(n, a.shape, mybir.dt.from_np(a.dtype), kind="ExternalInput").ap()
           for n, a in arrays.items()}
    out = nc.dram_tensor("out", (B * S, D), F32, kind="ExternalOutput").ap()
    build(nc, *aps.values(), out)
    result = run_bass_kernel_spmd(nc, [arrays], core_ids=[0])
    return result.results[0]["out"].reshape(B, S, D)
```

```python
from contextlib import ExitStack

import concourse.bass as bass
from concourse import mybir

F32 = mybir.dt.float32
F16 = mybir.dt.float16
U8 = mybir.dt.uint8
ALU = mybir.AluOpType
ACT = mybir.ActivationFunctionType
AX = mybir.AxisListType

P = 128
D = 512
C = D // P
B, S, SK = 4, 2048, 154
KM = 128
KR = SK - KM
KP = 32
KA = KM + KP
T = 512
SUB = T // P
NT = B * S // T
TPB = S // T
H0, D0 = 16, 32
H1, D1 = 8, 16
G0 = H0 // 4
G1 = H1 // 4
EPS = 1e-6
WS = 64.0
UNIT = 2 * SK

K0_ST, K0_BLK, K0_V, K0_VR, K0_E, K0_ER = H0 * KA, G0 * 4 * SK, 2 * D, 2 * G0 * P, 2 * 4 * 32, 2 * 32
IMG0 = K0_ST + K0_BLK + K0_V + K0_VR + K0_E + K0_ER
K1_ST, K1_BLK, K1_V, K1_VR = H1 * KA, H1 * SK, 2 * H1 * 32, 2 * G1 * P
IMG1 = K1_ST + K1_BLK + K1_V + K1_VR


class Steps:

    def __init__(self, names):
        self.names = names.split() if isinstance(names, str) else list(names)
        assert len(set(self.names)) == len(self.names)
        self.at = {n: i + 1 for i, n in enumerate(self.names)}

    def upto(self, turn, name):
        return turn * len(self.names) + self.at[name]


def nums(fmt, n):
    return [fmt.format(i) for i in range(n)]


def order_qm():
    return ["q0", "q1"] + [n for m in range(2, G0) for n in nums("m{}", 8 * m - 8)[8 * m - 16:] + [f"q{m}"]] \
        + nums("m{}", 32)[16:]


def order_sc0():
    return [("s", 0), ("s", 1), ("v", 0), ("s", 2), ("v", 1), ("s", 3), ("v", 2), ("v", 3)]


PRE_ACT = Steps("sq sqr")
PRE_POOL = Steps("r")
PRE_PE = Steps("ta0 tb0 k0 k1 k2 k3 v0 vr0 ta1 tb1 kk v1 vr1")
PRE_DVE = Steps("masks ms sc0 cn0 ct0 sum0 mean0 ck0 cks0 k0_0 k0_1 k0_2 k0_3 kst0 v0 vr0 "
                "ct1 sum1 mean1 ck1 cks1 kk km kst1 v1 vr1")

PE_F = Steps(nums("xt{}", SUB) + order_qm() + ["mt"])
ACT_F = Steps(nums("sq{}", SUB) + nums("xh{}", SUB) + nums("qh{}", G0) + ["negm"])
DVE_F = Steps(["ms"] + nums("xn{}", SUB) + nums("xl{}", SUB)
              + ["ql0", "ql1"] + nums("mx{}", 8) + ["ql2"] + nums("mx{}", 16)[8:] + ["ql3"] + nums("mx{}", 32)[16:])
POOL_F = Steps("r")
PE_A = Steps([n for k, g in order_sc0() for n in (nums(f"s{g}" + "{}", 4) + [f"r{g}"] if k == "s" else [f"v{g}"])]
             + ["dt"] + nums("rb{}", G0) + nums("y{}", SUB) + nums("x2t{}", SUB))
ACT_A = Steps([n for g in range(G0) for n in nums(f"e{g}" + "{}", 4) + [f"er{g}"]]
              + ["dsb"] + nums("oh{}", G0) + nums("sqy{}", SUB)
              + [n for s in range(SUB) for n in (f"xf{s}", f"x2h{s}")])
DVE_A = Steps(nums("o{}", G0) + ["dm", "dd", "dg", "rc"] + "on0 on1 ol0 on2 ol1 on3 ol2 ol3".split()
              + "y0 y1 ms0 y2 ms1 x2_0 y3 ms2 x2_1 x2l0 ms3 x2_2 x2l1 x2_3 x2l2 x2l3".split())
POOL_A = Steps(nums("rr{}", G0) + nums("ry{}", SUB))
PE_B = Steps(["q"] + nums("m{}", 16) + ["mt"]
             + [n for g in range(G1) for n in nums(f"s{g}" + "{}", 4) + [f"r{g}", f"v{g}"]]
             + ["od0", "od1", "ot"] + nums("xo{}", C) + nums("h{}", C) + nums("f{}", C) + nums("t{}", SUB))
ACT_B = Steps(["qh", "negm"] + [n for g in range(G1) for n in nums(f"e{g}" + "{}", 4) + [f"er{g}", f"od{g}"]]
              + ["oh"] + nums("xh{}", C) + nums("h{}", C) + nums("t{}", SUB))
DVE_B = Steps(["ql"] + nums("mx{}", 16) + ["rc0", "on0", "rc1", "on1", "ol"]
              + ["xo0", "xo1", "xl0", "xo2", "xl1", "xo3", "xl2", "xl3"]
              + [n for f in range(C) for n in (f"hh{f}", f"hl{f}")] + nums("f{}", C))
POOL_B = Steps(nums("xb{}", C))

def in_turn(units, banks):
    return [(u, banks[i % len(banks)]) for i, u in enumerate(units)]


RING_F = in_turn(PE_F.names, (0, 1))
READER_F = {**{f"xt{s}": ("dve", f"xl{s}") for s in range(SUB)}, **{f"q{m}": ("dve", f"ql{m}") for m in range(G0)},
            **{f"m{n}": ("dve", f"mx{n}") for n in range(32)}, "mt": ("act", "negm")}
RING_A = in_turn([n for n in PE_A.names if n[0] != "v"], (0, 1))
READER_A = {**{f"s{g}{j}": ("act", f"e{g}{j}") for g in range(G0) for j in range(4)},
            **{f"r{g}": ("act", f"er{g}") for g in range(G0)}, "dt": ("dve", "dd"),
            **{f"rb{m}": ("dve", f"on{m}") for m in range(G0)}, **{f"y{s}": ("dve", f"y{s}") for s in range(SUB)},
            **{f"x2t{s}": ("dve", f"x2l{s}") for s in range(SUB)}}
RING_B = in_turn(["q"] + nums("m{}", 16) + ["mt"] + [n for g in range(G1) for n in nums(f"s{g}" + "{}", 4) + [f"r{g}"]] \
    + ["od0", "od1", "ot"] + nums("xo{}", C) + nums("h{}", C) + nums("f{}", C) + nums("t{}", SUB), (0, 1))
READER_B = {"q": ("dve", "ql"), **{f"m{n}": ("dve", f"mx{n}") for n in range(16)}, "mt": ("act", "negm"),
            **{f"s{g}{j}": ("act", f"e{g}{j}") for g in range(G1) for j in range(4)},
            **{f"r{g}": ("act", f"er{g}") for g in range(G1)}, "od0": ("dve", "on0"), "od1": ("dve", "on1"),
            "ot": ("dve", "ol"), **{f"xo{m}": ("dve", f"xo{m}") for m in range(C)},
            **{f"h{f}": ("act", f"h{f}") for f in range(C)}, **{f"f{m}": ("dve", f"f{m}") for m in range(C)},
            **{f"t{s}": ("act", f"t{s}") for s in range(SUB)}}
QS0 = D0 ** -0.5 / WS
QS1 = D1 ** -0.5 / WS


def bank_before(ring, unit):
    same = [u for u, bank in ring if bank == dict(ring)[unit]]
    k = same.index(unit)
    return (same[k - 1], 0) if k else (same[-1], 1)


def bank_f(unit):
    return dict(RING_F)[unit]


def bank_a(unit):
    return dict(RING_A)[unit]


def bank_b(unit):
    return dict(RING_B)[unit]


def static_first(t):
    return isinstance(t, int) and t == 0


def batch_of(t):
    return t // TPB


def build(nc, x, ctxt, mask, mask_col, wq, wk, wv, wo, gq, gc, gout, wq1, wk1, wv1, wo1, w1t, b1, w2t, b2, out):
    stack = ExitStack()
    with stack:
        def sb(name, shape, dt=F32):
            return stack.enter_context(nc.sbuf_tensor(name, shape, dt))

        def sem(name):
            return stack.enter_context(nc.semaphore(name))

        WQ, WO, W1, W2 = (sb(n, [P, 2, C, D], F16) for n in ("WQ", "WO", "W1", "W2"))
        WQ1 = sb("WQ1", [P, 2, C, P], F16)
        WO1 = sb("WO1", [P, 2, 1, D], F16)
        ident = sb("ident", [P, P])
        gout_b = sb("gout_b", [P, D])
        gq_c, gc_c, b1_c, b2_c = (sb(n, [P, C]) for n in ("gq_c", "gc_c", "b1_c", "b2_c"))
        one = sb("one", [P, 1])
        mhalf = sb("mhalf", [P, SUB])
        img0 = sb("img0", [P, IMG0], F16)
        img1 = sb("img1", [P, IMG1], F16)
        o = 0
        Kblk = img0[:, o:o + K0_BLK].rearrange("p (m k) -> p m k", m=G0); o += K0_BLK
        Kst = img0[:, o:o + K0_ST].rearrange("p (h k) -> p h k", h=H0); o += K0_ST
        V0 = img0[:, o:o + K0_V].bitcast(F32); o += K0_V
        V0r = img0[:, o:o + K0_VR].bitcast(F32).rearrange("p (m k) -> p m k", m=G0); o += K0_VR
        E0 = img0[:, o:o + K0_E].bitcast(F32); o += K0_E
        E0r = img0[:, o:o + K0_ER].bitcast(F32)
        o = 0
        K1st = img1[:, o:o + K1_ST].rearrange("p (h k) -> p h k", h=H1); o += K1_ST
        K1blk = img1[:, o:o + K1_BLK]; o += K1_BLK
        V1 = img1[:, o:o + K1_V].bitcast(F32).rearrange("p (h k) -> p h k", h=H1); o += K1_V
        V1r = img1[:, o:o + K1_VR].bitcast(F32).rearrange("p (g k) -> p g k", g=G1)
        xin = sb("xin", [P, SUB, D])
        xres = sb("xres", [P, SUB, D])
        xn = sb("xn", [P, 2, D])
        ybuf = sb("ybuf", [P, SUB, D])
        AT = sb("AT", [P, 2, C, T], F16)
        Qs = sb("Qs", [P, 2, G0, T], F16)
        Qst = sb("Qst", [P, H0, T], F16)
        Pr = sb("Pr", [P, 10, T])
        Ou = ybuf
        AO = sb("AO", [P, 2, C, T], F16)
        Dsb = sb("Dsb", [P, T])
        mx = sb("mx", [P, SUB, H0])
        negm = sb("negm", [H0, T], F16)
        dq = sb("dq", [P, SUB, H0])
        rq = sb("rq", [P, SUB, H0])
        junk = sb("junk", [P, D], F16)
        junk_y = sb("junk_y", [P, 2, D], F16)
        ss, r1, ssy, ry = (sb(n, [P, SUB]) for n in ("ss", "r1", "ssy", "ry"))
        ms, msy = sb("ms", [P, SUB]), sb("msy", [P, SUB])
        XT = sb("XT", [P, C, T])
        XS = sb("XS", [P, 2, C, T], F16)
        Q1s = sb("Q1s", [P, 2, T], F16)
        Q1st = sb("Q1st", [P, 4, T], F16)
        OD = sb("OD", [P, G1, T])
        rq1 = sb("rq1", [P, G1, SUB, 4])
        On1 = sb("On1", [P, SUB, P])
        O1s = sb("O1s", [P, 2, T], F16)
        mx1 = sb("mx1", [P, SUB, H1])
        negm1 = sb("negm1", [H1, T], F16)
        Ht = sb("Ht", [P, 2, T])
        HS = sb("HS", [P, 2, C, T], F16)
        outb = sb("outb", [P, 2, D])
        mrow_u8 = sb("mrow_u8", [P, SK], U8)
        mcol_u8, mrem_u8 = sb("mcol_u8", [P, 1], U8), sb("mrem_u8", [P, 1], U8)
        mcol, mrem = sb("mcol", [P, 1]), sb("mrem", [P, 1])
        quad, par, sel, valid = sb("quad", [P, 4]), sb("par", [P, 2]), sb("sel", [P, H1]), sb("valid", [P, 1])
        junk2 = sb("junk2", [P, D], F16)
        cntv, cntm, cntr = sb("cntv", [P, 1]), sb("cntm", [P, 1]), sb("cntr", [P, 1])
        ssc, msc, rsc = sb("ssc", [P, 2]), sb("msc", [P, 2]), sb("rsc", [P, 2])
        scl = sb("scl", [P, 2])
        csum, cnt, mean = sb("csum", [P, C]), sb("cnt", [P, 1]), sb("mean", [P, C])
        stage = [xin, ybuf]
        stage_small = xres
        WKV = Qst[:, :, :].rearrange("p (w q c) n -> p w q c n", w=2, q=2)
        WKV1 = Q1st[:, :, :].rearrange("p (w q) (c n) -> p w q c n", w=2, c=C)
        crow = Pr
        cn = XT
        cT = OD[:, :, :].rearrange("p a b -> p (a b)")[:, 0:C * KA].rearrange("p (c k) -> p c k", c=C)
        ck32 = Ht[:, :, :].rearrange("p a b -> p (a b)")[:, 0:C * KA].rearrange("p (c k) -> p c k", c=C)
        inv = [outb[:, 0, 0:KA], outb[:, 1, 0:KA]]
        ATf = AT[:, :, :, :].rearrange("p a c t -> p (a c t)")
        cks = ATf[:, 0:2 * C * KA].rearrange("p (a c k) -> p a c k", a=2, c=C)
        cvs = ATf[:, 2 * C * KA:4 * C * KA].rearrange("p (a c k) -> p a c k", a=2, c=C)
        KTs = Qs[:, :, :, 0:KA]
        psum = [stack.enter_context(nc.psum_tensor(f"bank{i}", [P, T], F32)) for i in range(8)]
        ring_f, ring_a, ring_b, bank_o, bank_d = psum[0:2], psum[2:4], psum[4:6], psum[6], psum[7]
        image0 = nc.dram_tensor("image0", [B * P, IMG0 // 2], F32, kind="Internal").ap()
        image1 = nc.dram_tensor("image1", [B * P, IMG1 // 2], F32, kind="Internal").ap()

        const_ready, weights_in, vec_in = sem("const_ready"), sem("weights_in"), sem("vec_in")
        stage_in = [sem("stage_in0"), sem("stage_in1")]
        weight_hi, weight_split, weight_g = sem("weight_hi"), sem("weight_split"), sem("weight_g")
        pre_zero = sem("pre_zero")
        pre_act, pre_pool, pre_pe, pre_dve = (sem(n) for n in ("pre_act", "pre_pool", "pre_pe", "pre_dve"))
        ctx_in, image_out = sem("ctx_in"), sem("image_out")
        pre_tmp, pre_tmp2, pre_kt = sem("pre_tmp"), sem("pre_tmp2"), sem("pre_kt")
        N_ZERO = 9 + 6 + 1 + 4 * G1 + 2
        pe_f, act_f, dve_f, pool_f = (sem(n) for n in ("pe_f", "act_f", "dve_f", "pool_f"))
        pe_a, act_a, dve_a, pool_a = (sem(n) for n in ("pe_a", "act_a", "dve_a", "pool_a"))
        pe_b, act_b, dve_b, pool_b = (sem(n) for n in ("pe_b", "act_b", "dve_b", "pool_b"))
        x_in, xres_in, blk0_in, kv0_in, kv1_in = (sem(n) for n in ("x_in", "xres_in", "blk0_in", "kv0_in", "kv1_in"))
        stack0_in, stack1_in, max0_in, max1_in = (sem(n) for n in ("stack0_in", "stack1_in", "max0_in", "max1_in"))
        out_done = [sem("out_done0"), sem("out_done1")]
        N_STACK = 12 * 16

        block = stack.enter_context(nc.Block())

        BIG = [(wk, gc_c, lambda q, c: WKV[:, 0, q, c, :]), (wv, gc_c, lambda q, c: WKV[:, 1, q, c, :]),
               (wq, gq_c, lambda q, c: WQ[:, q, c, :]), (wo, None, lambda q, c: WO[:, q, c, :]),
               (w1t, None, lambda q, c: W1[:, q, c, :]), (w2t, None, lambda q, c: W2[:, q, c, :])]
        SMALL = [(wk1, lambda q: WKV1[:, 0, q, :, :].rearrange("p c n -> p (c n)")),
                 (wv1, lambda q: WKV1[:, 1, q, :, :].rearrange("p c n -> p (c n)")),
                 (wq1, lambda q: WQ1[:, q, :, :].rearrange("p c n -> p (c n)")),
                 (wo1, lambda q: WO1[:, q, 0, :])]

        def started(e):
            e.wait_ge(image_out, 32 * B)
            e.wait_ge(weight_split, 4 * len(BIG) + len(SMALL))

        @block.sync
        def _(sp):
            for v, dst in ((gq, gq_c), (gc, gc_c), (b1, b1_c), (b2, b2_c)):
                sp.dma_start(dst[:, :], v).then_inc(vec_in, 16)
            sp.dma_start(gout_b[:, :], gout.rearrange("(a n) -> a n", a=1).to_broadcast([P, D])).then_inc(vec_in, 16)
            for i, (w, _) in enumerate(SMALL):
                src = w.rearrange("(c p) n -> p c n", p=P)
                dst = stage_small[:, i, :].rearrange("p (c n) -> p c n", c=src.shape[1])
                sp.dma_start(dst, src).then_inc(weights_in, 16)
            for i, (w, _, _) in enumerate(BIG):
                if i >= 2:
                    sp.wait_ge(weight_split, 4 * (i - 1) + len(SMALL))
                    sp.wait_ge(stage_in[i % 2], 16 * (i // 2))
                sp.dma_start(stage[i % 2][:, :, :], w.rearrange("(c p) n -> p c n", p=P)).then_inc(stage_in[i % 2], 16)
            sp.wait_ge(pre_zero, N_ZERO)

            def load_context(b):
                sp.dma_start(crow[:, 0, :], ctxt[bass.ds(b * SK, KM), :]).then_inc(ctx_in, 16)
                sp.dma_start(crow[0:KR, 1, :], ctxt[bass.ds(b * SK + KM, KR), :]).then_inc(ctx_in, 16)
                sp.dma_start(mrow_u8[:, :], mask[bass.ds(b, 1), :].to_broadcast([P, SK])).then_inc(ctx_in, 16)
                sp.dma_start(mcol_u8[:, :], mask_col[bass.ds(b * SK, KM), :]).then_inc(ctx_in, 16)
                for j in range(4):
                    sp.dma_start(mrem_u8[32 * j:32 * j + KR, :],
                                 mask_col[bass.ds(b * SK + KM, KR), :]).then_inc(ctx_in, 16)

            def store_images(b):
                sp.wait_ge(pre_dve, PRE_DVE.upto(b, "vr0"))
                sp.dma_start(image0[bass.ds(b * P, P), :], img0[:, :].bitcast(F32)).then_inc(image_out, 16)
                sp.wait_ge(pre_dve, PRE_DVE.upto(b, "vr1"))
                sp.dma_start(image1[bass.ds(b * P, P), :], img1[:, :].bitcast(F32)).then_inc(image_out, 16)

            load_context(0)
            with sp.Fori(0, B - 1) as b:
                store_images(b)
                sp.wait_ge(image_out, 32 * b + 32)
                load_context(b + 1)
            store_images(B - 1)
            started(sp)

            def value(v):
                return v if isinstance(v, int) else sp.to_reg(v)

            def load_image1(b_):
                if not static_first(b_):
                    sp.wait_ge(pe_b, PE_B.upto(b_ - 1, "v1"))
                sp.dma_start(img1[:, :].bitcast(F32), image1[bass.ds(batch_of(b_) * P, P), :]).then_inc(kv1_in, 16)

            def load_blocks0(f):
                if not static_first(f):
                    sp.wait_ge(pe_f, PE_F.upto(f - 1, "m31"))
                sp.dma_start(img0[:, 0:K0_BLK].bitcast(F32),
                             image0[bass.ds(batch_of(f) * P, P), 0:K0_BLK // 2]).then_inc(blk0_in, 16)

            def load_image0(a):
                if not static_first(a):
                    sp.wait_ge(pe_a, PE_A.upto(a - 1, "v3"))
                sp.dma_start(img0[:, K0_BLK:].bitcast(F32),
                             image0[bass.ds(batch_of(a) * P, P), K0_BLK // 2:]).then_inc(kv0_in, 16)

            def stack1(b_):
                lo, hi = value(DVE_B.upto(b_, "ql")), value(ACT_B.upto(b_, "qh"))
                if not static_first(b_):
                    used = value(PE_B.upto(b_ - 1, "r1"))
                    sp.wait_ge(pe_b, used)
                sp.wait_ge(dve_b, lo)
                sp.wait_ge(act_b, hi)
                for piece, part in enumerate((0, 0, 1)):
                    for j in range(4):
                        sp.dma_start(Q1st[32 * piece:32 * piece + 32, j, :],
                                     Q1s[32 * j:32 * j + 32, part, :]).then_inc(stack1_in, 16)

            def stack0(f):
                hi, lo = value(ACT_F.upto(f, "qh3")), value(DVE_F.upto(f, "ql3"))
                if not static_first(f):
                    used = value(PE_A.upto(f - 1, "r3"))
                    sp.wait_ge(pe_a, used)
                sp.wait_ge(act_f, hi)
                sp.wait_ge(dve_f, lo)
                for piece, part in enumerate((0, 0, 1)):
                    for j in range(4):
                        sp.dma_start(Qst[32 * piece:32 * piece + 32, j::4, :],
                                     Qs[32 * j:32 * j + 32, part, :, :]).then_inc(stack0_in, 16)

            def stack_max1(b_):
                sp.wait_ge(act_b, ACT_B.upto(b_, "negm"))
                sp.dma_start(Q1st[96:98, :, :], negm1[:, :]).then_inc(max1_in, 16)

            def stack_max0(f):
                sp.wait_ge(act_f, ACT_F.upto(f, "negm"))
                sp.dma_start(Qst[96:97, :, :], negm[:, :]).then_inc(max0_in, 16)

            def store(b_, s):
                sp.wait_ge(act_b, ACT_B.upto(b_, f"t{s}"))
                sp.dma_start(out[bass.ds(b_ * T + s * P, P), :], outb[:, s % 2, :]).then_inc(out_done[s % 2], 16)

            def keep_x(f):
                arrived = value(16 * f + 16)
                if not static_first(f):
                    read = value(DVE_A.upto(f - 1, "y3"))
                    sp.wait_ge(dve_a, read)
                sp.wait_ge(x_in, arrived)
                sp.dma_start(xres[:, :, :], xin[:, :, :]).then_inc(xres_in, 16)

            def load_x(t, read_by=None):
                if read_by is not None:
                    copied, squared, normed = (value(v) for v in (
                        16 * read_by + 16, ACT_F.upto(read_by, "sq3"), DVE_F.upto(read_by, "xn3")))
                    sp.wait_ge(xres_in, copied)
                    sp.wait_ge(act_f, squared)
                    sp.wait_ge(dve_f, normed)
                sp.dma_start(xin[:, :, :], x[bass.ds(t * T, T), :].rearrange("(s p) d -> p s d", p=P)).then_inc(x_in, 16)

            def step(f, a, b_, x_next):
                if b_ is not None:
                    load_image1(b_)
                    stack1(b_)
                if f is not None:
                    load_blocks0(f)
                if a is not None:
                    load_image0(a)
                if b_ is not None:
                    stack_max1(b_)
                if f is not None:
                    keep_x(f)
                if x_next is not None:
                    load_x(x_next, read_by=f)
                if b_ is not None:
                    for n in range(2):
                        store(b_, n)
                if f is not None:
                    stack0(f)
                if b_ is not None:
                    for n in range(2, 4):
                        store(b_, n)
                if f is not None:
                    stack_max0(f)

            load_x(0)
            step(0, None, None, 1)
            step(1, 0, None, 2)
            step(2, 1, 0, 3)
            with sp.Fori(1, NT - 3) as i:
                step(i + 2, i + 1, i, i + 3)
            step(NT - 1, NT - 2, NT - 3, None)
            step(None, NT - 1, NT - 2, None)
            step(None, None, NT - 1, None)
            for k in range(2):
                sp.wait_ge(out_done[k], 2 * 16 * NT)

        @block.gpsimd
        def _(pool):
            pool.memset(ident[:, :], 0.0).then_inc(const_ready, 1)
            pool.memset(quad[:, :], 0.0).then_inc(const_ready, 1)
            pool.memset(par[:, :], 0.0).then_inc(const_ready, 1)
            pool.memset(sel[:, :], 0.0).then_inc(const_ready, 1)
            pool.memset(mhalf[:, :], -0.5).then_inc(const_ready, 1)
            pool.memset(one[:, :], 1.0).then_inc(const_ready, 1)
            pool.memset(K1st, 0.0).then_inc(const_ready, 1)
            pool.wait_ge(const_ready, 7)
            pool.affine_select(out=ident[:, :], in_=ident[:, :], compare_op=ALU.not_equal, fill=1.0, base=0,
                               pattern=[[-1, P]], channel_multiplier=1).then_inc(const_ready, 1)
            pool.affine_select(out=sel[:, :], in_=sel[:, :], compare_op=ALU.is_gt, fill=1.0, base=0,
                               pattern=[[D1, H1]], channel_multiplier=-1).then_inc(const_ready, 1)
            pool.affine_select(out=quad[:, :], in_=quad[:, :], compare_op=ALU.is_gt, fill=1.0, base=0,
                               pattern=[[32, 4]], channel_multiplier=-1).then_inc(const_ready, 1)
            pool.wait_ge(const_ready, 10)
            pool.affine_select(out=sel[:, :], in_=sel[:, :], compare_op=ALU.is_gt, fill=0.0, base=D1,
                               pattern=[[D1, H1]], channel_multiplier=-1).then_inc(const_ready, 1)
            pool.affine_select(out=quad[:, :], in_=quad[:, :], compare_op=ALU.is_gt, fill=0.0, base=32,
                               pattern=[[32, 4]], channel_multiplier=-1).then_inc(const_ready, 1)
            pool.wait_ge(const_ready, 12)
            with pool.Fori(0, B) as b:
                pool.wait_ge(pre_dve, PRE_DVE.upto(b, "ms"))
                pool.tensor_tensor(rsc[:, :], msc[:, :], mhalf[:, 0:2], ALU.pow).then_inc(pre_pool, 1)
            started(pool)

            def norm_x(f):
                pool.wait_ge(dve_f, DVE_F.upto(f, "ms"))
                pool.tensor_tensor(r1[:, :], ms[:, :], mhalf[:, :], ALU.pow).then_inc(pool_f, 1)

            def spread(a, m):
                if m == 0:
                    pool.wait_ge(dve_a, DVE_A.upto(a, "rc"))
                if m >= 2:
                    pool.wait_ge(pe_a, PE_A.upto(a, f"rb{m - 2}"))
                pool.tensor_tensor(xn[:, m % 2, :].rearrange("p (s j r) -> p s j r", s=SUB, j=4),
                                   rq[:, :, 4 * m:4 * m + 4].unsqueeze(3).to_broadcast([P, SUB, 4, D0]),
                                   one[:, :].unsqueeze(2).unsqueeze(3).to_broadcast([P, SUB, 4, D0]),
                                   ALU.mult).then_inc(pool_a, 1)

            def norm_y(a, s):
                pool.wait_ge(dve_a, DVE_A.upto(a, f"ms{s}"))
                pool.tensor_tensor(ry[:, s:s + 1], msy[:, s:s + 1], mhalf[:, 0:1], ALU.pow).then_inc(pool_a, 1)

            def add_b2(b_, m):
                pool.wait_ge(dve_b, DVE_B.upto(b_, f"xl{m}"))
                pool.tensor_tensor(XT[:, m, :], XT[:, m, :], b2_c[:, m:m + 1].to_broadcast([P, T]), ALU.add).then_inc(pool_b, 1)

            def step(f, a, b_):
                if b_ is not None:
                    for n in range(2):
                        add_b2(b_, n)
                if a is not None:
                    for n in range(4):
                        spread(a, n)
                if f is not None:
                    norm_x(f)
                if a is not None:
                    for n in range(3):
                        norm_y(a, n)
                if b_ is not None:
                    for n in range(2, 4):
                        add_b2(b_, n)
                if a is not None:
                    norm_y(a, 3)

            step(0, None, None)
            step(1, 0, None)
            step(2, 1, 0)
            with pool.Fori(1, NT - 2) as i:
                step(i + 2, i + 1, i)
            step(None, NT - 1, NT - 2)
            step(None, None, NT - 1)

        @block.scalar
        def _(act):
            act.wait_ge(weights_in, 16 * len(SMALL))
            for i, (_, dst) in enumerate(SMALL):
                act.activation(dst(0), stage_small[:, i, :], ACT.Copy, scale=WS).then_inc(weight_hi, 1)
            act.wait_ge(vec_in, 16 * 5)
            for i, (_, g, dst) in enumerate(BIG):
                if g is None:
                    act.wait_ge(stage_in[i % 2], 16 * (i // 2 + 1))
                else:
                    act.wait_ge(weight_g, 4 * (i + 1))
                for c in range(C):
                    act.activation(dst(0, c), stage[i % 2][:, c, :], ACT.Copy, scale=WS).then_inc(weight_hi, 1)
            act.wait_ge(pre_zero, N_ZERO)
            with act.Fori(0, B) as b:
                act.wait_ge(ctx_in, 128 * b + 128)
                act.activation(junk[:, :], crow[:, 0, :], ACT.Square, accum_out=ssc[:, 0:1]).then_inc(pre_act, 1)
                act.activation(junk2[0:KP, :], crow[0:KP, 1, :], ACT.Square, accum_out=ssc[0:KP, 1:2]).then_inc(pre_act, 1)
            started(act)

            def norm_x(f, s):
                if s == 0:
                    act.wait_ge(x_in, 16 * f + 16)
                if s >= 2:
                    act.wait_ge(act_f, ACT_F.upto(f, f"sq{s - 2}"))
                act.activation(junk[:, :] if s % 2 else junk2[:, :], xin[:, s, :], ACT.Square,
                               accum_out=ss[:, s:s + 1]).then_inc(act_f, 1)

            def x_hi(f, s):
                if s == 0 and not static_first(f):
                    act.wait_ge(pe_f, PE_F.upto(f - 1, "q3"))
                act.wait_ge(pe_f, PE_F.upto(f, f"xt{s}"))
                act.activation(AT[:, 0, :, s * P:(s + 1) * P], ring_f[bank_f(f"xt{s}")][:, :].rearrange(
                    "p (c q) -> p c q", c=C), ACT.Copy).then_inc(act_f, 1)

            def q_hi(f, m):
                act.wait_ge(pe_f, PE_F.upto(f, f"q{m}"))
                if m == 0 and not static_first(f):
                    act.wait_ge(stack0_in, N_STACK * f)
                act.activation(Qs[:, 0, m, :], ring_f[bank_f(f"q{m}")][:, :], ACT.Copy,
                               scale=QS0).then_inc(act_f, 1)

            def neg_max(f):
                act.wait_ge(pe_f, PE_F.upto(f, "mt"))
                if not static_first(f):
                    act.wait_ge(max0_in, 16 * f)
                act.activation(negm[:, :], ring_f[bank_f("mt")][0:H0, :], ACT.Copy, scale=-1.0).then_inc(act_f, 1)

            def exps(a, g, j):
                unit = f"s{g}{j}" if j < 4 else f"r{g}"
                if g < 2 and j == 0 and not static_first(a):
                    act.wait_ge(pe_b, PE_B.upto(a - 1, f"v{g}"))
                act.wait_ge(pe_a, PE_A.upto(a, unit))
                act.activation(Pr[:, 5 * (g % 2) + j, :], ring_a[bank_a(unit)][:, :], ACT.Exp).then_inc(act_a, 1)

            def den(a):
                act.wait_ge(pe_a, PE_A.upto(a, "v3"))
                act.activation(Dsb[:, :], bank_d[:, :], ACT.Copy).then_inc(act_a, 1)

            def o_hi(a, m):
                if m == 0 and not static_first(a):
                    act.wait_ge(pe_a, PE_A.upto(a - 1, "y3"))
                act.wait_ge(dve_a, DVE_A.upto(a, f"on{m}"))
                act.activation(AO[:, 0, m, :], Ou[:, m, :], ACT.Copy).then_inc(act_a, 1)

            def y_sq(a, s):
                act.wait_ge(dve_a, DVE_A.upto(a, f"y{s}"))
                if s >= 2:
                    act.wait_ge(act_a, ACT_A.upto(a, f"sqy{s - 2}"))
                act.activation(junk_y[:, s % 2, :], ybuf[:, s, :], ACT.Square,
                               accum_out=ssy[:, s:s + 1]).then_inc(act_a, 1)

            def x2_evac(a, s):
                if s == 0 and not static_first(a):
                    act.wait_ge(pe_b, PE_B.upto(a - 1, "t3"))
                act.wait_ge(pe_a, PE_A.upto(a, f"x2t{s}"))
                src = ring_a[bank_a(f"x2t{s}")][:, :].rearrange("p (c q) -> p c q", c=C)
                act.activation(XT[:, :, s * P:(s + 1) * P], src, ACT.Copy).then_inc(act_a, 1)
                act.activation(XS[:, 0, :, s * P:(s + 1) * P], src, ACT.Copy).then_inc(act_a, 1)

            def q1_hi(b_):
                act.wait_ge(pe_b, PE_B.upto(b_, "q"))
                if not static_first(b_):
                    act.wait_ge(stack1_in, N_STACK * b_)
                act.activation(Q1s[:, 0, :], ring_b[bank_b("q")][:, :], ACT.Copy, scale=QS1).then_inc(act_b, 1)

            def neg_max1(b_):
                act.wait_ge(pe_b, PE_B.upto(b_, "mt"))
                if not static_first(b_):
                    act.wait_ge(max1_in, 16 * b_)
                act.activation(negm1[:, :], ring_b[bank_b("mt")][0:H1, :], ACT.Copy, scale=-1.0).then_inc(act_b, 1)

            def exps1(b_, g, j):
                unit = f"s{g}{j}" if j < 4 else f"r{g}"
                if j == 0:
                    act.wait_ge(pe_a, PE_A.upto(b_, f"v{g + 2}"))
                act.wait_ge(pe_b, PE_B.upto(b_, unit))
                act.activation(Pr[:, 5 * g + j, :], ring_b[bank_b(unit)][:, :], ACT.Exp).then_inc(act_b, 1)

            def od(b_, g):
                act.wait_ge(pe_b, PE_B.upto(b_, f"v{g}"))
                act.activation(OD[:, g, :], bank_o[:, :], ACT.Copy).then_inc(act_b, 1)

            def o1_hi(b_):
                act.wait_ge(pe_b, PE_B.upto(b_, "ot"))
                act.activation(O1s[:, 0, :], ring_b[bank_b("ot")][:, :], ACT.Copy).then_inc(act_b, 1)

            def x_split(b_, m):
                act.wait_ge(dve_b, DVE_B.upto(b_, f"xo{m}"))
                act.activation(XS[:, 0, m, :], XT[:, m, :], ACT.Copy).then_inc(act_b, 1)

            def hidden(b_, f):
                act.wait_ge(pe_b, PE_B.upto(b_, f"h{f}"))
                if f >= 2:
                    act.wait_ge(dve_b, DVE_B.upto(b_, f"hl{f - 2}"))
                act.activation(Ht[:, f % 2, :], ring_b[bank_b(f"h{f}")][:, :], ACT.Relu, bias=b1_c[:, f:f + 1],
                               scale=1.0 / WS).then_inc(act_b, 1)

            def out_copy(b_, s):
                act.wait_ge(pe_b, PE_B.upto(b_, f"t{s}"))
                if s >= 2 or not static_first(b_):
                    act.wait_ge(out_done[s % 2], 16 * (2 * b_ + s // 2))
                act.activation(outb[:, s % 2, :], ring_b[bank_b(f"t{s}")][:, :], ACT.Copy).then_inc(act_b, 1)

            def step(f, a, b_):
                if b_ is not None:
                    q1_hi(b_)
                    neg_max1(b_)
                if f is not None:
                    norm_x(f, 0)
                if b_ is not None:
                    for n in range(5):
                        exps1(b_, 0, n)
                if f is not None:
                    norm_x(f, 1)
                if b_ is not None:
                    od(b_, 0)
                    for n in range(2):
                        exps1(b_, 1, n)
                if a is not None:
                    exps(a, 0, 0)
                if b_ is not None:
                    exps1(b_, 1, 2)
                if a is not None:
                    exps(a, 0, 1)
                if b_ is not None:
                    for n in range(3, 5):
                        exps1(b_, 1, n)
                if a is not None:
                    for n in range(2, 4):
                        exps(a, 0, n)
                if b_ is not None:
                    od(b_, 1)
                if a is not None:
                    exps(a, 0, 4)
                    for n in range(3):
                        exps(a, 1, n)
                if b_ is not None:
                    o1_hi(b_)
                if a is not None:
                    for n in range(3, 5):
                        exps(a, 1, n)
                    for n in range(3):
                        exps(a, 2, n)
                if b_ is not None:
                    x_split(b_, 0)
                if a is not None:
                    for n in range(3, 5):
                        exps(a, 2, n)
                    for n in range(4):
                        exps(a, 3, n)
                if f is not None:
                    norm_x(f, 2)
                if a is not None:
                    exps(a, 3, 4)
                if f is not None:
                    norm_x(f, 3)
                if b_ is not None:
                    for n in range(1, 4):
                        x_split(b_, n)
                if a is not None:
                    den(a)
                if b_ is not None:
                    hidden(b_, 0)
                if a is not None:
                    o_hi(a, 0)
                if b_ is not None:
                    hidden(b_, 1)
                if a is not None:
                    for n in range(1, 4):
                        o_hi(a, n)
                    for n in range(2):
                        y_sq(a, n)
                if b_ is not None:
                    hidden(b_, 2)
                if a is not None:
                    y_sq(a, 2)
                if f is not None:
                    for n in range(4):
                        x_hi(f, n)
                if b_ is not None:
                    hidden(b_, 3)
                if f is not None:
                    for n in range(4):
                        q_hi(f, n)
                if b_ is not None:
                    out_copy(b_, 0)
                if a is not None:
                    y_sq(a, 3)
                if b_ is not None:
                    out_copy(b_, 1)
                if a is not None:
                    for n in range(2):
                        x2_evac(a, n)
                if b_ is not None:
                    out_copy(b_, 2)
                if a is not None:
                    for n in range(2, 4):
                        x2_evac(a, n)
                if b_ is not None:
                    out_copy(b_, 3)
                if f is not None:
                    neg_max(f)

            step(0, None, None)
            step(1, 0, None)
            step(2, 1, 0)
            with act.Fori(1, NT - 2) as i:
                step(i + 2, i + 1, i)
            step(None, NT - 1, NT - 2)
            step(None, None, NT - 1)

        @block.vector
        def _(dve):
            zeroed = [(img0[:, :].bitcast(F32), 0.0), (img1[:, K1_ST:].bitcast(F32), 0.0), (crow[:, 1, :], 0.0),
                      (cn[:, 1, :], 0.0), (mrem_u8[:, :], 0), (inv[0], 1.0), (inv[1], 0.0), (ssc[:, :], 1.0),
                      (valid[:, :], 0.0)]
            for ap, v in zeroed:
                dve.memset(ap, v).then_inc(pre_zero, 1)
            dve.wait_ge(pre_zero, len(zeroed))
            later = [(Kst[96:97, :, :], 1.0), (inv[1][:, SK:KA], 1.0)] \
                + [(valid[32 * j:32 * j + KR, :], 1.0) for j in range(4)]
            for ap, v in later:
                dve.memset(ap, v).then_inc(pre_zero, 1)
            dve.wait_ge(pre_zero, len(zeroed) + len(later))
            dve.memset(V1[:, :, D1:2 * D1], 1.0).then_inc(pre_zero, 1)
            for g in range(G1):
                for j in range(4):
                    dve.tensor_copy(V1r[32 * j:32 * j + 32, g, 32 * j + D1:32 * j + 2 * D1],
                                    valid[32 * j:32 * j + 32, :].to_broadcast([32, D1])).then_inc(pre_zero, 1)
            dve.wait_ge(const_ready, 12)
            dve.tensor_copy(K1st[96:98, :, :].rearrange("p (j a) k -> p j a k", a=2),
                            ident[96:98, 96:98].unsqueeze(1).unsqueeze(3).to_broadcast([2, 4, 2, KA])).then_inc(pre_zero, 1)
            dve.tensor_reduce(par[:, :], sel[:, :].rearrange("p (j a) -> p a j", a=2), AX.X, ALU.add).then_inc(pre_zero, 1)

            for i, (_, dst) in enumerate(SMALL):
                dve.wait_ge(weight_hi, i + 1)
                dve.scalar_tensor_tensor(dst(1), stage_small[:, i, :], WS, dst(0), ALU.mult, ALU.subtract).then_inc(weight_split, 1)
            dve.wait_ge(vec_in, 16 * 5)
            done_g = 0
            for i, (_, g, dst) in enumerate(BIG):
                if g is not None:
                    dve.wait_ge(stage_in[i % 2], 16 * (i // 2 + 1))
                    for c in range(C):
                        dve.tensor_scalar(stage[i % 2][:, c, :], stage[i % 2][:, c, :], g[:, c:c + 1], None,
                                          ALU.mult).then_inc(weight_g, 1)
                for c in range(C):
                    dve.wait_ge(weight_hi, len(SMALL) + 4 * i + c + 1)
                    dve.scalar_tensor_tensor(dst(1, c), stage[i % 2][:, c, :], WS, dst(0, c), ALU.mult,
                                             ALU.subtract).then_inc(weight_split, 1)

            with dve.Fori(0, B) as b:
                def done(name):
                    dve.wait_ge(pre_dve, PRE_DVE.upto(b, name))

                dve.wait_ge(ctx_in, 128 * b + 128)
                dve.tensor_copy(mcol[:, :], mcol_u8[:, :])
                dve.tensor_copy(mrem[:, :], mrem_u8[:, :])
                dve.tensor_scalar(inv[0][:, 0:SK], mrow_u8[:, :], -1.0, 1.0, ALU.mult, ALU.add).then_inc(pre_dve, 1)
                dve.wait_ge(pre_act, PRE_ACT.upto(b, "sqr"))
                dve.tensor_scalar(msc[:, :], ssc[:, :], 1.0 / D, EPS, ALU.mult, ALU.add).then_inc(pre_dve, 1)
                dve.wait_ge(pre_pool, PRE_POOL.upto(b, "r"))
                dve.tensor_tensor(scl[:, 0:1], rsc[:, 0:1], mcol[:, :], ALU.mult)
                dve.tensor_tensor(scl[:, 1:2], rsc[:, 1:2], mrem[:, :], ALU.mult).then_inc(pre_dve, 1)
                done("sc0")
                dve.tensor_scalar(cn[:, 0, :], crow[:, 0, :], scl[:, 0:1], None, ALU.mult)
                dve.tensor_scalar(cn[0:KP, 1, :], crow[0:KP, 1, :], scl[0:KP, 1:2], None, ALU.mult).then_inc(pre_dve, 1)
                for layer in range(2):
                    L = str(layer)
                    dve.wait_ge(pre_pe, PRE_PE.upto(b, "tb" + L))
                    dve.tensor_copy(cT[:, :, 0:KM], psum[0][:, :].rearrange("p (c k) -> p c k", c=C))
                    dve.tensor_copy(cT[:, :, KM:KA], psum[1][:, 0:C * KP].rearrange("p (c k) -> p c k", c=C)).then_inc(pre_dve, 1)
                    done("ct" + L)
                    dve.tensor_reduce(csum[:, :], cT, AX.X, ALU.add)
                    dve.tensor_reduce(cnt[:, :], inv[layer][:, 0:SK], AX.X, ALU.add).then_inc(pre_dve, 1)
                    done("sum" + L)
                    dve.tensor_scalar(cntv[:, :], cnt[:, :], -1.0, float(SK), ALU.mult, ALU.add).then_inc(pre_tmp, 1)
                    dve.wait_ge(pre_tmp, 6 * b + 3 * layer + 1)
                    dve.tensor_scalar(cntm[:, :], cntv[:, :], 1.0, None, ALU.max).then_inc(pre_tmp, 1)
                    dve.wait_ge(pre_tmp, 6 * b + 3 * layer + 2)
                    dve.reciprocal(cntr[:, :], cntm[:, :]).then_inc(pre_tmp, 1)
                    dve.wait_ge(pre_tmp, 6 * b + 3 * layer + 3)
                    dve.tensor_scalar(mean[:, :], csum[:, :], cntr[:, :], None, ALU.mult).then_inc(pre_dve, 1)
                    done("mean" + L)
                    for c in range(C):
                        ins = dve.scalar_tensor_tensor(ck32[:, c, :], inv[layer], mean[:, c:c + 1], cT[:, c, :],
                                                       ALU.mult, ALU.add)
                    dve.tensor_copy(cvs[:, 0, :, :], cT).then_inc(pre_dve, 1)
                    done("ck" + L)
                    dve.tensor_copy(cks[:, 0, :, :], ck32)
                    dve.tensor_tensor(cvs[:, 1, :, :], cT, cvs[:, 0, :, :], ALU.subtract).then_inc(pre_tmp2, 1)
                    dve.wait_ge(pre_tmp2, 2 * b + layer + 1)
                    dve.tensor_tensor(cks[:, 1, :, :], ck32, cks[:, 0, :, :], ALU.subtract).then_inc(pre_dve, 1)
                    if layer == 0:
                        for m in range(G0):
                            dve.wait_ge(pre_pe, PRE_PE.upto(b, f"k{m}"))
                            dve.tensor_scalar(KTs[:, 0, m, :], psum[2 + m][:, 0:KA], 1.0 / WS, None, ALU.mult).then_inc(pre_kt, 1)
                            dve.wait_ge(pre_kt, 5 * b + m + 1)
                            dve.scalar_tensor_tensor(KTs[:, 1, m, :], psum[2 + m][:, 0:KA], 1.0 / WS, KTs[:, 0, m, :],
                                                     ALU.mult, ALU.subtract).then_inc(pre_dve, 1)
                        done("k0_3")
                        for j in range(4):
                            for piece, part in enumerate((0, 1, 0)):
                                dve.tensor_copy(Kst[32 * piece:32 * piece + 32, j::4, :],
                                                KTs[32 * j:32 * j + 32, part, :, :])
                            ins = dve.tensor_copy(Kblk[32 * j:32 * j + 32, :, j * SK:(j + 1) * SK],
                                                  KTs[32 * j:32 * j + 32, 0, :, 0:SK])
                        ins.then_inc(pre_dve, 1)
                        dve.wait_ge(pre_pe, PRE_PE.upto(b, "v0"))
                        dve.tensor_copy(E0[:, 0:3 * 33 + 1:33], mcol[:, :].to_broadcast([P, 4]))
                        dve.tensor_scalar(E0r[:, 4:8], quad[:, :], mrem[:, :], None, ALU.mult)
                        dve.tensor_scalar(V0, psum[6][:, :], 1.0 / WS, None, ALU.mult).then_inc(pre_dve, 1)
                        dve.wait_ge(pre_pe, PRE_PE.upto(b, "vr0"))
                        for j in range(4):
                            q = slice(32 * j, 32 * j + 32)
                            ins = dve.tensor_scalar(V0r[q, :, 32 * j:32 * j + 32], psum[7][q, 0:G0 * D0].rearrange(
                                "p (m d) -> p m d", m=G0), 1.0 / WS, None, ALU.mult)
                        ins.then_inc(pre_dve, 1)
                    else:
                        dve.wait_ge(pre_pe, PRE_PE.upto(b, "kk"))
                        dve.tensor_scalar(KTs[:, 0, 0, :], psum[2][:, 0:KA], 1.0 / WS, None, ALU.mult).then_inc(pre_kt, 1)
                        dve.wait_ge(pre_kt, 5 * b + 5)
                        dve.scalar_tensor_tensor(KTs[:, 1, 0, :], psum[2][:, 0:KA], 1.0 / WS, KTs[:, 0, 0, :],
                                                 ALU.mult, ALU.subtract).then_inc(pre_dve, 1)
                        done("kk")
                        for a in range(2):
                            ins = dve.tensor_scalar(KTs[:, :, 1 + a, :], KTs[:, :, 0, :], par[:, a:a + 1], None, ALU.mult)
                        ins.then_inc(pre_dve, 1)
                        done("km")
                        for j in range(4):
                            for piece, part in enumerate((0, 1, 0)):
                                dve.tensor_copy(K1st[32 * piece:32 * piece + 32, 2 * j:2 * j + 2, :],
                                                KTs[32 * j:32 * j + 32, part, 1:3, :])
                        for h in range(H1):
                            ins = dve.tensor_scalar(K1blk[:, h * SK:(h + 1) * SK], KTs[:, 0, 0, 0:SK], sel[:, h:h + 1],
                                                    None, ALU.mult)
                        ins.then_inc(pre_dve, 1)
                        dve.wait_ge(pre_pe, PRE_PE.upto(b, "v1"))
                        dve.tensor_scalar(V1[:, :, 0:D1], psum[6][:, 0:H1 * D1].rearrange("p (h d) -> p h d", h=H1),
                                          1.0 / WS, None, ALU.mult).then_inc(pre_dve, 1)
                        dve.wait_ge(pre_pe, PRE_PE.upto(b, "vr1"))
                        for j in range(4):
                            q = slice(32 * j, 32 * j + 32)
                            ins = dve.tensor_scalar(V1r[q, :, 32 * j:32 * j + D1], psum[7][q, 0:G1 * D1].rearrange(
                                "p (g d) -> p g d", g=G1), 1.0 / WS, None, ALU.mult)
                        ins.then_inc(pre_dve, 1)
            started(dve)

            def norm_x(f, s):
                if s == 0:
                    dve.wait_ge(act_f, ACT_F.upto(f, "sq3"))
                    dve.tensor_scalar(ms[:, :], ss[:, :], 1.0 / D, EPS, ALU.mult, ALU.add).then_inc(dve_f, 1)
                    dve.wait_ge(pool_f, POOL_F.upto(f, "r"))
                    if not static_first(f):
                        dve.wait_ge(pe_a, PE_A.upto(f - 1, "rb3"))
                if s >= 2:
                    dve.wait_ge(pe_f, PE_F.upto(f, f"xt{s - 2}"))
                dve.tensor_scalar(xn[:, s % 2, :], xin[:, s, :], r1[:, s:s + 1], None, ALU.mult).then_inc(dve_f, 1)

            def x_lo(f, s):
                dve.wait_ge(act_f, ACT_F.upto(f, f"xh{s}"))
                q = slice(s * P, (s + 1) * P)
                dve.tensor_tensor(AT[:, 1, :, q], ring_f[bank_f(f"xt{s}")][:, :].rearrange("p (c q) -> p c q", c=C),
                                  AT[:, 0, :, q], ALU.subtract).then_inc(dve_f, 1)

            def q_lo(f, m):
                dve.wait_ge(act_f, ACT_F.upto(f, f"qh{m}"))
                if m == 0 and not static_first(f):
                    dve.wait_ge(stack0_in, N_STACK * f)
                dve.scalar_tensor_tensor(Qs[:, 1, m, :], ring_f[bank_f(f"q{m}")][:, :], QS0, Qs[:, 0, m, :],
                                         ALU.mult, ALU.subtract).then_inc(dve_f, 1)

            def maxima(f, n):
                m, s, half = n // 8, n % 8 // 2, n % 2
                dve.wait_ge(pe_f, PE_F.upto(f, f"m{n}"))
                dve.tensor_reduce(mx[:, s, 4 * m + 2 * half:4 * m + 2 * half + 2],
                                  ring_f[bank_f(f"m{n}")][:, 0:UNIT].rearrange("p (h k) -> p h k", h=2),
                                  AX.X, ALU.max).then_inc(dve_f, 1)

            def o_evac(a, m):
                if m == 0 and not static_first(a):
                    dve.wait_ge(pe_a, PE_A.upto(a - 1, "x2t3"))
                dve.wait_ge(pe_a, PE_A.upto(a, f"v{m}"))
                dve.tensor_copy(Ou[:, m, :], bank_o[:, :]).then_inc(dve_a, 1)

            def den(a):
                dve.wait_ge(pe_a, PE_A.upto(a, "dt"))
                src = ring_a[bank_a("dt")][:, :].rearrange("p (s r) -> p s r", s=SUB)
                main = src.rearrange("p s (j m) -> p s m j", j=4)[:, :, 0:4, :]
                rest = src.rearrange("p s (m j) -> p s m j", m=4)[:, :, :, 4:8]
                dst = dq[:, :, :].rearrange("p s (m j) -> p s m j", m=4)
                dve.tensor_copy(dst, main).then_inc(dve_a, 1)
                dve.wait_ge(dve_a, DVE_A.upto(a, "dm"))
                dve.tensor_tensor(rq[:, :, :].rearrange("p s (m j) -> p s m j", m=4), rest, dst, ALU.add).then_inc(dve_a, 1)
                dve.wait_ge(dve_a, DVE_A.upto(a, "dd"))
                dve.tensor_scalar(dq[:, :, :], rq[:, :, :], 1e-30, None, ALU.max).then_inc(dve_a, 1)
                dve.wait_ge(dve_a, DVE_A.upto(a, "dg"))
                dve.reciprocal(rq[:, :, :], dq[:, :, :]).then_inc(dve_a, 1)

            def o_norm(a, m):
                dve.wait_ge(pe_a, PE_A.upto(a, f"rb{m}"))
                if m == 0:
                    dve.wait_ge(dve_a, DVE_A.upto(a, "o3"))
                dve.tensor_tensor(Ou[:, m, :], ring_a[bank_a(f"rb{m}")][:, :], Ou[:, m, :], ALU.mult).then_inc(dve_a, 1)

            def o_lo(a, m):
                dve.wait_ge(act_a, ACT_A.upto(a, f"oh{m}"))
                dve.tensor_tensor(AO[:, 1, m, :], Ou[:, m, :], AO[:, 0, m, :], ALU.subtract).then_inc(dve_a, 1)

            def residual_y(a, s):
                if s == 0:
                    dve.wait_ge(xres_in, 16 * a + 16)
                dve.wait_ge(pe_a, PE_A.upto(a, f"y{s}"))
                dve.scalar_tensor_tensor(ybuf[:, s, :], ring_a[bank_a(f"y{s}")][:, :], 1.0 / WS, xres[:, s, :],
                                         ALU.mult, ALU.add).then_inc(dve_a, 1)

            def mean_y(a, s):
                dve.wait_ge(act_a, ACT_A.upto(a, f"sqy{s}"))
                dve.tensor_scalar(msy[:, s:s + 1], ssy[:, s:s + 1], 1.0 / D, EPS, ALU.mult, ALU.add).then_inc(dve_a, 1)

            def norm_y(a, s):
                dve.wait_ge(pool_a, POOL_A.upto(a, f"ry{s}"))
                dve.scalar_tensor_tensor(ybuf[:, s, :], ybuf[:, s, :], ry[:, s:s + 1], gout_b[:, :], ALU.mult,
                                         ALU.mult).then_inc(dve_a, 1)

            def x2_lo(a, s):
                dve.wait_ge(act_a, ACT_A.upto(a, f"x2h{s}"))
                q = slice(s * P, (s + 1) * P)
                dve.tensor_tensor(XS[:, 1, :, q], ring_a[bank_a(f"x2t{s}")][:, :].rearrange("p (c q) -> p c q", c=C),
                                  XS[:, 0, :, q], ALU.subtract).then_inc(dve_a, 1)

            def q1_lo(b_):
                dve.wait_ge(act_b, ACT_B.upto(b_, "qh"))
                if not static_first(b_):
                    dve.wait_ge(stack1_in, N_STACK * b_)
                dve.scalar_tensor_tensor(Q1s[:, 1, :], ring_b[bank_b("q")][:, :], QS1, Q1s[:, 0, :],
                                         ALU.mult, ALU.subtract).then_inc(dve_b, 1)

            def maxima1(b_, n):
                s, j = n // 4, n % 4
                dve.wait_ge(pe_b, PE_B.upto(b_, f"m{n}"))
                dve.tensor_reduce(mx1[:, s, j::4], ring_b[bank_b(f"m{n}")][:, 0:UNIT].rearrange("p (h k) -> p h k", h=2),
                                  AX.X, ALU.max).then_inc(dve_b, 1)

            def o1_norm(b_, g):
                src = ring_b[bank_b(f"od{g}")][:, :].rearrange("p (s j k) -> p s j k", s=SUB, j=4)
                dve.wait_ge(pe_b, PE_B.upto(b_, f"od{g}"))
                dve.reciprocal(rq1[:, g, :, :].unsqueeze(3), src[:, :, :, D1:D1 + 1]).then_inc(dve_b, 1)
                dve.wait_ge(dve_b, DVE_B.upto(b_, f"rc{g}"))
                dst = On1[:, :, 64 * g:64 * g + 64].rearrange("p s (j d) -> p s j d", j=4)
                dve.tensor_tensor(dst, src[:, :, :, 0:D1], rq1[:, g, :, :].unsqueeze(3).to_broadcast([P, SUB, 4, D1]),
                                  ALU.mult).then_inc(dve_b, 1)

            def o1_lo(b_):
                dve.wait_ge(act_b, ACT_B.upto(b_, "oh"))
                dve.tensor_tensor(O1s[:, 1, :], ring_b[bank_b("ot")][:, :], O1s[:, 0, :], ALU.subtract).then_inc(dve_b, 1)

            def residual_x(b_, m):
                dve.wait_ge(pe_b, PE_B.upto(b_, f"xo{m}"))
                dve.scalar_tensor_tensor(XT[:, m, :], ring_b[bank_b(f"xo{m}")][:, :], 1.0 / WS, XT[:, m, :],
                                         ALU.mult, ALU.add).then_inc(dve_b, 1)

            def x_split(b_, m):
                dve.wait_ge(act_b, ACT_B.upto(b_, f"xh{m}"))
                dve.tensor_tensor(XS[:, 1, m, :], XT[:, m, :], XS[:, 0, m, :], ALU.subtract).then_inc(dve_b, 1)

            def hidden(b_, f):
                dve.wait_ge(act_b, ACT_B.upto(b_, f"h{f}"))
                dve.tensor_copy(HS[:, 0, f, :], Ht[:, f % 2, :]).then_inc(dve_b, 1)
                dve.wait_ge(dve_b, DVE_B.upto(b_, f"hh{f}"))
                dve.tensor_tensor(HS[:, 1, f, :], Ht[:, f % 2, :], HS[:, 0, f, :], ALU.subtract).then_inc(dve_b, 1)

            def residual_out(b_, m):
                dve.wait_ge(pe_b, PE_B.upto(b_, f"f{m}"))
                dve.wait_ge(pool_b, POOL_B.upto(b_, f"xb{m}"))
                dve.scalar_tensor_tensor(XT[:, m, :], ring_b[bank_b(f"f{m}")][:, :], 1.0 / WS, XT[:, m, :],
                                         ALU.mult, ALU.add).then_inc(dve_b, 1)

            def step(f, a, b_):
                if b_ is not None:
                    q1_lo(b_)
                    for n in range(16):
                        maxima1(b_, n)
                    for n in range(2):
                        o1_norm(b_, n)
                    o1_lo(b_)
                if a is not None:
                    o_evac(a, 0)
                if b_ is not None:
                    for n in range(2):
                        residual_x(b_, n)
                    x_split(b_, 0)
                if a is not None:
                    o_evac(a, 1)
                if b_ is not None:
                    residual_x(b_, 2)
                if a is not None:
                    o_evac(a, 2)
                if b_ is not None:
                    x_split(b_, 1)
                    residual_x(b_, 3)
                    x_split(b_, 2)
                if a is not None:
                    o_evac(a, 3)
                if b_ is not None:
                    x_split(b_, 3)
                if a is not None:
                    den(a)
                    for n in range(2):
                        o_norm(a, n)
                    o_lo(a, 0)
                    o_norm(a, 2)
                    o_lo(a, 1)
                    o_norm(a, 3)
                    for n in range(2, 4):
                        o_lo(a, n)
                if f is not None:
                    norm_x(f, 0)
                if a is not None:
                    residual_y(a, 0)
                if f is not None:
                    norm_x(f, 1)
                if a is not None:
                    residual_y(a, 1)
                if b_ is not None:
                    for n in range(2):
                        hidden(b_, n)
                if f is not None:
                    norm_x(f, 2)
                if a is not None:
                    mean_y(a, 0)
                    residual_y(a, 2)
                if f is not None:
                    norm_x(f, 3)
                if b_ is not None:
                    hidden(b_, 2)
                if f is not None:
                    for n in range(4):
                        x_lo(f, n)
                if a is not None:
                    mean_y(a, 1)
                if b_ is not None:
                    hidden(b_, 3)
                if f is not None:
                    q_lo(f, 0)
                if a is not None:
                    norm_y(a, 0)
                    residual_y(a, 3)
                if f is not None:
                    q_lo(f, 1)
                    maxima(f, 0)
                if b_ is not None:
                    residual_out(b_, 0)
                if f is not None:
                    for n in range(1, 7):
                        maxima(f, n)
                if a is not None:
                    mean_y(a, 2)
                if f is not None:
                    maxima(f, 7)
                if b_ is not None:
                    residual_out(b_, 1)
                if f is not None:
                    q_lo(f, 2)
                    for n in range(8, 16):
                        maxima(f, n)
                if b_ is not None:
                    residual_out(b_, 2)
                if a is not None:
                    norm_y(a, 1)
                if b_ is not None:
                    residual_out(b_, 3)
                if f is not None:
                    q_lo(f, 3)
                    for n in range(16, 23):
                        maxima(f, n)
                if a is not None:
                    x2_lo(a, 0)
                if f is not None:
                    for n in range(23, 25):
                        maxima(f, n)
                if a is not None:
                    mean_y(a, 3)
                if f is not None:
                    maxima(f, 25)
                if a is not None:
                    norm_y(a, 2)
                if f is not None:
                    for n in range(26, 28):
                        maxima(f, n)
                if a is not None:
                    x2_lo(a, 1)
                    norm_y(a, 3)
                if f is not None:
                    for n in range(28, 32):
                        maxima(f, n)
                if a is not None:
                    for n in range(2, 4):
                        x2_lo(a, n)

            step(0, None, None)
            step(1, 0, None)
            step(2, 1, 0)
            with dve.Fori(1, NT - 2) as i:
                step(i + 2, i + 1, i)
            step(None, NT - 1, NT - 2)
            step(None, None, NT - 1)

        @block.tensor
        def _(pe):
            PASSES = ((0, 0), (1, 0), (0, 1))

            def split_chunk(dst, lhs, rhs, c, chunks):
                for n, (p, q) in enumerate(PASSES):
                    ins = pe.matmul(dst, lhs(p, c), rhs(q, c), start=c == 0 and n == 0,
                                    stop=c == chunks - 1 and n == len(PASSES) - 1)
                return ins

            def split_matmul(dst, lhs, rhs, chunks):
                for c in range(chunks):
                    ins = split_chunk(dst, lhs, rhs, c, chunks)
                return ins

            pe.wait_ge(const_ready, 8)
            pe.wait_ge(weight_split, 4 * 2 + len(SMALL))
            with pe.Fori(0, B) as b:
                for layer in range(2):
                    L = str(layer)
                    src = cn if layer == 0 else crow
                    if layer == 0:
                        pe.wait_ge(pre_dve, PRE_DVE.upto(b, "cn0"))
                    else:
                        pe.wait_ge(pre_dve, PRE_DVE.upto(b, "vr0"))
                    for c in range(C):
                        ins = pe.transpose(psum[0][:, c * P:(c + 1) * P], src[:, 0, c * P:(c + 1) * P], ident[:, :])
                    ins.then_inc(pre_pe, 1)
                    for c in range(C):
                        ins = pe.transpose(psum[1][:, c * KP:(c + 1) * KP], src[0:KP, 1, c * P:(c + 1) * P],
                                           ident[0:KP, 0:KP])
                    ins.then_inc(pre_pe, 1)
                    pe.wait_ge(pre_dve, PRE_DVE.upto(b, "cks" + L))
                    if layer == 0:
                        for m in range(G0):
                            split_matmul(psum[2 + m][:, 0:KA], lambda p, c: WKV[:, 0, p, c, m * P:(m + 1) * P],
                                         lambda q, c: cks[:, q, c, :], C).then_inc(pre_pe, 1)
                        split_matmul(psum[6][:, :], lambda p, c: cvs[:, p, c, 0:KM],
                                     lambda q, c: WKV[:, 1, q, c, :], C).then_inc(pre_pe, 1)
                        for j in range(4):
                            ins = split_matmul(
                                psum[7][32 * j:32 * j + 32, 0:G0 * D0], lambda p, c: cvs[:, p, c, KM:KA],
                                lambda q, c: WKV[:, 1, q, c, :].rearrange("p (m n) -> p m n", m=G0)[
                                    :, :, 32 * j:32 * j + 32], C)
                        ins.then_inc(pre_pe, 1)
                    else:
                        split_matmul(psum[2][:, 0:KA], lambda p, c: WKV1[:, 0, p, c, :],
                                     lambda q, c: cks[:, q, c, :], C).then_inc(pre_pe, 1)
                        split_matmul(psum[6][:, 0:P], lambda p, c: cvs[:, p, c, 0:KM],
                                     lambda q, c: WKV1[:, 1, q, c, :], C).then_inc(pre_pe, 1)
                        for j in range(4):
                            ins = split_matmul(
                                psum[7][32 * j:32 * j + 32, 0:G1 * D1], lambda p, c: cvs[:, p, c, KM:KA],
                                lambda q, c: WKV1[:, 1, q, c, :].rearrange("p (g n) -> p g n", g=G1)[
                                    :, :, D1 * j:D1 * j + D1], C)
                        ins.then_inc(pre_pe, 1)
            started(pe)

            def wait_bank(ring, reader, sems, steps, t, unit):
                before, ago = bank_before(ring, unit)
                if ago and static_first(t):
                    return
                engine, name = reader[before]
                pe.wait_ge(sems[engine], steps[engine].upto(t - ago, name))

            def free_f(f, unit):
                wait_bank(RING_F, READER_F, {"act": act_f, "dve": dve_f}, {"act": ACT_F, "dve": DVE_F}, f, unit)
                return ring_f[bank_f(unit)]

            def free_a(a, unit):
                wait_bank(RING_A, READER_A, {"act": act_a, "dve": dve_a}, {"act": ACT_A, "dve": DVE_A}, a, unit)
                return ring_a[bank_a(unit)]

            def free_b(b_, unit):
                wait_bank(RING_B, READER_B, {"act": act_b, "dve": dve_b}, {"act": ACT_B, "dve": DVE_B}, b_, unit)
                return ring_b[bank_b(unit)]

            def x_transpose(f, s):
                bank = free_f(f, f"xt{s}")
                pe.wait_ge(dve_f, DVE_F.upto(f, f"xn{s}"))
                for c in range(C):
                    ins = pe.transpose(bank[:, c * P:(c + 1) * P], xn[:, s % 2, c * P:(c + 1) * P], ident[:, :])
                ins.then_inc(pe_f, 1)

            def query(f, m, k):
                bank = free_f(f, f"q{m}") if k == 0 else ring_f[bank_f(f"q{m}")]
                if m == 0 and k == 0:
                    pe.wait_ge(dve_f, DVE_F.upto(f, "xl3"))
                ins = split_chunk(bank[:, :], lambda p, c: WQ[:, p, c, m * P:(m + 1) * P],
                             lambda q, c: AT[:, q, c, :], k, C)
                if k == C - 1:
                    ins.then_inc(pe_f, 1)

            def max_unit(f, n):
                m, s, half = n // 8, n % 8 // 2, n % 2
                bank = free_f(f, f"m{n}")
                if n % 8 == 0:
                    pe.wait_ge(act_f, ACT_F.upto(f, f"qh{m}"))
                if n == 0:
                    pe.wait_ge(blk0_in, 16 * f + 16)
                pe.matmul(bank[:, 0:UNIT], Qs[:, 0, m, s * P:(s + 1) * P], Kblk[:, m, half * UNIT:(half + 1) * UNIT],
                          start=True, stop=True).then_inc(pe_f, 1)

            def max_transpose(f):
                bank = free_f(f, "mt")
                pe.wait_ge(dve_f, DVE_F.upto(f, "mx31"))
                for s in range(SUB):
                    ins = pe.transpose(bank[0:H0, s * P:(s + 1) * P], mx[:, s, :], ident[:, :])
                ins.then_inc(pe_f, 1)

            def scores(a, g, j):
                if g == 0 and j == 0:
                    pe.wait_ge(stack0_in, N_STACK * (a + 1))
                    pe.wait_ge(max0_in, 16 * a + 16)
                    pe.wait_ge(kv0_in, 16 * a + 16)
                if j < 4:
                    bank = free_a(a, f"s{g}{j}")
                    ins = pe.matmul(bank[:, :], Kst[0:97, 4 * g + j, 0:KM], Qst[0:97, 4 * g + j, :], start=True, stop=True)
                else:
                    bank = free_a(a, f"r{g}")
                    for i in range(4):
                        ins = pe.matmul(bank[32 * i:32 * i + 32, :], Kst[0:97, 4 * g + i, KM:KA],
                                        Qst[0:97, 4 * g + i, :], start=True, stop=True)
                ins.then_inc(pe_a, 1)

            def values_rest(a, g):
                if g:
                    pe.wait_ge(dve_a, DVE_A.upto(a, f"o{g - 1}"))
                elif not static_first(a):
                    pe.wait_ge(act_b, ACT_B.upto(a - 1, "od1"))
                    pe.wait_ge(act_a, ACT_A.upto(a - 1, "dsb"))
                pe.wait_ge(act_a, ACT_A.upto(a, f"er{g}"))
                pe.matmul(bank_o[:, :], V0r[:, g, :], Pr[:, 5 * (g % 2) + 4, :], start=True, stop=False)

            def values(a, g):
                for j in range(4):
                    h = 4 * g + j
                    pe.matmul(bank_o[32 * j:32 * j + 32, :], V0[:, h * D0:(h + 1) * D0], Pr[:, 5 * (g % 2) + j, :],
                              start=False, stop=True)

            def denominators(a, g):
                slot = 5 * (g % 2)
                for j in range(4):
                    pe.matmul(bank_d[32 * j:32 * j + 32, :], E0[:, 32 * g:32 * g + 32], Pr[:, slot + j, :],
                              start=g == 0, stop=False, skip_group_check=True)
                pe.matmul(bank_d[32 * g:32 * g + 32, :], E0r[:, :], Pr[:, slot + 4, :],
                          start=False, stop=g == G0 - 1, skip_group_check=True).then_inc(pe_a, 1)

            def den_transpose(a):
                bank = free_a(a, "dt")
                pe.wait_ge(act_a, ACT_A.upto(a, "dsb"))
                for s in range(SUB):
                    ins = pe.transpose(bank[:, s * P:(s + 1) * P], Dsb[:, s * P:(s + 1) * P], ident[:, :])
                ins.then_inc(pe_a, 1)

            def den_spread(a, m):
                bank = free_a(a, f"rb{m}")
                pe.wait_ge(pool_a, POOL_A.upto(a, f"rr{m}"))
                for s in range(SUB):
                    ins = pe.transpose(bank[:, s * P:(s + 1) * P], xn[:, m % 2, s * P:(s + 1) * P], ident[:, :])
                ins.then_inc(pe_a, 1)

            def project_out(a, s, k):
                bank = free_a(a, f"y{s}") if k == 0 else ring_a[bank_a(f"y{s}")]
                if s == 0:
                    pe.wait_ge(dve_a, DVE_A.upto(a, f"ol{k}"))
                ins = split_chunk(bank[:, :], lambda p, c: AO[:, p, c, s * P:(s + 1) * P],
                             lambda q, c: WO[:, q, c, :], k, C)
                if k == C - 1:
                    ins.then_inc(pe_a, 1)

            def x2_transpose(a, s):
                bank = free_a(a, f"x2t{s}")
                pe.wait_ge(dve_a, DVE_A.upto(a, f"x2_{s}"))
                for c in range(C):
                    ins = pe.transpose(bank[:, c * P:(c + 1) * P], ybuf[:, s, c * P:(c + 1) * P], ident[:, :])
                ins.then_inc(pe_a, 1)

            def query1(b_, k):
                bank = free_b(b_, "q") if k == 0 else ring_b[bank_b("q")]
                if k == 0:
                    pe.wait_ge(dve_a, DVE_A.upto(b_, "x2l3"))
                ins = split_chunk(bank[:, :], lambda p, c: WQ1[:, p, c, :], lambda q, c: XS[:, q, c, :], k, C)
                if k == C - 1:
                    ins.then_inc(pe_b, 1)

            def max_unit1(b_, n):
                s, j = n // 4, n % 4
                bank = free_b(b_, f"m{n}")
                if n == 0:
                    pe.wait_ge(act_b, ACT_B.upto(b_, "qh"))
                    pe.wait_ge(kv1_in, 16 * b_ + 16)
                pe.matmul(bank[:, 0:UNIT], Q1s[:, 0, s * P:(s + 1) * P], K1blk[:, j * UNIT:(j + 1) * UNIT],
                          start=True, stop=True).then_inc(pe_b, 1)

            def max_transpose1(b_):
                bank = free_b(b_, "mt")
                pe.wait_ge(dve_b, DVE_B.upto(b_, "mx15"))
                for s in range(SUB):
                    ins = pe.transpose(bank[0:H1, s * P:(s + 1) * P], mx1[:, s, :], ident[:, :])
                ins.then_inc(pe_b, 1)

            def scores1(b_, g, j):
                if g == 0 and j == 0:
                    pe.wait_ge(stack1_in, N_STACK * (b_ + 1))
                    pe.wait_ge(max1_in, 16 * b_ + 16)
                if j < 4:
                    h = 4 * g + j
                    bank = free_b(b_, f"s{g}{j}")
                    ins = pe.matmul(bank[:, :], K1st[0:98, h, 0:KM], Q1st[0:98, h // 2, :], start=True, stop=True)
                else:
                    bank = free_b(b_, f"r{g}")
                    for i in range(4):
                        h = 4 * g + i
                        ins = pe.matmul(bank[32 * i:32 * i + 32, :], K1st[0:98, h, KM:KA], Q1st[0:98, h // 2, :],
                                        start=True, stop=True)
                ins.then_inc(pe_b, 1)

            def values1(b_, g):
                if g:
                    pe.wait_ge(act_b, ACT_B.upto(b_, "od0"))
                else:
                    pe.wait_ge(dve_a, DVE_A.upto(b_, "o3"))
                pe.wait_ge(act_b, ACT_B.upto(b_, f"er{g}"))
                pe.matmul(bank_o[:, :], V1r[:, g, :], Pr[:, 5 * g + 4, :], start=True, stop=False)
                for j in range(4):
                    ins = pe.matmul(bank_o[32 * j:32 * j + 32, :], V1[:, 4 * g + j, :], Pr[:, 5 * g + j, :],
                                    start=False, stop=True)
                ins.then_inc(pe_b, 1)

            def o1_transpose(b_, g):
                bank = free_b(b_, f"od{g}")
                pe.wait_ge(act_b, ACT_B.upto(b_, f"od{g}"))
                for s in range(SUB):
                    ins = pe.transpose(bank[:, s * P:(s + 1) * P], OD[:, g, s * P:(s + 1) * P], ident[:, :])
                ins.then_inc(pe_b, 1)

            def o1_back(b_):
                bank = free_b(b_, "ot")
                pe.wait_ge(dve_b, DVE_B.upto(b_, "on1"))
                for s in range(SUB):
                    ins = pe.transpose(bank[:, s * P:(s + 1) * P], On1[:, s, :], ident[:, :])
                ins.then_inc(pe_b, 1)

            def project_out1(b_, m):
                bank = free_b(b_, f"xo{m}")
                if m == 0:
                    pe.wait_ge(dve_b, DVE_B.upto(b_, "ol"))
                split_matmul(bank[:, :], lambda p, c: WO1[:, p, c, m * P:(m + 1) * P],
                             lambda q, c: O1s[:, q, :], 1).then_inc(pe_b, 1)

            def hidden(b_, f, k):
                bank = free_b(b_, f"h{f}") if k == 0 else ring_b[bank_b(f"h{f}")]
                if f == 0:
                    pe.wait_ge(dve_b, DVE_B.upto(b_, f"xl{k}"))
                ins = split_chunk(bank[:, :], lambda p, c: W1[:, p, c, f * P:(f + 1) * P],
                             lambda q, c: XS[:, q, c, :], k, C)
                if k == C - 1:
                    ins.then_inc(pe_b, 1)

            def ffn_out(b_, m, k):
                bank = free_b(b_, f"f{m}") if k == 0 else ring_b[bank_b(f"f{m}")]
                if m == 0:
                    pe.wait_ge(dve_b, DVE_B.upto(b_, f"hl{k}"))
                ins = split_chunk(bank[:, :], lambda p, c: W2[:, p, c, m * P:(m + 1) * P],
                             lambda q, c: HS[:, q, c, :], k, C)
                if k == C - 1:
                    ins.then_inc(pe_b, 1)

            def out_transpose(b_, s):
                bank = free_b(b_, f"t{s}")
                if s == 0:
                    pe.wait_ge(dve_b, DVE_B.upto(b_, "f3"))
                for c in range(C):
                    ins = pe.transpose(bank[:, c * P:(c + 1) * P], XT[:, c, s * P:(s + 1) * P], ident[:, :])
                ins.then_inc(pe_b, 1)

            def step(f, a, b_):
                if b_ is not None:
                    for n in range(4):
                        query1(b_, n)
                    for n in range(16):
                        max_unit1(b_, n)
                    max_transpose1(b_)
                    for n in range(5):
                        scores1(b_, 0, n)
                if a is not None:
                    scores(a, 0, 0)
                if b_ is not None:
                    values1(b_, 0)
                if a is not None:
                    scores(a, 0, 1)
                if b_ is not None:
                    for n in range(4):
                        scores1(b_, 1, n)
                if a is not None:
                    scores(a, 0, 2)
                if b_ is not None:
                    scores1(b_, 1, 4)
                if a is not None:
                    scores(a, 0, 3)
                if b_ is not None:
                    values1(b_, 1)
                if a is not None:
                    scores(a, 0, 4)
                    scores(a, 1, 0)
                if b_ is not None:
                    for n in range(2):
                        o1_transpose(b_, n)
                if a is not None:
                    values_rest(a, 0)
                    for n in range(1, 3):
                        scores(a, 1, n)
                if b_ is not None:
                    o1_back(b_)
                if a is not None:
                    values(a, 0)
                    for n in range(3, 5):
                        scores(a, 1, n)
                    denominators(a, 0)
                if b_ is not None:
                    for n in range(2):
                        project_out1(b_, n)
                if a is not None:
                    scores(a, 2, 0)
                    values_rest(a, 1)
                    for n in range(1, 3):
                        scores(a, 2, n)
                    values(a, 1)
                    for n in range(3, 5):
                        scores(a, 2, n)
                    denominators(a, 1)
                if b_ is not None:
                    project_out1(b_, 2)
                if a is not None:
                    scores(a, 3, 0)
                    values_rest(a, 2)
                    for n in range(1, 3):
                        scores(a, 3, n)
                    values(a, 2)
                    for n in range(3, 5):
                        scores(a, 3, n)
                    denominators(a, 2)
                if b_ is not None:
                    project_out1(b_, 3)
                    hidden(b_, 0, 0)
                if a is not None:
                    values_rest(a, 3)
                    values(a, 3)
                    denominators(a, 3)
                if b_ is not None:
                    for n in range(1, 3):
                        hidden(b_, 0, n)
                if a is not None:
                    den_transpose(a)
                if b_ is not None:
                    hidden(b_, 0, 3)
                    for n in range(4):
                        hidden(b_, 1, n)
                if a is not None:
                    den_spread(a, 0)
                if b_ is not None:
                    hidden(b_, 2, 0)
                if a is not None:
                    den_spread(a, 1)
                if b_ is not None:
                    hidden(b_, 2, 1)
                if a is not None:
                    den_spread(a, 2)
                if b_ is not None:
                    hidden(b_, 2, 2)
                if a is not None:
                    den_spread(a, 3)
                if b_ is not None:
                    hidden(b_, 2, 3)
                if a is not None:
                    for n in range(4):
                        project_out(a, 0, n)
                    for n in range(4):
                        project_out(a, 1, n)
                    for n in range(2):
                        project_out(a, 2, n)
                if f is not None:
                    x_transpose(f, 0)
                if a is not None:
                    project_out(a, 2, 2)
                if f is not None:
                    x_transpose(f, 1)
                if a is not None:
                    project_out(a, 2, 3)
                    for n in range(4):
                        project_out(a, 3, n)
                if b_ is not None:
                    for n in range(3):
                        hidden(b_, 3, n)
                if f is not None:
                    for n in range(2, 4):
                        x_transpose(f, n)
                if b_ is not None:
                    hidden(b_, 3, 3)
                    for n in range(2):
                        ffn_out(b_, 0, n)
                if f is not None:
                    for n in range(4):
                        query(f, 0, n)
                    for n in range(4):
                        query(f, 1, n)
                    max_unit(f, 0)
                if b_ is not None:
                    for n in range(2, 4):
                        ffn_out(b_, 0, n)
                    ffn_out(b_, 1, 0)
                if f is not None:
                    for n in range(1, 3):
                        max_unit(f, n)
                if b_ is not None:
                    ffn_out(b_, 1, 1)
                if f is not None:
                    max_unit(f, 3)
                if b_ is not None:
                    ffn_out(b_, 1, 2)
                if f is not None:
                    for n in range(4, 6):
                        max_unit(f, n)
                if b_ is not None:
                    ffn_out(b_, 1, 3)
                if f is not None:
                    max_unit(f, 6)
                if b_ is not None:
                    ffn_out(b_, 2, 0)
                if f is not None:
                    max_unit(f, 7)
                    for n in range(4):
                        query(f, 2, n)
                if b_ is not None:
                    ffn_out(b_, 2, 1)
                if f is not None:
                    max_unit(f, 8)
                if b_ is not None:
                    for n in range(2, 4):
                        ffn_out(b_, 2, n)
                if f is not None:
                    for n in range(9, 11):
                        max_unit(f, n)
                if b_ is not None:
                    ffn_out(b_, 3, 0)
                if f is not None:
                    max_unit(f, 11)
                if b_ is not None:
                    ffn_out(b_, 3, 1)
                if f is not None:
                    for n in range(12, 14):
                        max_unit(f, n)
                if b_ is not None:
                    ffn_out(b_, 3, 2)
                if f is not None:
                    max_unit(f, 14)
                if b_ is not None:
                    ffn_out(b_, 3, 3)
                if f is not None:
                    max_unit(f, 15)
                    for n in range(4):
                        query(f, 3, n)
                    max_unit(f, 16)
                if b_ is not None:
                    out_transpose(b_, 0)
                if a is not None:
                    x2_transpose(a, 0)
                if b_ is not None:
                    out_transpose(b_, 1)
                if f is not None:
                    max_unit(f, 17)
                if b_ is not None:
                    out_transpose(b_, 2)
                if f is not None:
                    for n in range(18, 20):
                        max_unit(f, n)
                if b_ is not None:
                    out_transpose(b_, 3)
                if f is not None:
                    for n in range(20, 25):
                        max_unit(f, n)
                if a is not None:
                    x2_transpose(a, 1)
                if f is not None:
                    for n in range(25, 30):
                        max_unit(f, n)
                if a is not None:
                    for n in range(2, 4):
                        x2_transpose(a, n)
                if f is not None:
                    for n in range(30, 32):
                        max_unit(f, n)
                    max_transpose(f)

            step(0, None, None)
            step(1, 0, None)
            step(2, 1, 0)
            with pe.Fori(1, NT - 2) as i:
                step(i + 2, i + 1, i)
            step(None, NT - 1, NT - 2)
            step(None, None, NT - 1)


def kernel(x, ctx_1024, mask_BxS2_bf1, L0_xattn_Wq, L0_xattn_Wk, L0_xattn_Wv, L0_xattn_Wo, L0_xattn_g_q,
           L0_xattn_g_c, L0_xattn_g_out, L1_xattn_W_q, L1_xattn_W_k, L1_xattn_W_v, L1_xattn_W_o, L1_xattn_w1,
           L1_xattn_b1, L1_xattn_w2, L1_xattn_b2):
    import numpy as np
    import concourse.bacc as bacc
    from concourse.bass_utils import run_bass_kernel_spmd

    def by_chunk(v):
        return np.asarray(v).reshape(C, P).T

    nc = bacc.Bacc("TRN2", target_bir_lowering=False, num_devices=1)
    arrays = {
        "x": np.asarray(x).reshape(B * S, D), "ctxt": np.asarray(ctx_1024).reshape(B * SK, D),
        "mask": np.asarray(mask_BxS2_bf1).view(np.uint8), "mask_col": np.asarray(mask_BxS2_bf1).view(np.uint8).reshape(B * SK, 1),
        "wq": L0_xattn_Wq, "wk": L0_xattn_Wk, "wv": L0_xattn_Wv, "wo": L0_xattn_Wo,
        "gq": by_chunk(L0_xattn_g_q), "gc": by_chunk(L0_xattn_g_c), "gout": L0_xattn_g_out,
        "wq1": L1_xattn_W_q, "wk1": L1_xattn_W_k, "wv1": L1_xattn_W_v, "wo1": L1_xattn_W_o,
        "w1t": np.asarray(L1_xattn_w1).T, "b1": by_chunk(L1_xattn_b1), "w2t": np.asarray(L1_xattn_w2).T, "b2": by_chunk(L1_xattn_b2),
    }
    arrays = {n: np.ascontiguousarray(a) for n, a in arrays.items()}
    aps = {n: nc.dram_tensor(n, a.shape, mybir.dt.from_np(a.dtype), kind="ExternalInput").ap()
           for n, a in arrays.items()}
    out = nc.dram_tensor("out", (B * S, D), F32, kind="ExternalOutput").ap()
    build(nc, *aps.values(), out)
    result = run_bass_kernel_spmd(nc, [arrays], core_ids=[0])
    return result.results[0]["out"].reshape(B, S, D)
```

```python
from contextlib import ExitStack

import concourse.bass as bass
from concourse import mybir

F32 = mybir.dt.float32
F16 = mybir.dt.float16
U8 = mybir.dt.uint8
ALU = mybir.AluOpType
ACT = mybir.ActivationFunctionType
AX = mybir.AxisListType

P = 128
D = 512
C = D // P
B, S, SK = 4, 2048, 154
KM = 128
KR = SK - KM
KP = 32
KA = KM + KP
T = 512
SUB = T // P
NT = B * S // T
TPB = S // T
H0, D0 = 16, 32
H1, D1 = 8, 16
G0 = H0 // 4
G1 = H1 // 4
EPS = 1e-6
WS = 64.0
UNIT = 2 * SK

K0_ST, K0_BLK, K0_V, K0_VR, K0_E, K0_ER = H0 * KA, G0 * 4 * SK, 2 * D, 2 * G0 * P, 2 * 4 * 32, 2 * 32
IMG0 = K0_ST + K0_BLK + K0_V + K0_VR + K0_E + K0_ER
K1_ST, K1_BLK, K1_V, K1_VR = H1 * KA, H1 * SK, 2 * H1 * 32, 2 * G1 * P
IMG1 = K1_ST + K1_BLK + K1_V + K1_VR


class Steps:

    def __init__(self, names):
        self.names = names.split() if isinstance(names, str) else list(names)
        assert len(set(self.names)) == len(self.names)
        self.at = {n: i + 1 for i, n in enumerate(self.names)}

    def upto(self, turn, name):
        return turn * len(self.names) + self.at[name]


def nums(fmt, n):
    return [fmt.format(i) for i in range(n)]


def order_qm():
    return ["q0", "q1"] + [n for m in range(2, G0) for n in nums("m{}", 8 * m - 8)[8 * m - 16:] + [f"q{m}"]] \
        + nums("m{}", 32)[16:]


def order_scores():
    names = ["r0"] + nums("s0{}", 4)
    for g in range(G0 - 1):
        n = g + 1
        names += [f"r{n}", f"s{n}0", f"s{n}1", f"w{g}", f"s{n}2", f"s{n}3", f"v{g}"]
    return names + [f"w{G0 - 1}", f"v{G0 - 1}"]


PRE_ACT = Steps("sq sqr kst0")
PRE_POOL = Steps("r")
PRE_PE = Steps("ta0 tb0 ta1 tb1 k0 k1 k2 k3 v0 vr0 kk v1 vr1")
PRE_DVE = Steps("masks ms sc0 cn0 ct0 sum0 mean0 ck0 cks0 ct1 sum1 mean1 ck1 cks1 "
                "k0_0 k0_1 k0_2 k0_3 kst0 v0 vr0 kk km kst1 v1 vr1")

PE_F = Steps(nums("xt{}", SUB) + order_qm() + ["mt"])
ACT_F = Steps(nums("sq{}", SUB) + nums("xh{}", SUB) + nums("qh{}", G0) + ["negm"])
DVE_F = Steps(["ms"] + nums("xn{}", SUB) + nums("xl{}", SUB)
              + ["ql0", "ql1"] + nums("mx{}", 8) + ["ql2"] + nums("mx{}", 16)[8:] + ["ql3"] + nums("mx{}", 32)[16:])
POOL_F = Steps("r")
PE_A = Steps(order_scores() + ["dt"] + nums("rb{}", G0) + nums("y{}", SUB) + nums("x2t{}", SUB))
ACT_A = Steps([n for g in range(G0) for n in [f"er{g}"] + nums(f"e{g}" + "{}", 4)]
              + ["dsb"] + nums("oh{}", G0) + nums("sqy{}", SUB)
              + [n for s in range(SUB) for n in (f"xf{s}", f"x2h{s}")])
DVE_A = Steps(nums("o{}", G0) + ["dm", "dd", "dg", "rc"] + "on0 on1 ol0 on2 ol1 on3 ol2 ol3".split()
              + "y0 y1 ms0 y2 ms1 x2_0 y3 ms2 x2_1 x2l0 ms3 x2_2 x2l1 x2_3 x2l2 x2l3".split())
POOL_A = Steps(nums("rr{}", G0) + nums("ry{}", SUB))
PE_B = Steps(["q"] + nums("m{}", 16) + ["mt"]
             + [n for g in range(G1) for n in [f"r{g}"] + nums(f"s{g}" + "{}", 4) + [f"v{g}"]]
             + ["od0", "od1", "ot"] + nums("xo{}", C) + nums("h{}", C) + nums("f{}", C) + nums("t{}", SUB))
ACT_B = Steps(["qh", "negm"] + [n for g in range(G1) for n in [f"er{g}"] + nums(f"e{g}" + "{}", 4) + [f"od{g}"]]
              + ["oh"] + nums("xh{}", C) + nums("h{}", C) + nums("t{}", SUB))
DVE_B = Steps(["ql"] + nums("mx{}", 16) + ["rc0", "on0", "rc1", "on1", "ol"]
              + ["xo0", "xo1", "xl0", "xo2", "xl1", "xo3", "xl2", "xl3"]
              + [n for f in range(C) for n in (f"hh{f}", f"hl{f}")] + nums("f{}", C))
POOL_B = Steps(nums("xb{}", C))

def in_turn(units, banks):
    return [(u, banks[i % len(banks)]) for i, u in enumerate(units)]


RING_F = in_turn(PE_F.names, (0, 1))
READER_F = {**{f"xt{s}": ("dve", f"xl{s}") for s in range(SUB)}, **{f"q{m}": ("dve", f"ql{m}") for m in range(G0)},
            **{f"m{n}": ("dve", f"mx{n}") for n in range(32)}, "mt": ("act", "negm")}
RING_A = in_turn([n for n in PE_A.names if n[0] not in "wv"], (0, 1))
READER_A = {**{f"s{g}{j}": ("act", f"e{g}{j}") for g in range(G0) for j in range(4)},
            **{f"r{g}": ("act", f"er{g}") for g in range(G0)}, "dt": ("dve", "dd"),
            **{f"rb{m}": ("dve", f"on{m}") for m in range(G0)}, **{f"y{s}": ("dve", f"y{s}") for s in range(SUB)},
            **{f"x2t{s}": ("dve", f"x2l{s}") for s in range(SUB)}}
RING_B = in_turn(["q"] + nums("m{}", 16) + ["mt"] + [n for g in range(G1) for n in [f"r{g}"] + nums(f"s{g}" + "{}", 4)] \
    + ["od0", "od1", "ot"] + nums("xo{}", C) + nums("h{}", C) + nums("f{}", C) + nums("t{}", SUB), (0, 1))
READER_B = {"q": ("dve", "ql"), **{f"m{n}": ("dve", f"mx{n}") for n in range(16)}, "mt": ("act", "negm"),
            **{f"s{g}{j}": ("act", f"e{g}{j}") for g in range(G1) for j in range(4)},
            **{f"r{g}": ("act", f"er{g}") for g in range(G1)}, "od0": ("dve", "on0"), "od1": ("dve", "on1"),
            "ot": ("dve", "ol"), **{f"xo{m}": ("dve", f"xo{m}") for m in range(C)},
            **{f"h{f}": ("act", f"h{f}") for f in range(C)}, **{f"f{m}": ("dve", f"f{m}") for m in range(C)},
            **{f"t{s}": ("act", f"t{s}") for s in range(SUB)}}
QS0 = D0 ** -0.5 / WS
QS1 = D1 ** -0.5 / WS


def bank_before(ring, unit):
    same = [u for u, bank in ring if bank == dict(ring)[unit]]
    k = same.index(unit)
    return (same[k - 1], 0) if k else (same[-1], 1)


def bank_f(unit):
    return dict(RING_F)[unit]


def bank_a(unit):
    return dict(RING_A)[unit]


def bank_b(unit):
    return dict(RING_B)[unit]


def static_first(t):
    return isinstance(t, int) and t == 0


def early(t):
    return isinstance(t, int) and t < 2


def static_last(t):
    return isinstance(t, int) and t == NT - 1


def batch_of(t):
    return t // TPB


def build(nc, x, ctxt, mask, mask_col, wq, wk, wv, wo, gq, gc, gout, wq1, wk1, wv1, wo1, w1t, b1, w2t, b2, out):
    stack = ExitStack()
    with stack:
        def sb(name, shape, dt=F32):
            return stack.enter_context(nc.sbuf_tensor(name, shape, dt))

        def sem(name):
            return stack.enter_context(nc.semaphore(name))

        WQ, WO, W1, W2 = (sb(n, [P, 2, C, D], F16) for n in ("WQ", "WO", "W1", "W2"))
        WQ1 = sb("WQ1", [P, 2, C, P], F16)
        WO1 = sb("WO1", [P, 2, 1, D], F16)
        ident = sb("ident", [P, P])
        gout_b = sb("gout_b", [P, D])
        gq_c, gc_c, b1_c, b2_c = (sb(n, [P, C]) for n in ("gq_c", "gc_c", "b1_c", "b2_c"))
        one = sb("one", [P, 1])
        mhalf = sb("mhalf", [P, SUB])
        img0 = sb("img0", [P, IMG0], F16)
        img1 = sb("img1", [P, IMG1], F16)
        o = 0
        Kblk = img0[:, o:o + K0_BLK].rearrange("p (m k) -> p m k", m=G0); o += K0_BLK
        Kst = img0[:, o:o + K0_ST].rearrange("p (h k) -> p h k", h=H0); o += K0_ST
        V0 = img0[:, o:o + K0_V].bitcast(F32); o += K0_V
        V0r = img0[:, o:o + K0_VR].bitcast(F32).rearrange("p (m k) -> p m k", m=G0); o += K0_VR
        E0 = img0[:, o:o + K0_E].bitcast(F32); o += K0_E
        E0r = img0[:, o:o + K0_ER].bitcast(F32)
        o = 0
        K1st = img1[:, o:o + K1_ST].rearrange("p (h k) -> p h k", h=H1); o += K1_ST
        K1blk = img1[:, o:o + K1_BLK]; o += K1_BLK
        V1 = img1[:, o:o + K1_V].bitcast(F32).rearrange("p (h k) -> p h k", h=H1); o += K1_V
        V1r = img1[:, o:o + K1_VR].bitcast(F32).rearrange("p (g k) -> p g k", g=G1)
        xin = sb("xin", [P, SUB, D])
        xres = sb("xres", [P, SUB, D])
        xn = sb("xn", [P, 2, D])
        ybuf = sb("ybuf", [P, SUB, D])
        AT = sb("AT", [P, 2, C, T], F16)
        Qs = sb("Qs", [P, 2, G0, T], F16)
        Qst = sb("Qst", [P, H0, T], F16)
        Pr = sb("Pr", [P, 10, T])
        Ou = ybuf
        AO = sb("AO", [P, 2, C, T], F16)
        Dsb = sb("Dsb", [P, T])
        mx = sb("mx", [P, SUB, H0])
        negm = sb("negm", [H0, T], F16)
        dq = sb("dq", [P, SUB, H0])
        rq = sb("rq", [P, SUB, H0])
        junk = sb("junk", [P, D], F16)
        junk_y = sb("junk_y", [P, 2, D], F16)
        ss, r1, ssy, ry = (sb(n, [P, SUB]) for n in ("ss", "r1", "ssy", "ry"))
        ms, msy = sb("ms", [P, SUB]), sb("msy", [P, SUB])
        XT = sb("XT", [P, C, T])
        XS = sb("XS", [P, 2, C, T], F16)
        Q1s = sb("Q1s", [P, 2, T], F16)
        Q1st = sb("Q1st", [P, 4, T], F16)
        OD = sb("OD", [P, G1, T])
        rq1 = sb("rq1", [P, G1, SUB, 4])
        On1 = sb("On1", [P, SUB, P])
        O1s = sb("O1s", [P, 2, T], F16)
        mx1 = sb("mx1", [P, SUB, H1])
        negm1 = sb("negm1", [H1, T], F16)
        Ht = sb("Ht", [P, 2, T])
        HS = sb("HS", [P, 2, C, T], F16)
        outb = sb("outb", [P, 2, D])
        mrow_u8 = sb("mrow_u8", [P, SK], U8)
        mcol_u8, mrem_u8, mval_u8 = (sb(n, [P, 1], U8) for n in ("mcol_u8", "mrem_u8", "mval_u8"))
        mcol, mrem = sb("mcol", [P, 1]), sb("mrem", [P, 1])
        quad, par, sel, valid = sb("quad", [P, 4]), sb("par", [P, 2]), sb("sel", [P, H1]), sb("valid", [P, 1])
        junk2 = sb("junk2", [P, D], F16)
        cntv, cntm, cntr = sb("cntv", [P, 1]), sb("cntm", [P, 1]), sb("cntr", [P, 1])
        ssc, msc, rsc = sb("ssc", [P, 2]), sb("msc", [P, 2]), sb("rsc", [P, 2])
        scl = sb("scl", [P, 2])
        csum, cnt, mean = sb("csum", [P, C]), sb("cnt", [P, 1]), sb("mean", [P, C])
        stage = [xin[:, :, :], ybuf[:, :, :], *(buf[:, :, :, :].bitcast(F32).rearrange("p a c t -> p (a c t)").rearrange(
            "p (c t) -> p c t", c=C) for buf in (XS, HS)), ybuf[:, :, :], Pr[:, 4:8, :]]
        stage_small = xres
        WKV = Qst[:, :, :].rearrange("p (w q c) n -> p w q c n", w=2, q=2)
        WKV1 = Q1st[:, :, :].rearrange("p (w q) (c n) -> p w q c n", w=2, c=C)
        crow = Pr
        cn = XT
        cT = OD[:, :, :].rearrange("p a b -> p (a b)")[:, 0:C * KA].rearrange("p (c k) -> p c k", c=C)
        ck32 = Ht[:, :, :].rearrange("p a b -> p (a b)")[:, 0:C * KA].rearrange("p (c k) -> p c k", c=C)
        inv = [outb[:, 0, 0:KA], outb[:, 1, 0:KA]]
        split = [buf[:, :, :, :].rearrange("p a c t -> p (a c t)") for buf in (AT, AO)]
        keys_in = [buf[:, 0:2 * C * KA].rearrange("p (a c k) -> p a c k", a=2, c=C) for buf in split]
        values_in = [buf[:, 2 * C * KA:4 * C * KA].rearrange("p (a c k) -> p a c k", a=2, c=C) for buf in split]
        KTs, KTs1 = Qs[:, :, :, 0:KA], Qs[:, :, :, KA:2 * KA]
        psum = [stack.enter_context(nc.psum_tensor(f"bank{i}", [P, T], F32)) for i in range(8)]
        ring_f, ring_a, ring_b, bank_o, bank_d = psum[0:2], psum[2:4], psum[4:6], psum[6], psum[7]
        image0 = nc.dram_tensor("image0", [B * P, IMG0 // 2], F32, kind="Internal").ap()
        image1 = nc.dram_tensor("image1", [B * P, IMG1 // 2], F32, kind="Internal").ap()

        const_ready, weights_in, vec_in = sem("const_ready"), sem("weights_in"), sem("vec_in")
        stage_in = [sem(f"stage_in{i}") for i in range(6)]
        weight_hi, weight_split, weight_g = sem("weight_hi"), sem("weight_split"), sem("weight_g")
        pre_zero = sem("pre_zero")
        pre_act, pre_pool, pre_pe, pre_dve = (sem(n) for n in ("pre_act", "pre_pool", "pre_pe", "pre_dve"))
        ctx_in, image_out, images_free = sem("ctx_in"), sem("image_out"), sem("images_free")
        pre_tmp, pre_tmp2, pre_kt = sem("pre_tmp"), sem("pre_tmp2"), sem("pre_kt")
        N_ZERO = 9 + 6 + 1 + 4 * G1 + 2
        pe_f, act_f, dve_f, pool_f = (sem(n) for n in ("pe_f", "act_f", "dve_f", "pool_f"))
        pe_a, act_a, dve_a, pool_a = (sem(n) for n in ("pe_a", "act_a", "dve_a", "pool_a"))
        pe_b, act_b, dve_b, pool_b = (sem(n) for n in ("pe_b", "act_b", "dve_b", "pool_b"))
        x_in, xres_in, blk0_in, kv0_in, kv1_in = (sem(n) for n in ("x_in", "xres_in", "blk0_in", "kv0_in", "kv1_in"))
        stack0_in, stack1_in, max0_in, max1_in = (sem(n) for n in ("stack0_in", "stack1_in", "max0_in", "max1_in"))
        out_done = [sem("out_done0"), sem("out_done1")]
        N_STACK = 12 * 16

        block = stack.enter_context(nc.Block())

        BIG = [(wk, gc_c, lambda q, c: WKV[:, 0, q, c, :]), (wv, gc_c, lambda q, c: WKV[:, 1, q, c, :]),
               (wq, gq_c, lambda q, c: WQ[:, q, c, :]), (wo, None, lambda q, c: WO[:, q, c, :]),
               (w1t, None, lambda q, c: W1[:, q, c, :]), (w2t, None, lambda q, c: W2[:, q, c, :])]
        SMALL = [(wk1, lambda q: WKV1[:, 0, q, :, :].rearrange("p c n -> p (c n)")),
                 (wv1, lambda q: WKV1[:, 1, q, :, :].rearrange("p c n -> p (c n)")),
                 (wq1, lambda q: WQ1[:, q, :, :].rearrange("p c n -> p (c n)")),
                 (wo1, lambda q: WO1[:, q, 0, :])]

        def stack_keys(copy, j):
            for piece, part in enumerate((0, 1, 0)):
                copy(Kst[32 * piece:32 * piece + 32, j::4, :], KTs[32 * j:32 * j + 32, part, :, :])
            return copy(Kblk[32 * j:32 * j + 32, :, j * SK:(j + 1) * SK], KTs[32 * j:32 * j + 32, 0, :, 0:SK])

        def started(e):
            e.wait_ge(image_out, 32 * B)
            e.wait_ge(weight_split, 4 * 3 + len(SMALL))

        def weights_done(e):
            e.wait_ge(weight_split, 4 * len(BIG) + len(SMALL))

        @block.sync
        def _(sp):
            for v, dst in ((gq, gq_c), (gc, gc_c), (b1, b1_c), (b2, b2_c)):
                sp.dma_start(dst[:, :], v).then_inc(vec_in, 16)
            sp.dma_start(gout_b[:, :], gout.rearrange("(a n) -> a n", a=1).to_broadcast([P, D])).then_inc(vec_in, 16)
            for i, (w, _) in enumerate(SMALL):
                src = w.rearrange("(c p) n -> p c n", p=P)
                dst = stage_small[:, i, :].rearrange("p (c n) -> p c n", c=src.shape[1])
                sp.dma_start(dst, src).then_inc(weights_in, 16)

            def load_weight(i):
                sp.dma_start(stage[i], BIG[i][0].rearrange("(c p) n -> p c n", p=P)).then_inc(stage_in[i], 16)

            load_weight(0)
            load_weight(1)
            sp.wait_ge(pre_zero, N_ZERO)

            def value(v):
                return v if isinstance(v, int) else sp.to_reg(v)

            def load_context(b):
                sp.dma_start(crow[:, 0, :], ctxt[bass.ds(b * SK, KM), :]).then_inc(ctx_in, 16)
                sp.dma_start(crow[0:KR, 1, :], ctxt[bass.ds(b * SK + KM, KR), :]).then_inc(ctx_in, 16)
                sp.dma_start(mcol_u8[:, :], mask_col[bass.ds(b * SK, KM), :]).then_inc(ctx_in, 16)
                for j in range(4):
                    sp.dma_start(mrem_u8[32 * j:32 * j + KR, :],
                                 mask_col[bass.ds(b * SK + KM, KR), :]).then_inc(ctx_in, 16)

                sp.dma_start(mrow_u8[:, :], mask[bass.ds(b, 1), :].to_broadcast([P, SK])).then_inc(ctx_in, 16)

            def load_values_mask(b):
                sp.dma_start(mval_u8[:, :], mask_col[bass.ds(b * SK, KM), :]).then_inc(images_free, 16)

            def store_images(b):
                stacked, values = value(PRE_ACT.upto(b, "kst0")), value(PRE_DVE.upto(b, "vr0"))
                sp.wait_ge(pre_act, stacked)
                sp.wait_ge(pre_dve, values)
                sp.dma_start(image0[bass.ds(b * P, P), :], img0[:, :].bitcast(F32)).then_inc(image_out, 16)
                sp.wait_ge(pre_dve, PRE_DVE.upto(b, "vr1"))
                sp.dma_start(image1[bass.ds(b * P, P), :], img1[:, :].bitcast(F32)).then_inc(image_out, 16)

            load_context(0)
            load_values_mask(0)
            for i in (2, 3, 5):
                load_weight(i)
            sp.wait_ge(weight_split, 4 * 2 + len(SMALL))
            load_weight(4)
            with sp.Fori(0, B - 1) as b:
                sp.wait_ge(pre_pe, PRE_PE.upto(b, "tb1"))
                load_context(b + 1)
                store_images(b)
                sp.wait_ge(image_out, 32 * b + 32)
                load_values_mask(b + 1)
            store_images(B - 1)
            started(sp)

            def load_image1(b_):
                if not static_first(b_):
                    sp.wait_ge(pe_b, PE_B.upto(b_ - 1, "v1"))
                sp.dma_start(img1[:, :].bitcast(F32), image1[bass.ds(batch_of(b_) * P, P), :]).then_inc(kv1_in, 16)

            def load_blocks0(f):
                if not static_first(f):
                    sp.wait_ge(pe_f, PE_F.upto(f - 1, "m31"))
                sp.dma_start(img0[:, 0:K0_BLK].bitcast(F32),
                             image0[bass.ds(batch_of(f) * P, P), 0:K0_BLK // 2]).then_inc(blk0_in, 16)

            def load_image0(a):
                if not static_first(a):
                    sp.wait_ge(pe_a, PE_A.upto(a - 1, "v3"))
                sp.dma_start(img0[:, K0_BLK:].bitcast(F32),
                             image0[bass.ds(batch_of(a) * P, P), K0_BLK // 2:]).then_inc(kv0_in, 16)

            def stack1(b_):
                lo, hi = value(DVE_B.upto(b_, "ql")), value(ACT_B.upto(b_, "qh"))
                if not static_first(b_):
                    used = value(PE_B.upto(b_ - 1, "r1"))
                    sp.wait_ge(pe_b, used)
                sp.wait_ge(dve_b, lo)
                sp.wait_ge(act_b, hi)
                for piece, part in enumerate((0, 0, 1)):
                    for j in range(4):
                        sp.dma_start(Q1st[32 * piece:32 * piece + 32, j, :],
                                     Q1s[32 * j:32 * j + 32, part, :]).then_inc(stack1_in, 16)

            def stack0(f):
                hi, lo = value(ACT_F.upto(f, "qh3")), value(DVE_F.upto(f, "ql3"))
                if not static_first(f):
                    used = value(PE_A.upto(f - 1, "r3"))
                    sp.wait_ge(pe_a, used)
                sp.wait_ge(act_f, hi)
                sp.wait_ge(dve_f, lo)
                for piece, part in enumerate((0, 0, 1)):
                    for j in range(4):
                        sp.dma_start(Qst[32 * piece:32 * piece + 32, j::4, :],
                                     Qs[32 * j:32 * j + 32, part, :, :]).then_inc(stack0_in, 16)

            def stack_max1(b_):
                sp.wait_ge(act_b, ACT_B.upto(b_, "negm"))
                sp.dma_start(Q1st[96:98, :, :], negm1[:, :]).then_inc(max1_in, 16)

            def stack_max0(f):
                sp.wait_ge(act_f, ACT_F.upto(f, "negm"))
                sp.dma_start(Qst[96:97, :, :], negm[:, :]).then_inc(max0_in, 16)

            def store(b_, s):
                sp.wait_ge(act_b, ACT_B.upto(b_, f"t{s}"))
                sp.dma_start(out[bass.ds(b_ * T + s * P, P), :], outb[:, s % 2, :]).then_inc(out_done[s % 2], 16)

            def keep_x(f):
                arrived = value(16 * f + 16)
                if not static_first(f):
                    read = value(DVE_A.upto(f - 1, "y3"))
                    sp.wait_ge(dve_a, read)
                sp.wait_ge(x_in, arrived)
                sp.dma_start(xres[:, :, :], xin[:, :, :]).then_inc(xres_in, 16)

            def load_x(t, read_by=None):
                if read_by is not None:
                    copied, squared, normed = (value(v) for v in (
                        16 * read_by + 16, ACT_F.upto(read_by, "sq3"), DVE_F.upto(read_by, "xn3")))
                    sp.wait_ge(xres_in, copied)
                    sp.wait_ge(act_f, squared)
                    sp.wait_ge(dve_f, normed)
                sp.dma_start(xin[:, :, :], x[bass.ds(t * T, T), :].rearrange("(s p) d -> p s d", p=P)).then_inc(x_in, 16)

            def step(f, a, b_, x_next, new=()):
                if "b" in new:
                    load_image1(b_)
                if "a" in new:
                    load_image0(a)
                if b_ is not None:
                    stack1(b_)
                if "f" in new:
                    load_blocks0(f)
                if b_ is not None:
                    stack_max1(b_)
                if f is not None:
                    keep_x(f)
                if x_next is not None:
                    load_x(x_next, read_by=f)
                if f is not None:
                    stack0(f)
                if b_ is not None:
                    for n in range(3):
                        store(b_, n)
                if f is not None:
                    stack_max0(f)
                if b_ is not None:
                    store(b_, 3)

            load_x(0)
            step(0, None, None, 1, "f")
            step(1, 0, None, 2, "a")
            step(2, 1, 0, 3, "b")
            with sp.Fori(0, (NT - 4) // TPB) as k:
                for n in range(TPB):
                    i = TPB * k + (n + 1)
                    new = [name for name, ahead in (("f", 2), ("a", 1), ("b", 0)) if (n + 1 + ahead) % TPB == 0]
                    step(i + 2, i + 1, i, i + 3, new)
            step(NT - 1, NT - 2, NT - 3, None)
            step(None, NT - 1, NT - 2, None)
            step(None, None, NT - 1, None)
            for k in range(2):
                sp.wait_ge(out_done[k], 2 * 16 * NT)

        @block.gpsimd
        def _(pool):
            pool.memset(ident[:, :], 0.0).then_inc(const_ready, 1)
            pool.memset(quad[:, :], 0.0).then_inc(const_ready, 1)
            pool.memset(par[:, :], 0.0).then_inc(const_ready, 1)
            pool.memset(sel[:, :], 0.0).then_inc(const_ready, 1)
            pool.memset(mhalf[:, :], -0.5).then_inc(const_ready, 1)
            pool.memset(one[:, :], 1.0).then_inc(const_ready, 1)
            pool.memset(K1st, 0.0).then_inc(const_ready, 1)
            pool.wait_ge(const_ready, 7)
            pool.affine_select(out=ident[:, :], in_=ident[:, :], compare_op=ALU.not_equal, fill=1.0, base=0,
                               pattern=[[-1, P]], channel_multiplier=1).then_inc(const_ready, 1)
            pool.affine_select(out=sel[:, :], in_=sel[:, :], compare_op=ALU.is_gt, fill=1.0, base=0,
                               pattern=[[D1, H1]], channel_multiplier=-1).then_inc(const_ready, 1)
            pool.affine_select(out=quad[:, :], in_=quad[:, :], compare_op=ALU.is_gt, fill=1.0, base=0,
                               pattern=[[32, 4]], channel_multiplier=-1).then_inc(const_ready, 1)
            pool.wait_ge(const_ready, 10)
            pool.affine_select(out=sel[:, :], in_=sel[:, :], compare_op=ALU.is_gt, fill=0.0, base=D1,
                               pattern=[[D1, H1]], channel_multiplier=-1).then_inc(const_ready, 1)
            pool.affine_select(out=quad[:, :], in_=quad[:, :], compare_op=ALU.is_gt, fill=0.0, base=32,
                               pattern=[[32, 4]], channel_multiplier=-1).then_inc(const_ready, 1)
            pool.wait_ge(const_ready, 12)
            with pool.Fori(0, B) as b:
                pool.wait_ge(pre_dve, PRE_DVE.upto(b, "ms"))
                pool.tensor_tensor(rsc[:, :], msc[:, :], mhalf[:, 0:2], ALU.pow).then_inc(pre_pool, 1)
            started(pool)

            def norm_x(f):
                pool.wait_ge(dve_f, DVE_F.upto(f, "ms"))
                pool.tensor_tensor(r1[:, :], ms[:, :], mhalf[:, :], ALU.pow).then_inc(pool_f, 1)

            def spread(a, m):
                if m == 0:
                    pool.wait_ge(dve_a, DVE_A.upto(a, "rc"))
                if m >= 2:
                    pool.wait_ge(pe_a, PE_A.upto(a, f"rb{m - 2}"))
                pool.tensor_tensor(xn[:, m % 2, :].rearrange("p (s j r) -> p s j r", s=SUB, j=4),
                                   rq[:, :, 4 * m:4 * m + 4].unsqueeze(3).to_broadcast([P, SUB, 4, D0]),
                                   one[:, :].unsqueeze(2).unsqueeze(3).to_broadcast([P, SUB, 4, D0]),
                                   ALU.mult).then_inc(pool_a, 1)

            def norm_y(a, s):
                pool.wait_ge(dve_a, DVE_A.upto(a, f"ms{s}"))
                pool.tensor_tensor(ry[:, s:s + 1], msy[:, s:s + 1], mhalf[:, 0:1], ALU.pow).then_inc(pool_a, 1)

            def add_b2(b_, m):
                pool.wait_ge(dve_b, DVE_B.upto(b_, f"xl{m}"))
                pool.tensor_tensor(XT[:, m, :], XT[:, m, :], b2_c[:, m:m + 1].to_broadcast([P, T]), ALU.add).then_inc(pool_b, 1)

            def step(f, a, b_):
                if a is not None:
                    for n in range(4):
                        spread(a, n)
                if f is not None:
                    norm_x(f)
                if a is not None:
                    for n in range(2):
                        norm_y(a, n)
                if b_ is not None:
                    for n in range(3):
                        add_b2(b_, n)
                if a is not None:
                    norm_y(a, 2)
                if b_ is not None:
                    add_b2(b_, 3)
                if a is not None:
                    norm_y(a, 3)

            step(0, None, None)
            step(1, 0, None)
            step(2, 1, 0)
            with pool.Fori(1, NT - 2) as i:
                step(i + 2, i + 1, i)
            step(None, NT - 1, NT - 2)
            step(None, None, NT - 1)

        @block.scalar
        def _(act):
            act.wait_ge(weights_in, 16 * len(SMALL))
            for i, (_, dst) in enumerate(SMALL):
                act.activation(dst(0), stage_small[:, i, :], ACT.Copy, scale=WS).then_inc(weight_hi, 1)
            act.wait_ge(weight_g, 2)

            def weight_hi_part(i):
                _, g, dst = BIG[i]
                act.wait_ge(stage_in[i], 16)
                for c in range(C):
                    act.activation(dst(0, c), stage[i][:, c, :], ACT.Copy,
                                   scale=WS if g is None else g[:, c:c + 1]).then_inc(weight_hi, 1)

            weight_hi_part(0)
            weight_hi_part(1)
            act.wait_ge(pre_zero, N_ZERO)
            with act.Fori(0, B) as b:
                act.wait_ge(ctx_in, 128 * b + 128)
                act.activation(junk[:, :], crow[:, 0, :], ACT.Square, accum_out=ssc[:, 0:1]).then_inc(pre_act, 1)
                act.activation(junk2[0:KP, :], crow[0:KP, 1, :], ACT.Square, accum_out=ssc[0:KP, 1:2]).then_inc(pre_act, 1)
                act.wait_ge(images_free, 16 * b + 16)
                act.wait_ge(pre_dve, PRE_DVE.upto(b, "k0_3"))
                for j in range(2, 4):
                    ins = stack_keys(act.copy, j)
                ins.then_inc(pre_act, 1)
            weight_hi_part(2)
            started(act)

            def norm_x(f, s):
                if s == 0:
                    act.wait_ge(x_in, 16 * f + 16)
                if s >= 2:
                    act.wait_ge(act_f, ACT_F.upto(f, f"sq{s - 2}"))
                act.activation(junk[:, :] if s % 2 else junk2[:, :], xin[:, s, :], ACT.Square,
                               accum_out=ss[:, s:s + 1]).then_inc(act_f, 1)

            def x_hi(f, s):
                if s == 0 and not static_first(f):
                    act.wait_ge(pe_f, PE_F.upto(f - 1, "q3"))
                act.wait_ge(pe_f, PE_F.upto(f, f"xt{s}"))
                act.activation(AT[:, 0, :, s * P:(s + 1) * P], ring_f[bank_f(f"xt{s}")][:, :].rearrange(
                    "p (c q) -> p c q", c=C), ACT.Copy).then_inc(act_f, 1)

            def q_hi(f, m):
                act.wait_ge(pe_f, PE_F.upto(f, f"q{m}"))
                if m == 0 and not static_first(f):
                    act.wait_ge(stack0_in, N_STACK * f)
                act.activation(Qs[:, 0, m, :], ring_f[bank_f(f"q{m}")][:, :], ACT.Copy,
                               scale=QS0).then_inc(act_f, 1)

            def neg_max(f):
                act.wait_ge(pe_f, PE_F.upto(f, "mt"))
                if not static_first(f):
                    act.wait_ge(max0_in, 16 * f)
                act.activation(negm[:, :], ring_f[bank_f("mt")][0:H0, :], ACT.Copy, scale=-1.0).then_inc(act_f, 1)

            def exps(a, g, j):
                unit = f"s{g}{j}" if j < 4 else f"r{g}"
                if g < 2 and j == 4 and not early(a):
                    act.wait_ge(pe_b, PE_B.upto(a - 2, f"v{g}"))
                act.wait_ge(pe_a, PE_A.upto(a, unit))
                act.activation(Pr[:, 5 * (g % 2) + j, :], ring_a[bank_a(unit)][:, :], ACT.Exp).then_inc(act_a, 1)

            def den(a):
                act.wait_ge(pe_a, PE_A.upto(a, "v3"))
                act.activation(Dsb[:, :], bank_d[:, :], ACT.Copy).then_inc(act_a, 1)

            def o_hi(a, m):
                if m == 0 and not static_first(a):
                    act.wait_ge(pe_a, PE_A.upto(a - 1, "y3"))
                act.wait_ge(dve_a, DVE_A.upto(a, f"on{m}"))
                act.activation(AO[:, 0, m, :], Ou[:, m, :], ACT.Copy).then_inc(act_a, 1)

            def y_sq(a, s):
                act.wait_ge(dve_a, DVE_A.upto(a, f"y{s}"))
                if s >= 2:
                    act.wait_ge(act_a, ACT_A.upto(a, f"sqy{s - 2}"))
                act.activation(junk_y[:, s % 2, :], ybuf[:, s, :], ACT.Square,
                               accum_out=ssy[:, s:s + 1]).then_inc(act_a, 1)

            def x2_evac(a, s):
                if not static_first(a):
                    act.wait_ge(pe_b, PE_B.upto(a - 1, f"t{s}"))
                act.wait_ge(pe_a, PE_A.upto(a, f"x2t{s}"))
                src = ring_a[bank_a(f"x2t{s}")][:, :].rearrange("p (c q) -> p c q", c=C)
                act.activation(XT[:, :, s * P:(s + 1) * P], src, ACT.Copy).then_inc(act_a, 1)
                act.activation(XS[:, 0, :, s * P:(s + 1) * P], src, ACT.Copy).then_inc(act_a, 1)

            def q1_hi(b_):
                act.wait_ge(pe_b, PE_B.upto(b_, "q"))
                if not static_first(b_):
                    act.wait_ge(stack1_in, N_STACK * b_)
                act.activation(Q1s[:, 0, :], ring_b[bank_b("q")][:, :], ACT.Copy, scale=QS1).then_inc(act_b, 1)

            def neg_max1(b_):
                act.wait_ge(pe_b, PE_B.upto(b_, "mt"))
                if not static_first(b_):
                    act.wait_ge(max1_in, 16 * b_)
                act.activation(negm1[:, :], ring_b[bank_b("mt")][0:H1, :], ACT.Copy, scale=-1.0).then_inc(act_b, 1)

            def exps1(b_, g, j):
                unit = f"s{g}{j}" if j < 4 else f"r{g}"
                if j == 4 and not static_last(b_):
                    act.wait_ge(pe_a, PE_A.upto(b_ + 1, f"v{g + 2}"))
                act.wait_ge(pe_b, PE_B.upto(b_, unit))
                act.activation(Pr[:, 5 * g + j, :], ring_b[bank_b(unit)][:, :], ACT.Exp).then_inc(act_b, 1)

            def od(b_, g):
                act.wait_ge(pe_b, PE_B.upto(b_, f"v{g}"))
                act.activation(OD[:, g, :], bank_o[:, :], ACT.Copy).then_inc(act_b, 1)

            def o1_hi(b_):
                act.wait_ge(pe_b, PE_B.upto(b_, "ot"))
                act.activation(O1s[:, 0, :], ring_b[bank_b("ot")][:, :], ACT.Copy).then_inc(act_b, 1)

            def x_split(b_, m):
                act.wait_ge(dve_b, DVE_B.upto(b_, f"xo{m}"))
                act.activation(XS[:, 0, m, :], XT[:, m, :], ACT.Copy).then_inc(act_b, 1)

            def hidden(b_, f):
                act.wait_ge(pe_b, PE_B.upto(b_, f"h{f}"))
                if f >= 2:
                    act.wait_ge(dve_b, DVE_B.upto(b_, f"hl{f - 2}"))
                act.activation(Ht[:, f % 2, :], ring_b[bank_b(f"h{f}")][:, :], ACT.Relu, bias=b1_c[:, f:f + 1],
                               scale=1.0 / WS).then_inc(act_b, 1)

            def out_copy(b_, s):
                act.wait_ge(pe_b, PE_B.upto(b_, f"t{s}"))
                if s >= 2 or not static_first(b_):
                    act.wait_ge(out_done[s % 2], 16 * (2 * b_ + s // 2))
                act.activation(outb[:, s % 2, :], ring_b[bank_b(f"t{s}")][:, :], ACT.Copy).then_inc(act_b, 1)

            def step(f, a, b_):
                if f is not None:
                    for n in range(3):
                        norm_x(f, n)
                if a is not None:
                    exps(a, 0, 4)
                    for n in range(3):
                        exps(a, 0, n)
                if b_ is not None:
                    q1_hi(b_)
                if a is not None:
                    exps(a, 0, 3)
                    exps(a, 1, 4)
                    for n in range(3):
                        exps(a, 1, n)
                if f is not None:
                    norm_x(f, 3)
                if a is not None:
                    exps(a, 1, 3)
                    exps(a, 2, 4)
                    for n in range(4):
                        exps(a, 2, n)
                    exps(a, 3, 4)
                    for n in range(4):
                        exps(a, 3, n)
                if b_ is not None:
                    neg_max1(b_)
                if a is not None:
                    den(a)
                if b_ is not None:
                    exps1(b_, 0, 4)
                    for n in range(4):
                        exps1(b_, 0, n)
                    od(b_, 0)
                    exps1(b_, 1, 4)
                    for n in range(2):
                        exps1(b_, 1, n)
                if a is not None:
                    o_hi(a, 0)
                if b_ is not None:
                    for n in range(2, 4):
                        exps1(b_, 1, n)
                if a is not None:
                    o_hi(a, 1)
                if f is not None:
                    x_hi(f, 0)
                if a is not None:
                    o_hi(a, 2)
                if b_ is not None:
                    od(b_, 1)
                if a is not None:
                    o_hi(a, 3)
                if f is not None:
                    x_hi(f, 1)
                if b_ is not None:
                    o1_hi(b_)
                if f is not None:
                    for n in range(2, 4):
                        x_hi(f, n)
                if a is not None:
                    y_sq(a, 0)
                if b_ is not None:
                    x_split(b_, 0)
                if f is not None:
                    q_hi(f, 0)
                if b_ is not None:
                    for n in range(1, 3):
                        x_split(b_, n)
                if f is not None:
                    q_hi(f, 1)
                if b_ is not None:
                    x_split(b_, 3)
                    hidden(b_, 0)
                if f is not None:
                    q_hi(f, 2)
                if b_ is not None:
                    for n in range(1, 3):
                        hidden(b_, n)
                if a is not None:
                    y_sq(a, 1)
                if b_ is not None:
                    hidden(b_, 3)
                if a is not None:
                    y_sq(a, 2)
                if f is not None:
                    q_hi(f, 3)
                if a is not None:
                    y_sq(a, 3)
                    x2_evac(a, 0)
                if b_ is not None:
                    out_copy(b_, 0)
                if a is not None:
                    x2_evac(a, 1)
                if b_ is not None:
                    out_copy(b_, 1)
                if a is not None:
                    x2_evac(a, 2)
                if b_ is not None:
                    out_copy(b_, 2)
                if a is not None:
                    x2_evac(a, 3)
                if b_ is not None:
                    out_copy(b_, 3)
                if f is not None:
                    neg_max(f)

            step(0, None, None)
            for i in range(3, len(BIG)):
                weight_hi_part(i)
            weights_done(act)
            step(1, 0, None)
            step(2, 1, 0)
            with act.Fori(1, NT - 2) as i:
                step(i + 2, i + 1, i)
            step(None, NT - 1, NT - 2)
            step(None, None, NT - 1)

        @block.vector
        def _(dve):
            zeroed = [(img0[:, :].bitcast(F32), 0.0), (img1[:, K1_ST:].bitcast(F32), 0.0), (crow[:, 1, :], 0.0),
                      (cn[:, 1, :], 0.0), (mrem_u8[:, :], 0), (inv[0], 1.0), (inv[1], 0.0), (ssc[:, :], 1.0),
                      (valid[:, :], 0.0)]
            for ap, v in zeroed:
                dve.memset(ap, v).then_inc(pre_zero, 1)
            dve.wait_ge(pre_zero, len(zeroed))
            later = [(Kst[96:97, :, :], 1.0), (inv[1][:, SK:KA], 1.0)] \
                + [(valid[32 * j:32 * j + KR, :], 1.0) for j in range(4)]
            for ap, v in later:
                dve.memset(ap, v).then_inc(pre_zero, 1)
            dve.wait_ge(pre_zero, len(zeroed) + len(later))
            dve.memset(V1[:, :, D1:2 * D1], 1.0).then_inc(pre_zero, 1)
            for g in range(G1):
                for j in range(4):
                    dve.tensor_copy(V1r[32 * j:32 * j + 32, g, 32 * j + D1:32 * j + 2 * D1],
                                    valid[32 * j:32 * j + 32, :].to_broadcast([32, D1])).then_inc(pre_zero, 1)
            dve.wait_ge(const_ready, 12)
            dve.tensor_copy(K1st[96:98, :, :].rearrange("p (j a) k -> p j a k", a=2),
                            ident[96:98, 96:98].unsqueeze(1).unsqueeze(3).to_broadcast([2, 4, 2, KA])).then_inc(pre_zero, 1)
            dve.tensor_reduce(par[:, :], sel[:, :].rearrange("p (j a) -> p a j", a=2), AX.X, ALU.add).then_inc(pre_zero, 1)

            dve.wait_ge(vec_in, 16 * 5)
            for g in (gq_c, gc_c):
                dve.tensor_scalar(g[:, :], g[:, :], WS, None, ALU.mult).then_inc(weight_g, 1)
            dve.wait_ge(weight_g, 2)
            for i, (_, dst) in enumerate(SMALL):
                dve.wait_ge(weight_hi, i + 1)
                dve.scalar_tensor_tensor(dst(1), stage_small[:, i, :], WS, dst(0), ALU.mult, ALU.subtract).then_inc(weight_split, 1)

            def weight_lo_part(i):
                _, g, dst = BIG[i]
                for c in range(C):
                    dve.wait_ge(weight_hi, len(SMALL) + 4 * i + c + 1)
                    dve.scalar_tensor_tensor(dst(1, c), stage[i][:, c, :], WS if g is None else g[:, c:c + 1],
                                             dst(0, c), ALU.mult, ALU.subtract).then_inc(weight_split, 1)

            weight_lo_part(0)
            weight_lo_part(1)
            with dve.Fori(0, B) as b:
                def done(name):
                    dve.wait_ge(pre_dve, PRE_DVE.upto(b, name))

                dve.wait_ge(ctx_in, 128 * b + 128)
                dve.tensor_copy(mcol[:, :], mcol_u8[:, :])
                dve.tensor_copy(mrem[:, :], mrem_u8[:, :])
                dve.tensor_scalar(inv[0][:, 0:SK], mrow_u8[:, :], -1.0, 1.0, ALU.mult, ALU.add).then_inc(pre_dve, 1)
                dve.wait_ge(pre_act, PRE_ACT.upto(b, "sqr"))
                dve.tensor_scalar(msc[:, :], ssc[:, :], 1.0 / D, EPS, ALU.mult, ALU.add).then_inc(pre_dve, 1)
                dve.wait_ge(pre_pool, PRE_POOL.upto(b, "r"))
                dve.tensor_tensor(scl[:, 0:1], rsc[:, 0:1], mcol[:, :], ALU.mult)
                dve.tensor_tensor(scl[:, 1:2], rsc[:, 1:2], mrem[:, :], ALU.mult).then_inc(pre_dve, 1)
                done("sc0")
                dve.tensor_scalar(cn[:, 0, :], crow[:, 0, :], scl[:, 0:1], None, ALU.mult)
                dve.tensor_scalar(cn[0:KP, 1, :], crow[0:KP, 1, :], scl[0:KP, 1:2], None, ALU.mult).then_inc(pre_dve, 1)
                for layer in range(2):
                    L = str(layer)
                    cks, cvs = keys_in[layer], values_in[layer]
                    if layer == 1:
                        done("cks0")
                    dve.wait_ge(pre_pe, PRE_PE.upto(b, "tb" + L))
                    dve.tensor_copy(cT[:, :, 0:KM], psum[0][:, :].rearrange("p (c k) -> p c k", c=C))
                    dve.tensor_copy(cT[:, :, KM:KA], psum[1][:, 0:C * KP].rearrange("p (c k) -> p c k", c=C)).then_inc(pre_dve, 1)
                    done("ct" + L)
                    dve.tensor_reduce(csum[:, :], cT, AX.X, ALU.add)
                    dve.tensor_reduce(cnt[:, :], inv[layer][:, 0:SK], AX.X, ALU.add).then_inc(pre_dve, 1)
                    done("sum" + L)
                    dve.tensor_scalar(cntv[:, :], cnt[:, :], -1.0, float(SK), ALU.mult, ALU.add).then_inc(pre_tmp, 1)
                    dve.wait_ge(pre_tmp, 6 * b + 3 * layer + 1)
                    dve.tensor_scalar(cntm[:, :], cntv[:, :], 1.0, None, ALU.max).then_inc(pre_tmp, 1)
                    dve.wait_ge(pre_tmp, 6 * b + 3 * layer + 2)
                    dve.reciprocal(cntr[:, :], cntm[:, :]).then_inc(pre_tmp, 1)
                    dve.wait_ge(pre_tmp, 6 * b + 3 * layer + 3)
                    dve.tensor_scalar(mean[:, :], csum[:, :], cntr[:, :], None, ALU.mult).then_inc(pre_dve, 1)
                    done("mean" + L)
                    for c in range(C):
                        ins = dve.scalar_tensor_tensor(ck32[:, c, :], inv[layer], mean[:, c:c + 1], cT[:, c, :],
                                                       ALU.mult, ALU.add)
                    dve.tensor_copy(cvs[:, 0, :, :], cT).then_inc(pre_dve, 1)
                    done("ck" + L)
                    dve.tensor_copy(cks[:, 0, :, :], ck32)
                    dve.tensor_tensor(cvs[:, 1, :, :], cT, cvs[:, 0, :, :], ALU.subtract).then_inc(pre_tmp2, 1)
                    dve.wait_ge(pre_tmp2, 2 * b + layer + 1)
                    dve.tensor_tensor(cks[:, 1, :, :], ck32, cks[:, 0, :, :], ALU.subtract).then_inc(pre_dve, 1)
                for layer in range(2):
                    if layer == 0:
                        for m in range(G0):
                            dve.wait_ge(pre_pe, PRE_PE.upto(b, f"k{m}"))
                            dve.tensor_scalar(KTs[:, 0, m, :], psum[2 + m][:, 0:KA], 1.0 / WS, None, ALU.mult).then_inc(pre_kt, 1)
                            dve.wait_ge(pre_kt, 5 * b + m + 1)
                            dve.scalar_tensor_tensor(KTs[:, 1, m, :], psum[2 + m][:, 0:KA], 1.0 / WS, KTs[:, 0, m, :],
                                                     ALU.mult, ALU.subtract).then_inc(pre_dve, 1)
                        done("k0_3")
                        dve.wait_ge(images_free, 16 * b + 16)
                        for j in range(2):
                            ins = stack_keys(dve.tensor_copy, j)
                        ins.then_inc(pre_dve, 1)
                        dve.wait_ge(pre_pe, PRE_PE.upto(b, "v0"))
                        dve.tensor_copy(E0[:, 0:3 * 33 + 1:33], mval_u8[:, :].to_broadcast([P, 4]))
                        dve.tensor_scalar(E0r[:, 4:8], quad[:, :], mrem[:, :], None, ALU.mult)
                        dve.tensor_scalar(V0, psum[6][:, :], 1.0 / WS, None, ALU.mult).then_inc(pre_dve, 1)
                        dve.wait_ge(pre_pe, PRE_PE.upto(b, "vr0"))
                        for j in range(4):
                            q = slice(32 * j, 32 * j + 32)
                            ins = dve.tensor_scalar(V0r[q, :, 32 * j:32 * j + 32], psum[7][q, 0:G0 * D0].rearrange(
                                "p (m d) -> p m d", m=G0), 1.0 / WS, None, ALU.mult)
                        ins.then_inc(pre_dve, 1)
                    else:
                        dve.wait_ge(pre_pe, PRE_PE.upto(b, "kk"))
                        dve.tensor_scalar(KTs1[:, 0, 0, :], psum[2][:, 0:KA], 1.0 / WS, None, ALU.mult).then_inc(pre_kt, 1)
                        dve.wait_ge(pre_kt, 5 * b + 5)
                        dve.scalar_tensor_tensor(KTs1[:, 1, 0, :], psum[2][:, 0:KA], 1.0 / WS, KTs1[:, 0, 0, :],
                                                 ALU.mult, ALU.subtract).then_inc(pre_dve, 1)
                        done("kk")
                        for a in range(2):
                            ins = dve.tensor_scalar(KTs1[:, :, 1 + a, :], KTs1[:, :, 0, :], par[:, a:a + 1], None, ALU.mult)
                        ins.then_inc(pre_dve, 1)
                        done("km")
                        for j in range(4):
                            for piece, part in enumerate((0, 1, 0)):
                                dve.tensor_copy(K1st[32 * piece:32 * piece + 32, 2 * j:2 * j + 2, :],
                                                KTs1[32 * j:32 * j + 32, part, 1:3, :])
                        for h in range(H1):
                            ins = dve.tensor_scalar(K1blk[:, h * SK:(h + 1) * SK], KTs1[:, 0, 0, 0:SK], sel[:, h:h + 1],
                                                    None, ALU.mult)
                        ins.then_inc(pre_dve, 1)
                        dve.wait_ge(pre_pe, PRE_PE.upto(b, "v1"))
                        dve.tensor_scalar(V1[:, :, 0:D1], psum[6][:, 0:H1 * D1].rearrange("p (h d) -> p h d", h=H1),
                                          1.0 / WS, None, ALU.mult).then_inc(pre_dve, 1)
                        dve.wait_ge(pre_pe, PRE_PE.upto(b, "vr1"))
                        for j in range(4):
                            q = slice(32 * j, 32 * j + 32)
                            ins = dve.tensor_scalar(V1r[q, :, 32 * j:32 * j + D1], psum[7][q, 0:G1 * D1].rearrange(
                                "p (g d) -> p g d", g=G1), 1.0 / WS, None, ALU.mult)
                        ins.then_inc(pre_dve, 1)
            weight_lo_part(2)
            started(dve)

            def norm_x(f, s):
                if s == 0:
                    dve.wait_ge(act_f, ACT_F.upto(f, "sq3"))
                    dve.tensor_scalar(ms[:, :], ss[:, :], 1.0 / D, EPS, ALU.mult, ALU.add).then_inc(dve_f, 1)
                    dve.wait_ge(pool_f, POOL_F.upto(f, "r"))
                    if not static_first(f):
                        dve.wait_ge(pe_a, PE_A.upto(f - 1, "rb3"))
                if s >= 2:
                    dve.wait_ge(pe_f, PE_F.upto(f, f"xt{s - 2}"))
                dve.tensor_scalar(xn[:, s % 2, :], xin[:, s, :], r1[:, s:s + 1], None, ALU.mult).then_inc(dve_f, 1)

            def x_lo(f, s):
                dve.wait_ge(act_f, ACT_F.upto(f, f"xh{s}"))
                q = slice(s * P, (s + 1) * P)
                dve.tensor_tensor(AT[:, 1, :, q], ring_f[bank_f(f"xt{s}")][:, :].rearrange("p (c q) -> p c q", c=C),
                                  AT[:, 0, :, q], ALU.subtract).then_inc(dve_f, 1)

            def q_lo(f, m):
                dve.wait_ge(act_f, ACT_F.upto(f, f"qh{m}"))
                if m == 0 and not static_first(f):
                    dve.wait_ge(stack0_in, N_STACK * f)
                dve.scalar_tensor_tensor(Qs[:, 1, m, :], ring_f[bank_f(f"q{m}")][:, :], QS0, Qs[:, 0, m, :],
                                         ALU.mult, ALU.subtract).then_inc(dve_f, 1)

            def maxima(f, n):
                m, s, half = n // 8, n % 8 // 2, n % 2
                dve.wait_ge(pe_f, PE_F.upto(f, f"m{n}"))
                dve.tensor_reduce(mx[:, s, 4 * m + 2 * half:4 * m + 2 * half + 2],
                                  ring_f[bank_f(f"m{n}")][:, 0:UNIT].rearrange("p (h k) -> p h k", h=2),
                                  AX.X, ALU.max).then_inc(dve_f, 1)

            def o_evac(a, m):
                if m == 0 and not static_first(a):
                    dve.wait_ge(pe_a, PE_A.upto(a - 1, "x2t3"))
                dve.wait_ge(pe_a, PE_A.upto(a, f"w{m}"))
                dve.tensor_copy(Ou[:, m, :], bank_o[:, :]).then_inc(dve_a, 1)

            def den(a):
                dve.wait_ge(pe_a, PE_A.upto(a, "dt"))
                src = ring_a[bank_a("dt")][:, :].rearrange("p (s r) -> p s r", s=SUB)
                main = src.rearrange("p s (j m) -> p s m j", j=4)[:, :, 0:4, :]
                rest = src.rearrange("p s (m j) -> p s m j", m=4)[:, :, :, 4:8]
                dst = dq[:, :, :].rearrange("p s (m j) -> p s m j", m=4)
                dve.tensor_copy(dst, main).then_inc(dve_a, 1)
                dve.wait_ge(dve_a, DVE_A.upto(a, "dm"))
                dve.tensor_tensor(rq[:, :, :].rearrange("p s (m j) -> p s m j", m=4), rest, dst, ALU.add).then_inc(dve_a, 1)
                dve.wait_ge(dve_a, DVE_A.upto(a, "dd"))
                dve.tensor_scalar(dq[:, :, :], rq[:, :, :], 1e-30, None, ALU.max).then_inc(dve_a, 1)
                dve.wait_ge(dve_a, DVE_A.upto(a, "dg"))
                dve.reciprocal(rq[:, :, :], dq[:, :, :]).then_inc(dve_a, 1)

            def o_norm(a, m):
                dve.wait_ge(pe_a, PE_A.upto(a, f"rb{m}"))
                if m == 0:
                    dve.wait_ge(dve_a, DVE_A.upto(a, "o3"))
                dve.tensor_tensor(Ou[:, m, :], ring_a[bank_a(f"rb{m}")][:, :], Ou[:, m, :], ALU.mult).then_inc(dve_a, 1)

            def o_lo(a, m):
                dve.wait_ge(act_a, ACT_A.upto(a, f"oh{m}"))
                dve.tensor_tensor(AO[:, 1, m, :], Ou[:, m, :], AO[:, 0, m, :], ALU.subtract).then_inc(dve_a, 1)

            def residual_y(a, s):
                if s == 0:
                    dve.wait_ge(xres_in, 16 * a + 16)
                dve.wait_ge(pe_a, PE_A.upto(a, f"y{s}"))
                dve.scalar_tensor_tensor(ybuf[:, s, :], ring_a[bank_a(f"y{s}")][:, :], 1.0 / WS, xres[:, s, :],
                                         ALU.mult, ALU.add).then_inc(dve_a, 1)

            def mean_y(a, s):
                dve.wait_ge(act_a, ACT_A.upto(a, f"sqy{s}"))
                dve.tensor_scalar(msy[:, s:s + 1], ssy[:, s:s + 1], 1.0 / D, EPS, ALU.mult, ALU.add).then_inc(dve_a, 1)

            def norm_y(a, s):
                dve.wait_ge(pool_a, POOL_A.upto(a, f"ry{s}"))
                dve.scalar_tensor_tensor(ybuf[:, s, :], ybuf[:, s, :], ry[:, s:s + 1], gout_b[:, :], ALU.mult,
                                         ALU.mult).then_inc(dve_a, 1)

            def x2_lo(a, s):
                dve.wait_ge(act_a, ACT_A.upto(a, f"x2h{s}"))
                q = slice(s * P, (s + 1) * P)
                dve.tensor_tensor(XS[:, 1, :, q], ring_a[bank_a(f"x2t{s}")][:, :].rearrange("p (c q) -> p c q", c=C),
                                  XS[:, 0, :, q], ALU.subtract).then_inc(dve_a, 1)

            def q1_lo(b_):
                dve.wait_ge(act_b, ACT_B.upto(b_, "qh"))
                if not static_first(b_):
                    dve.wait_ge(stack1_in, N_STACK * b_)
                dve.scalar_tensor_tensor(Q1s[:, 1, :], ring_b[bank_b("q")][:, :], QS1, Q1s[:, 0, :],
                                         ALU.mult, ALU.subtract).then_inc(dve_b, 1)

            def maxima1(b_, n):
                s, j = n // 4, n % 4
                dve.wait_ge(pe_b, PE_B.upto(b_, f"m{n}"))
                dve.tensor_reduce(mx1[:, s, j::4], ring_b[bank_b(f"m{n}")][:, 0:UNIT].rearrange("p (h k) -> p h k", h=2),
                                  AX.X, ALU.max).then_inc(dve_b, 1)

            def o1_norm(b_, g):
                src = ring_b[bank_b(f"od{g}")][:, :].rearrange("p (s j k) -> p s j k", s=SUB, j=4)
                dve.wait_ge(pe_b, PE_B.upto(b_, f"od{g}"))
                dve.reciprocal(rq1[:, g, :, :].unsqueeze(3), src[:, :, :, D1:D1 + 1]).then_inc(dve_b, 1)
                dve.wait_ge(dve_b, DVE_B.upto(b_, f"rc{g}"))
                dst = On1[:, :, 64 * g:64 * g + 64].rearrange("p s (j d) -> p s j d", j=4)
                dve.tensor_tensor(dst, src[:, :, :, 0:D1], rq1[:, g, :, :].unsqueeze(3).to_broadcast([P, SUB, 4, D1]),
                                  ALU.mult).then_inc(dve_b, 1)

            def o1_lo(b_):
                dve.wait_ge(act_b, ACT_B.upto(b_, "oh"))
                dve.tensor_tensor(O1s[:, 1, :], ring_b[bank_b("ot")][:, :], O1s[:, 0, :], ALU.subtract).then_inc(dve_b, 1)

            def residual_x(b_, m):
                dve.wait_ge(pe_b, PE_B.upto(b_, f"xo{m}"))
                dve.scalar_tensor_tensor(XT[:, m, :], ring_b[bank_b(f"xo{m}")][:, :], 1.0 / WS, XT[:, m, :],
                                         ALU.mult, ALU.add).then_inc(dve_b, 1)

            def x_split(b_, m):
                dve.wait_ge(act_b, ACT_B.upto(b_, f"xh{m}"))
                dve.tensor_tensor(XS[:, 1, m, :], XT[:, m, :], XS[:, 0, m, :], ALU.subtract).then_inc(dve_b, 1)

            def hidden(b_, f):
                dve.wait_ge(act_b, ACT_B.upto(b_, f"h{f}"))
                dve.tensor_copy(HS[:, 0, f, :], Ht[:, f % 2, :]).then_inc(dve_b, 1)
                dve.wait_ge(dve_b, DVE_B.upto(b_, f"hh{f}"))
                dve.tensor_tensor(HS[:, 1, f, :], Ht[:, f % 2, :], HS[:, 0, f, :], ALU.subtract).then_inc(dve_b, 1)

            def residual_out(b_, m):
                dve.wait_ge(pe_b, PE_B.upto(b_, f"f{m}"))
                dve.wait_ge(pool_b, POOL_B.upto(b_, f"xb{m}"))
                dve.scalar_tensor_tensor(XT[:, m, :], ring_b[bank_b(f"f{m}")][:, :], 1.0 / WS, XT[:, m, :],
                                         ALU.mult, ALU.add).then_inc(dve_b, 1)

            def step(f, a, b_):
                if b_ is not None:
                    q1_lo(b_)
                    for n in range(4):
                        maxima1(b_, n)
                if a is not None:
                    o_evac(a, 0)
                if b_ is not None:
                    for n in range(4, 9):
                        maxima1(b_, n)
                if a is not None:
                    o_evac(a, 1)
                if b_ is not None:
                    for n in range(9, 14):
                        maxima1(b_, n)
                if a is not None:
                    o_evac(a, 2)
                if b_ is not None:
                    for n in range(14, 16):
                        maxima1(b_, n)
                if a is not None:
                    o_evac(a, 3)
                    den(a)
                    for n in range(2):
                        o_norm(a, n)
                if f is not None:
                    norm_x(f, 0)
                if a is not None:
                    o_lo(a, 0)
                    o_norm(a, 2)
                    o_lo(a, 1)
                if f is not None:
                    norm_x(f, 1)
                if a is not None:
                    o_norm(a, 3)
                    for n in range(2, 4):
                        o_lo(a, n)
                if b_ is not None:
                    o1_norm(b_, 0)
                if f is not None:
                    norm_x(f, 2)
                if b_ is not None:
                    o1_norm(b_, 1)
                if f is not None:
                    norm_x(f, 3)
                    for n in range(2):
                        x_lo(f, n)
                if b_ is not None:
                    o1_lo(b_)
                if f is not None:
                    for n in range(2, 4):
                        x_lo(f, n)
                if a is not None:
                    residual_y(a, 0)
                if b_ is not None:
                    for n in range(2):
                        residual_x(b_, n)
                if a is not None:
                    residual_y(a, 1)
                if b_ is not None:
                    x_split(b_, 0)
                    residual_x(b_, 2)
                if a is not None:
                    mean_y(a, 0)
                if b_ is not None:
                    x_split(b_, 1)
                    residual_x(b_, 3)
                if f is not None:
                    q_lo(f, 0)
                if b_ is not None:
                    for n in range(2, 4):
                        x_split(b_, n)
                if f is not None:
                    q_lo(f, 1)
                    for n in range(8):
                        maxima(f, n)
                if a is not None:
                    residual_y(a, 2)
                if b_ is not None:
                    hidden(b_, 0)
                if f is not None:
                    q_lo(f, 2)
                    for n in range(8, 14):
                        maxima(f, n)
                if a is not None:
                    mean_y(a, 1)
                if f is not None:
                    for n in range(14, 16):
                        maxima(f, n)
                if b_ is not None:
                    for n in range(1, 3):
                        hidden(b_, n)
                if a is not None:
                    norm_y(a, 0)
                    residual_y(a, 3)
                if b_ is not None:
                    hidden(b_, 3)
                if f is not None:
                    q_lo(f, 3)
                if b_ is not None:
                    residual_out(b_, 0)
                if f is not None:
                    for n in range(16, 20):
                        maxima(f, n)
                if b_ is not None:
                    residual_out(b_, 1)
                if f is not None:
                    maxima(f, 20)
                if a is not None:
                    mean_y(a, 2)
                    norm_y(a, 1)
                if f is not None:
                    for n in range(21, 24):
                        maxima(f, n)
                if b_ is not None:
                    for n in range(2, 4):
                        residual_out(b_, n)
                if f is not None:
                    for n in range(24, 28):
                        maxima(f, n)
                if a is not None:
                    x2_lo(a, 0)
                    mean_y(a, 3)
                    norm_y(a, 2)
                    x2_lo(a, 1)
                    norm_y(a, 3)
                if f is not None:
                    for n in range(28, 32):
                        maxima(f, n)
                if a is not None:
                    for n in range(2, 4):
                        x2_lo(a, n)

            step(0, None, None)
            for i in range(3, len(BIG)):
                weight_lo_part(i)
            step(1, 0, None)
            step(2, 1, 0)
            with dve.Fori(1, NT - 2) as i:
                step(i + 2, i + 1, i)
            step(None, NT - 1, NT - 2)
            step(None, None, NT - 1)

        @block.tensor
        def _(pe):
            PASSES = ((0, 0), (1, 0), (0, 1))

            def split_chunk(dst, lhs, rhs, c, chunks):
                for n, (p, q) in enumerate(PASSES):
                    ins = pe.matmul(dst, lhs(p, c), rhs(q, c), start=c == 0 and n == 0,
                                    stop=c == chunks - 1 and n == len(PASSES) - 1)
                return ins

            def split_matmul(dst, lhs, rhs, chunks):
                for c in range(chunks):
                    ins = split_chunk(dst, lhs, rhs, c, chunks)
                return ins

            pe.wait_ge(const_ready, 8)
            pe.wait_ge(weight_split, 4 * 2 + len(SMALL))
            with pe.Fori(0, B) as b:
                for layer in range(2):
                    src = cn if layer == 0 else crow
                    pe.wait_ge(pre_dve, PRE_DVE.upto(b, "cn0" if layer == 0 else "ct0"))
                    for c in range(C):
                        ins = pe.transpose(psum[0][:, c * P:(c + 1) * P], src[:, 0, c * P:(c + 1) * P], ident[:, :])
                    ins.then_inc(pre_pe, 1)
                    for c in range(C):
                        ins = pe.transpose(psum[1][:, c * KP:(c + 1) * KP], src[0:KP, 1, c * P:(c + 1) * P],
                                           ident[0:KP, 0:KP])
                    ins.then_inc(pre_pe, 1)
                for layer in range(2):
                    cks, cvs = keys_in[layer], values_in[layer]
                    pe.wait_ge(pre_dve, PRE_DVE.upto(b, f"cks{layer}"))
                    if layer == 0:
                        for m in range(G0):
                            split_matmul(psum[2 + m][:, 0:KA], lambda p, c: WKV[:, 0, p, c, m * P:(m + 1) * P],
                                         lambda q, c: cks[:, q, c, :], C).then_inc(pre_pe, 1)
                        split_matmul(psum[6][:, :], lambda p, c: cvs[:, p, c, 0:KM],
                                     lambda q, c: WKV[:, 1, q, c, :], C).then_inc(pre_pe, 1)
                        for j in range(4):
                            ins = split_matmul(
                                psum[7][32 * j:32 * j + 32, 0:G0 * D0], lambda p, c: cvs[:, p, c, KM:KA],
                                lambda q, c: WKV[:, 1, q, c, :].rearrange("p (m n) -> p m n", m=G0)[
                                    :, :, 32 * j:32 * j + 32], C)
                        ins.then_inc(pre_pe, 1)
                    else:
                        pe.wait_ge(pre_dve, PRE_DVE.upto(b, "k0_0"))
                        split_matmul(psum[2][:, 0:KA], lambda p, c: WKV1[:, 0, p, c, :],
                                     lambda q, c: cks[:, q, c, :], C).then_inc(pre_pe, 1)
                        pe.wait_ge(pre_dve, PRE_DVE.upto(b, "v0"))
                        split_matmul(psum[6][:, 0:P], lambda p, c: cvs[:, p, c, 0:KM],
                                     lambda q, c: WKV1[:, 1, q, c, :], C).then_inc(pre_pe, 1)
                        pe.wait_ge(pre_dve, PRE_DVE.upto(b, "vr0"))
                        for j in range(4):
                            ins = split_matmul(
                                psum[7][32 * j:32 * j + 32, 0:G1 * D1], lambda p, c: cvs[:, p, c, KM:KA],
                                lambda q, c: WKV1[:, 1, q, c, :].rearrange("p (g n) -> p g n", g=G1)[
                                    :, :, D1 * j:D1 * j + D1], C)
                        ins.then_inc(pre_pe, 1)
            started(pe)

            def wait_bank(ring, reader, sems, steps, t, unit):
                before, ago = bank_before(ring, unit)
                if ago and static_first(t):
                    return
                engine, name = reader[before]
                pe.wait_ge(sems[engine], steps[engine].upto(t - ago, name))

            def free_f(f, unit):
                wait_bank(RING_F, READER_F, {"act": act_f, "dve": dve_f}, {"act": ACT_F, "dve": DVE_F}, f, unit)
                return ring_f[bank_f(unit)]

            def free_a(a, unit):
                wait_bank(RING_A, READER_A, {"act": act_a, "dve": dve_a}, {"act": ACT_A, "dve": DVE_A}, a, unit)
                return ring_a[bank_a(unit)]

            def free_b(b_, unit):
                wait_bank(RING_B, READER_B, {"act": act_b, "dve": dve_b}, {"act": ACT_B, "dve": DVE_B}, b_, unit)
                return ring_b[bank_b(unit)]

            def x_transpose(f, s):
                bank = free_f(f, f"xt{s}")
                pe.wait_ge(dve_f, DVE_F.upto(f, f"xn{s}"))
                for c in range(C):
                    ins = pe.transpose(bank[:, c * P:(c + 1) * P], xn[:, s % 2, c * P:(c + 1) * P], ident[:, :])
                ins.then_inc(pe_f, 1)

            def query(f, m, k):
                bank = free_f(f, f"q{m}") if k == 0 else ring_f[bank_f(f"q{m}")]
                if m == 0 and k == 0:
                    pe.wait_ge(dve_f, DVE_F.upto(f, "xl3"))
                ins = split_chunk(bank[:, :], lambda p, c: WQ[:, p, c, m * P:(m + 1) * P],
                             lambda q, c: AT[:, q, c, :], k, C)
                if k == C - 1:
                    ins.then_inc(pe_f, 1)

            def max_unit(f, n):
                m, s, half = n // 8, n % 8 // 2, n % 2
                bank = free_f(f, f"m{n}")
                if n % 8 == 0:
                    pe.wait_ge(act_f, ACT_F.upto(f, f"qh{m}"))
                if n == 0:
                    pe.wait_ge(blk0_in, 16 * batch_of(f) + 16)
                pe.matmul(bank[:, 0:UNIT], Qs[:, 0, m, s * P:(s + 1) * P], Kblk[:, m, half * UNIT:(half + 1) * UNIT],
                          start=True, stop=True).then_inc(pe_f, 1)

            def max_transpose(f):
                bank = free_f(f, "mt")
                pe.wait_ge(dve_f, DVE_F.upto(f, "mx31"))
                for s in range(SUB):
                    ins = pe.transpose(bank[0:H0, s * P:(s + 1) * P], mx[:, s, :], ident[:, :])
                ins.then_inc(pe_f, 1)

            def scores(a, g, j):
                if g == 0 and j == 4:
                    pe.wait_ge(stack0_in, N_STACK * (a + 1))
                    pe.wait_ge(max0_in, 16 * a + 16)
                    pe.wait_ge(kv0_in, 16 * batch_of(a) + 16)
                if j < 4:
                    bank = free_a(a, f"s{g}{j}")
                    ins = pe.matmul(bank[:, :], Kst[0:97, 4 * g + j, 0:KM], Qst[0:97, 4 * g + j, :], start=True, stop=True)
                else:
                    bank = free_a(a, f"r{g}")
                    for i in range(4):
                        ins = pe.matmul(bank[32 * i:32 * i + 32, :], Kst[0:97, 4 * g + i, KM:KA],
                                        Qst[0:97, 4 * g + i, :], start=True, stop=True)
                ins.then_inc(pe_a, 1)

            def values_rest(a, g):
                if g:
                    pe.wait_ge(dve_a, DVE_A.upto(a, f"o{g - 1}"))
                elif not static_first(a):
                    if not early(a):
                        pe.wait_ge(act_b, ACT_B.upto(a - 2, "od1"))
                    pe.wait_ge(act_a, ACT_A.upto(a - 1, "dsb"))
                pe.wait_ge(act_a, ACT_A.upto(a, f"er{g}"))
                pe.matmul(bank_o[:, :], V0r[:, g, :], Pr[:, 5 * (g % 2) + 4, :], start=True, stop=False)

            def values(a, g):
                pe.wait_ge(act_a, ACT_A.upto(a, f"e{g}3"))
                for j in range(4):
                    h = 4 * g + j
                    ins = pe.matmul(bank_o[32 * j:32 * j + 32, :], V0[:, h * D0:(h + 1) * D0], Pr[:, 5 * (g % 2) + j, :],
                                    start=False, stop=True)
                ins.then_inc(pe_a, 1)

            def denominators(a, g):
                slot = 5 * (g % 2)
                for j in range(4):
                    pe.matmul(bank_d[32 * j:32 * j + 32, :], E0[:, 32 * g:32 * g + 32], Pr[:, slot + j, :],
                              start=g == 0, stop=False, skip_group_check=True)
                pe.matmul(bank_d[32 * g:32 * g + 32, :], E0r[:, :], Pr[:, slot + 4, :],
                          start=False, stop=g == G0 - 1, skip_group_check=True).then_inc(pe_a, 1)

            def den_transpose(a):
                bank = free_a(a, "dt")
                pe.wait_ge(act_a, ACT_A.upto(a, "dsb"))
                for s in range(SUB):
                    ins = pe.transpose(bank[:, s * P:(s + 1) * P], Dsb[:, s * P:(s + 1) * P], ident[:, :])
                ins.then_inc(pe_a, 1)

            def den_spread(a, m):
                bank = free_a(a, f"rb{m}")
                pe.wait_ge(pool_a, POOL_A.upto(a, f"rr{m}"))
                for s in range(SUB):
                    ins = pe.transpose(bank[:, s * P:(s + 1) * P], xn[:, m % 2, s * P:(s + 1) * P], ident[:, :])
                ins.then_inc(pe_a, 1)

            def project_out(a, s, k):
                bank = free_a(a, f"y{s}") if k == 0 else ring_a[bank_a(f"y{s}")]
                if s == 0:
                    pe.wait_ge(dve_a, DVE_A.upto(a, f"ol{k}"))
                ins = split_chunk(bank[:, :], lambda p, c: AO[:, p, c, s * P:(s + 1) * P],
                             lambda q, c: WO[:, q, c, :], k, C)
                if k == C - 1:
                    ins.then_inc(pe_a, 1)

            def x2_transpose(a, s):
                bank = free_a(a, f"x2t{s}")
                pe.wait_ge(dve_a, DVE_A.upto(a, f"x2_{s}"))
                for c in range(C):
                    ins = pe.transpose(bank[:, c * P:(c + 1) * P], ybuf[:, s, c * P:(c + 1) * P], ident[:, :])
                ins.then_inc(pe_a, 1)

            def query1(b_, k):
                bank = free_b(b_, "q") if k == 0 else ring_b[bank_b("q")]
                if k == 0:
                    pe.wait_ge(dve_a, DVE_A.upto(b_, "x2l3"))
                ins = split_chunk(bank[:, :], lambda p, c: WQ1[:, p, c, :], lambda q, c: XS[:, q, c, :], k, C)
                if k == C - 1:
                    ins.then_inc(pe_b, 1)

            def max_unit1(b_, n):
                s, j = n // 4, n % 4
                bank = free_b(b_, f"m{n}")
                if n == 0:
                    pe.wait_ge(act_b, ACT_B.upto(b_, "qh"))
                    pe.wait_ge(kv1_in, 16 * batch_of(b_) + 16)
                pe.matmul(bank[:, 0:UNIT], Q1s[:, 0, s * P:(s + 1) * P], K1blk[:, j * UNIT:(j + 1) * UNIT],
                          start=True, stop=True).then_inc(pe_b, 1)

            def max_transpose1(b_):
                bank = free_b(b_, "mt")
                pe.wait_ge(dve_b, DVE_B.upto(b_, "mx15"))
                for s in range(SUB):
                    ins = pe.transpose(bank[0:H1, s * P:(s + 1) * P], mx1[:, s, :], ident[:, :])
                ins.then_inc(pe_b, 1)

            def scores1(b_, g, j):
                if g == 0 and j == 4:
                    pe.wait_ge(stack1_in, N_STACK * (b_ + 1))
                    pe.wait_ge(max1_in, 16 * b_ + 16)
                if j < 4:
                    h = 4 * g + j
                    bank = free_b(b_, f"s{g}{j}")
                    ins = pe.matmul(bank[:, :], K1st[0:98, h, 0:KM], Q1st[0:98, h // 2, :], start=True, stop=True)
                else:
                    bank = free_b(b_, f"r{g}")
                    for i in range(4):
                        h = 4 * g + i
                        ins = pe.matmul(bank[32 * i:32 * i + 32, :], K1st[0:98, h, KM:KA], Q1st[0:98, h // 2, :],
                                        start=True, stop=True)
                ins.then_inc(pe_b, 1)

            def values1_rest(b_, g):
                if g:
                    pe.wait_ge(act_b, ACT_B.upto(b_, "od0"))
                elif not static_last(b_):
                    pe.wait_ge(dve_a, DVE_A.upto(b_ + 1, "o3"))
                pe.wait_ge(act_b, ACT_B.upto(b_, f"er{g}"))
                pe.matmul(bank_o[:, :], V1r[:, g, :], Pr[:, 5 * g + 4, :], start=True, stop=False)

            def values1(b_, g):
                pe.wait_ge(act_b, ACT_B.upto(b_, f"e{g}3"))
                for j in range(4):
                    ins = pe.matmul(bank_o[32 * j:32 * j + 32, :], V1[:, 4 * g + j, :], Pr[:, 5 * g + j, :],
                                    start=False, stop=True)
                ins.then_inc(pe_b, 1)

            def o1_transpose(b_, g):
                bank = free_b(b_, f"od{g}")
                pe.wait_ge(act_b, ACT_B.upto(b_, f"od{g}"))
                for s in range(SUB):
                    ins = pe.transpose(bank[:, s * P:(s + 1) * P], OD[:, g, s * P:(s + 1) * P], ident[:, :])
                ins.then_inc(pe_b, 1)

            def o1_back(b_):
                bank = free_b(b_, "ot")
                pe.wait_ge(dve_b, DVE_B.upto(b_, "on1"))
                for s in range(SUB):
                    ins = pe.transpose(bank[:, s * P:(s + 1) * P], On1[:, s, :], ident[:, :])
                ins.then_inc(pe_b, 1)

            def project_out1(b_, m):
                bank = free_b(b_, f"xo{m}")
                if m == 0:
                    pe.wait_ge(dve_b, DVE_B.upto(b_, "ol"))
                split_matmul(bank[:, :], lambda p, c: WO1[:, p, c, m * P:(m + 1) * P],
                             lambda q, c: O1s[:, q, :], 1).then_inc(pe_b, 1)

            def hidden(b_, f, k):
                bank = free_b(b_, f"h{f}") if k == 0 else ring_b[bank_b(f"h{f}")]
                if f == 0:
                    pe.wait_ge(dve_b, DVE_B.upto(b_, f"xl{k}"))
                ins = split_chunk(bank[:, :], lambda p, c: W1[:, p, c, f * P:(f + 1) * P],
                             lambda q, c: XS[:, q, c, :], k, C)
                if k == C - 1:
                    ins.then_inc(pe_b, 1)

            def ffn_out(b_, m, k):
                bank = free_b(b_, f"f{m}") if k == 0 else ring_b[bank_b(f"f{m}")]
                if m == 0:
                    pe.wait_ge(dve_b, DVE_B.upto(b_, f"hl{k}"))
                ins = split_chunk(bank[:, :], lambda p, c: W2[:, p, c, m * P:(m + 1) * P],
                             lambda q, c: HS[:, q, c, :], k, C)
                if k == C - 1:
                    ins.then_inc(pe_b, 1)

            def out_transpose(b_, s):
                bank = free_b(b_, f"t{s}")
                if s == 0:
                    pe.wait_ge(dve_b, DVE_B.upto(b_, "f3"))
                for c in range(C):
                    ins = pe.transpose(bank[:, c * P:(c + 1) * P], XT[:, c, s * P:(s + 1) * P], ident[:, :])
                ins.then_inc(pe_b, 1)

            def step(f, a, b_):
                if b_ is not None:
                    for n in range(3):
                        query1(b_, n)
                if a is not None:
                    scores(a, 0, 4)
                    scores(a, 0, 0)
                if b_ is not None:
                    query1(b_, 3)
                if a is not None:
                    for n in range(1, 4):
                        scores(a, 0, n)
                    scores(a, 1, 4)
                    values_rest(a, 0)
                    scores(a, 1, 0)
                if b_ is not None:
                    max_unit1(b_, 0)
                if a is not None:
                    scores(a, 1, 1)
                if b_ is not None:
                    max_unit1(b_, 1)
                if a is not None:
                    values(a, 0)
                    scores(a, 1, 2)
                if b_ is not None:
                    for n in range(2, 4):
                        max_unit1(b_, n)
                if a is not None:
                    scores(a, 1, 3)
                    denominators(a, 0)
                    scores(a, 2, 4)
                if b_ is not None:
                    for n in range(4, 6):
                        max_unit1(b_, n)
                if a is not None:
                    values_rest(a, 1)
                if b_ is not None:
                    for n in range(6, 8):
                        max_unit1(b_, n)
                if a is not None:
                    for n in range(2):
                        scores(a, 2, n)
                    values(a, 1)
                if b_ is not None:
                    max_unit1(b_, 8)
                if a is not None:
                    scores(a, 2, 2)
                if b_ is not None:
                    max_unit1(b_, 9)
                if a is not None:
                    scores(a, 2, 3)
                    denominators(a, 1)
                if b_ is not None:
                    for n in range(10, 12):
                        max_unit1(b_, n)
                if a is not None:
                    scores(a, 3, 4)
                    values_rest(a, 2)
                if b_ is not None:
                    max_unit1(b_, 12)
                if a is not None:
                    scores(a, 3, 0)
                if b_ is not None:
                    max_unit1(b_, 13)
                if a is not None:
                    scores(a, 3, 1)
                    values(a, 2)
                if b_ is not None:
                    for n in range(14, 16):
                        max_unit1(b_, n)
                if a is not None:
                    for n in range(2, 4):
                        scores(a, 3, n)
                    denominators(a, 2)
                if b_ is not None:
                    max_transpose1(b_)
                if a is not None:
                    values_rest(a, 3)
                    values(a, 3)
                    denominators(a, 3)
                if b_ is not None:
                    scores1(b_, 0, 4)
                    scores1(b_, 0, 0)
                if a is not None:
                    den_transpose(a)
                if b_ is not None:
                    for n in range(1, 4):
                        scores1(b_, 0, n)
                    values1_rest(b_, 0)
                    values1(b_, 0)
                if a is not None:
                    den_spread(a, 0)
                if b_ is not None:
                    scores1(b_, 1, 4)
                    scores1(b_, 1, 0)
                if a is not None:
                    den_spread(a, 1)
                if b_ is not None:
                    scores1(b_, 1, 1)
                if a is not None:
                    den_spread(a, 2)
                if b_ is not None:
                    for n in range(2, 4):
                        scores1(b_, 1, n)
                if a is not None:
                    den_spread(a, 3)
                if b_ is not None:
                    values1_rest(b_, 1)
                    values1(b_, 1)
                if f is not None:
                    x_transpose(f, 0)
                if b_ is not None:
                    o1_transpose(b_, 0)
                if a is not None:
                    for n in range(2):
                        project_out(a, 0, n)
                if f is not None:
                    x_transpose(f, 1)
                if b_ is not None:
                    o1_transpose(b_, 1)
                if a is not None:
                    for n in range(2, 4):
                        project_out(a, 0, n)
                    for n in range(2):
                        project_out(a, 1, n)
                if b_ is not None:
                    o1_back(b_)
                if a is not None:
                    project_out(a, 1, 2)
                if f is not None:
                    for n in range(2, 4):
                        x_transpose(f, n)
                if a is not None:
                    project_out(a, 1, 3)
                if b_ is not None:
                    for n in range(2):
                        project_out1(b_, n)
                if f is not None:
                    for n in range(3):
                        query(f, 0, n)
                if b_ is not None:
                    project_out1(b_, 2)
                if f is not None:
                    query(f, 0, 3)
                if b_ is not None:
                    project_out1(b_, 3)
                if f is not None:
                    for n in range(2):
                        query(f, 1, n)
                if b_ is not None:
                    hidden(b_, 0, 0)
                if f is not None:
                    for n in range(2, 4):
                        query(f, 1, n)
                if b_ is not None:
                    hidden(b_, 0, 1)
                if a is not None:
                    for n in range(3):
                        project_out(a, 2, n)
                if f is not None:
                    max_unit(f, 0)
                if b_ is not None:
                    hidden(b_, 0, 2)
                if f is not None:
                    for n in range(1, 3):
                        max_unit(f, n)
                if b_ is not None:
                    hidden(b_, 0, 3)
                if f is not None:
                    max_unit(f, 3)
                if b_ is not None:
                    for n in range(2):
                        hidden(b_, 1, n)
                if f is not None:
                    max_unit(f, 4)
                if b_ is not None:
                    hidden(b_, 1, 2)
                if a is not None:
                    project_out(a, 2, 3)
                if f is not None:
                    max_unit(f, 5)
                if b_ is not None:
                    hidden(b_, 1, 3)
                if f is not None:
                    max_unit(f, 6)
                if b_ is not None:
                    hidden(b_, 2, 0)
                if f is not None:
                    max_unit(f, 7)
                    for n in range(4):
                        query(f, 2, n)
                if b_ is not None:
                    hidden(b_, 2, 1)
                if f is not None:
                    max_unit(f, 8)
                if a is not None:
                    project_out(a, 3, 0)
                if b_ is not None:
                    hidden(b_, 2, 2)
                if f is not None:
                    max_unit(f, 9)
                if b_ is not None:
                    hidden(b_, 2, 3)
                if f is not None:
                    for n in range(10, 12):
                        max_unit(f, n)
                if b_ is not None:
                    hidden(b_, 3, 0)
                if f is not None:
                    max_unit(f, 12)
                if b_ is not None:
                    hidden(b_, 3, 1)
                if a is not None:
                    project_out(a, 3, 1)
                if f is not None:
                    for n in range(13, 15):
                        max_unit(f, n)
                if b_ is not None:
                    hidden(b_, 3, 2)
                if f is not None:
                    max_unit(f, 15)
                if a is not None:
                    for n in range(2, 4):
                        project_out(a, 3, n)
                if f is not None:
                    query(f, 3, 0)
                if b_ is not None:
                    hidden(b_, 3, 3)
                if f is not None:
                    for n in range(1, 4):
                        query(f, 3, n)
                if b_ is not None:
                    for n in range(4):
                        ffn_out(b_, 0, n)
                    ffn_out(b_, 1, 0)
                if f is not None:
                    for n in range(16, 18):
                        max_unit(f, n)
                if b_ is not None:
                    ffn_out(b_, 1, 1)
                if f is not None:
                    max_unit(f, 18)
                if b_ is not None:
                    for n in range(2, 4):
                        ffn_out(b_, 1, n)
                if f is not None:
                    max_unit(f, 19)
                if b_ is not None:
                    ffn_out(b_, 2, 0)
                if f is not None:
                    max_unit(f, 20)
                if b_ is not None:
                    for n in range(1, 3):
                        ffn_out(b_, 2, n)
                if f is not None:
                    max_unit(f, 21)
                if b_ is not None:
                    ffn_out(b_, 2, 3)
                    ffn_out(b_, 3, 0)
                if f is not None:
                    max_unit(f, 22)
                if b_ is not None:
                    ffn_out(b_, 3, 1)
                if f is not None:
                    max_unit(f, 23)
                if b_ is not None:
                    for n in range(2, 4):
                        ffn_out(b_, 3, n)
                if f is not None:
                    max_unit(f, 24)
                if a is not None:
                    x2_transpose(a, 0)
                if f is not None:
                    max_unit(f, 25)
                if b_ is not None:
                    out_transpose(b_, 0)
                if f is not None:
                    max_unit(f, 26)
                if a is not None:
                    x2_transpose(a, 1)
                if f is not None:
                    for n in range(27, 29):
                        max_unit(f, n)
                if b_ is not None:
                    for n in range(1, 3):
                        out_transpose(b_, n)
                if f is not None:
                    max_unit(f, 29)
                if a is not None:
                    x2_transpose(a, 2)
                if b_ is not None:
                    out_transpose(b_, 3)
                if a is not None:
                    x2_transpose(a, 3)
                if f is not None:
                    for n in range(30, 32):
                        max_unit(f, n)
                    max_transpose(f)

            step(0, None, None)
            weights_done(pe)
            step(1, 0, None)
            step(2, 1, 0)
            with pe.Fori(1, NT - 2) as i:
                step(i + 2, i + 1, i)
            step(None, NT - 1, NT - 2)
            step(None, None, NT - 1)


def kernel(x, ctx_1024, mask_BxS2_bf1, L0_xattn_Wq, L0_xattn_Wk, L0_xattn_Wv, L0_xattn_Wo, L0_xattn_g_q,
           L0_xattn_g_c, L0_xattn_g_out, L1_xattn_W_q, L1_xattn_W_k, L1_xattn_W_v, L1_xattn_W_o, L1_xattn_w1,
           L1_xattn_b1, L1_xattn_w2, L1_xattn_b2):
    import numpy as np
    import concourse.bacc as bacc
    from concourse.bass_utils import run_bass_kernel_spmd

    def by_chunk(v):
        return np.asarray(v).reshape(C, P).T

    nc = bacc.Bacc("TRN2", target_bir_lowering=False, num_devices=1)
    arrays = {
        "x": np.asarray(x).reshape(B * S, D), "ctxt": np.asarray(ctx_1024).reshape(B * SK, D),
        "mask": np.asarray(mask_BxS2_bf1).view(np.uint8), "mask_col": np.asarray(mask_BxS2_bf1).view(np.uint8).reshape(B * SK, 1),
        "wq": L0_xattn_Wq, "wk": L0_xattn_Wk, "wv": L0_xattn_Wv, "wo": L0_xattn_Wo,
        "gq": by_chunk(L0_xattn_g_q), "gc": by_chunk(L0_xattn_g_c), "gout": L0_xattn_g_out,
        "wq1": L1_xattn_W_q, "wk1": L1_xattn_W_k, "wv1": L1_xattn_W_v, "wo1": L1_xattn_W_o,
        "w1t": np.asarray(L1_xattn_w1).T, "b1": by_chunk(L1_xattn_b1), "w2t": np.asarray(L1_xattn_w2).T, "b2": by_chunk(L1_xattn_b2),
    }
    arrays = {n: np.ascontiguousarray(a) for n, a in arrays.items()}
    aps = {n: nc.dram_tensor(n, a.shape, mybir.dt.from_np(a.dtype), kind="ExternalInput").ap()
           for n, a in arrays.items()}
    out = nc.dram_tensor("out", (B * S, D), F32, kind="ExternalOutput").ap()
    build(nc, *aps.values(), out)
    result = run_bass_kernel_spmd(nc, [arrays], core_ids=[0])
    return result.results[0]["out"].reshape(B, S, D)
```
